# Optimizing a Trainium2 kernel written in Bass

```python
import numpy as np
import jax
import jax.numpy as jnp

def _softmax(x, axis=-1):
    return jax.nn.softmax(x, axis=axis)

def _gelu(x):
    return jax.nn.gelu(x, approximate=True)

def _silu(x):
    return jax.nn.silu(x)

def _sigmoid(x):
    return jax.nn.sigmoid(x)

def _layernorm(x, axis=-1, eps=1e-05):
    m = jnp.mean(x, axis=axis, keepdims=True)
    v = jnp.var(x, axis=axis, keepdims=True)
    return (x - m) / jnp.sqrt(v + eps)

def _scatter_add(tgt, idx, src, axis=0):
    return tgt.at[idx].add(src)

def _segment_sum(src, seg, n):
    return jax.ops.segment_sum(src, seg, n)
kernel_name = 'mk_xattn_ffn_d4_seqx_r8_1b00a1'

def setup_inputs(seed: int=0):
    np.random.seed(seed)
    _w = jnp.asarray

    def _rec_inputs():
        import jax
        import jax.numpy as jnp
        _rk = jax.random.key(seed)
        x = -0.0003929 + 0.9999 * jax.random.normal(jax.random.fold_in(_rk, 1), (32, 56, 128), jnp.float32)
        _lenS = 56 - jax.random.randint(jax.random.fold_in(_rk, 7), (32,), 0, max(1, 56 // 4) + 1, jnp.int32)
        _lenS2 = 1500 - jax.random.randint(jax.random.fold_in(_rk, 8), (32,), 0, max(1, 1500 // 4) + 1, jnp.int32)
        _ctx_1024P = jax.random.normal(jax.random.fold_in(_rk, 11), (32, 16, 128), jnp.float32)
        _ctx_1024c = jax.random.dirichlet(jax.random.fold_in(_rk, 511), 0.3 * jnp.ones((16,), jnp.float32), (32, 1500))
        _ctx_1024t = jnp.einsum('bsk,bkd->bsd', _ctx_1024c, _ctx_1024P)
        _ctx_1024t = _ctx_1024t * jax.lax.rsqrt(jnp.mean(jnp.square(_ctx_1024t)) + 1e-12) * 0.953939
        ctx_1024 = 2.81802e-05 + 1.00001 * (_ctx_1024t + 0.3 * jax.random.normal(jax.random.fold_in(_rk, 611), (32, 1500, 128), jnp.float32))
        _validS = jnp.arange(56)[None, :] < _lenS[:, None]
        _validS2 = jnp.arange(1500)[None, :] < _lenS2[:, None]
        _causal = jnp.tril(jnp.ones((56, 56), dtype=bool))
        mask_BxS2_ik0 = jnp.where(jnp.broadcast_to(_validS2[:, :], (32, 1500)), 0, 1).astype(jnp.int32)
        mask_BxS2_bk0 = jnp.logical_not(jnp.broadcast_to(_validS2[:, :], (32, 1500)))
        return (x, ctx_1024, mask_BxS2_ik0, mask_BxS2_bk0)
    x, ctx_1024, mask_BxS2_ik0, mask_BxS2_bk0 = _rec_inputs()

    def _L0_xattn_setup():
        import jax, jax.numpy as jnp
        import numpy as np
        B, LQ, LKV, D = (8, 256, 256, 128)
        key = jax.random.key(seed)
        k1, k2, k3, k4, k5, k6, k7 = jax.random.split(key, 7)
        s = 1.0 / np.sqrt(D)
        return {'query': jax.random.normal(k1, (B, LQ, D), jnp.float32), 'key': jax.random.normal(k2, (B, LKV, D), jnp.float32), 'value': jax.random.normal(k3, (B, LKV, D), jnp.float32), 'Wq': jax.random.uniform(k4, (D, D), jnp.float32, -s, s), 'bq': jax.random.uniform(k5, (D,), jnp.float32, -s, s), 'Wk': jax.random.uniform(k6, (D, D), jnp.float32, -s, s), 'bk': jax.random.uniform(k7, (D,), jnp.float32, -s, s), 'scale_factor': 32, 'dropout_p': 0}
    _L0_xattn_all = _L0_xattn_setup()
    _L0_xattn_in = {k: v for k, v in _L0_xattn_all.items() if k in ('Wq', 'bq', 'Wk', 'bk')}
    del _L0_xattn_all

    def _L0_ffn_setup():
        import jax, jax.numpy as jnp
        import numpy as np
        B, S, D, H, E = (4, 256, 128, 512, 8)
        key = jax.random.key(seed)
        ks = jax.random.split(key, 8)
        s_d = 1.0 / np.sqrt(D)
        s_h = 1.0 / np.sqrt(H)
        return {'x': jax.random.normal(ks[0], (B, S, D), dtype=jnp.float32), 'gate_w': jax.random.uniform(ks[1], (E, D), jnp.float32, -s_d, s_d), 'gate_b': jax.random.uniform(ks[2], (E,), jnp.float32, -s_d, s_d), 'w1': jax.random.uniform(ks[3], (E, H, D), jnp.float32, -s_d, s_d), 'b1': jax.random.uniform(ks[4], (E, H), jnp.float32, -s_d, s_d), 'w2': jax.random.uniform(ks[5], (E, D, H), jnp.float32, -s_h, s_h), 'b2': jax.random.uniform(ks[6], (E, D), jnp.float32, -s_h, s_h)}
    _L0_ffn_all = _L0_ffn_setup()
    _L0_ffn_in = {k: v for k, v in _L0_ffn_all.items() if k in ('gate_w', 'gate_b', 'w1', 'b1', 'w2', 'b2')}
    del _L0_ffn_all

    def _L1_xattn_setup():
        import jax, jax.numpy as jnp
        import numpy as np
        D_MODEL = 128
        NUM_HEADS = 16
        D_K = D_MODEL // NUM_HEADS
        key = jax.random.key(seed)
        ks = jax.random.split(key, 13)
        B, S = (2, 256)
        s = 1.0 / np.sqrt(D_MODEL)
        inp = {'q': jax.random.normal(ks[0], (B, S, D_MODEL), jnp.float32), 'k': jax.random.normal(ks[1], (B, S, D_MODEL), jnp.float32), 'v': jax.random.normal(ks[2], (B, S, D_MODEL), jnp.float32), 'mask': jax.random.randint(ks[3], (B, S), 0, 2, jnp.int32), 'Wq': jax.random.normal(ks[4], (D_MODEL, D_MODEL), jnp.float32) * s, 'bq': jax.random.normal(ks[5], (D_MODEL,), jnp.float32) * s, 'Wk': jax.random.normal(ks[6], (D_MODEL, D_MODEL), jnp.float32) * s, 'bk': jax.random.normal(ks[7], (D_MODEL,), jnp.float32) * s, 'Wv': jax.random.normal(ks[8], (D_MODEL, D_MODEL), jnp.float32) * s, 'bv': jax.random.normal(ks[9], (D_MODEL,), jnp.float32) * s, 'Wo': jax.random.normal(ks[10], (D_MODEL, D_MODEL), jnp.float32) * s, 'bo': jax.random.normal(ks[11], (D_MODEL,), jnp.float32) * s}
        return inp
    _L1_xattn_all = _L1_xattn_setup()
    _L1_xattn_in = {k: v for k, v in _L1_xattn_all.items() if k in ('Wq', 'bq', 'Wk', 'bk', 'Wv', 'bv', 'Wo', 'bo')}
    del _L1_xattn_all

    def _L1_ffn_setup():
        import jax, jax.numpy as jnp
        import numpy as np
        B, S, H, F, E, K = (4, 256, 128, 512, 8, 2)
        key = jax.random.key(seed)
        ks = jax.random.split(key, 4)
        sc = lambda d: 1.0 / np.sqrt(d)
        return {'x': jax.random.normal(ks[0], (B, S, H), jnp.float32), 'gate_w': jax.random.normal(ks[1], (H, E), jnp.float32) * sc(H), 'gate_b': jnp.zeros((E,), jnp.float32), 'w1': jax.random.normal(ks[2], (E, H, F), jnp.float32) * sc(H), 'b1': jnp.zeros((E, F), jnp.float32), 'w2': jax.random.normal(ks[3], (E, F, H), jnp.float32) * sc(F), 'b2': jnp.zeros((E, H), jnp.float32)}
    _L1_ffn_all = _L1_ffn_setup()
    _L1_ffn_in = {k: v for k, v in _L1_ffn_all.items() if k in ('gate_w', 'gate_b', 'w1', 'b1', 'w2', 'b2')}
    del _L1_ffn_all

    def _L2_xattn_setup():
        import jax, jax.numpy as jnp
        import numpy as np
        D_MODEL = 128
        N_HEADS = 16
        HEAD_DIM = D_MODEL // N_HEADS
        key = jax.random.key(seed)
        k1, k2, k3, k4, k5, k6 = jax.random.split(key, 6)
        B, T_q, T_kv = (4, 128, 512)
        s = 1.0 / np.sqrt(D_MODEL)
        return {'query': jax.random.normal(k1, (B, T_q, D_MODEL), dtype=jnp.float32), 'kv_source': jax.random.normal(k2, (B, T_kv, D_MODEL), dtype=jnp.float32), 'w_q': jax.random.normal(k3, (D_MODEL, D_MODEL), dtype=jnp.float32) * s, 'w_k': jax.random.normal(k4, (D_MODEL, D_MODEL), dtype=jnp.float32) * s, 'w_v': jax.random.normal(k5, (D_MODEL, D_MODEL), dtype=jnp.float32) * s, 'w_o': jax.random.normal(k6, (D_MODEL, D_MODEL), dtype=jnp.float32) * s}
    _L2_xattn_all = _L2_xattn_setup()
    _L2_xattn_in = {k: v for k, v in _L2_xattn_all.items() if k in ('w_q', 'w_k', 'w_v', 'w_o')}
    del _L2_xattn_all

    def _L2_ffn_setup():
        import jax, jax.numpy as jnp
        import numpy as np
        MANT_BITS = 8
        _PWL_X = jnp.linspace(-4.0, 4.0, 33, dtype=jnp.float32)
        _PWL_Y = 0.5 * _PWL_X * (1.0 + jax.lax.erf(_PWL_X / jnp.sqrt(jnp.float32(2.0))))

        def float2fix(x, mantissa_bits):
            s = jnp.float32(2.0 ** mantissa_bits)
            q = jnp.round(x * s) / s
            return x + jax.lax.stop_gradient(q - x)

        def pwlin_gelu_basic(x, mantissa_bits_in, mantissa_bits_out):
            xq = float2fix(x, mantissa_bits_in)
            y = jnp.interp(xq, _PWL_X, _PWL_Y)
            y = jnp.where(xq > 4.0, xq, jnp.where(xq < -4.0, jnp.float32(0.0), y))
            return float2fix(y, mantissa_bits_out)
        key = jax.random.key(seed)
        k_x, k_w1, k_b1, k_w2, k_b2 = jax.random.split(key, 5)
        dim, ff_dim = (128, 512)
        B, S = (32, 64)
        sc1 = 1.0 / np.sqrt(dim)
        sc2 = 1.0 / np.sqrt(ff_dim)
        return {'x': jax.random.normal(k_x, (B, S, dim), dtype=jnp.float32), 'w1': jax.random.uniform(k_w1, (dim, ff_dim), jnp.float32, -sc1, sc1), 'b1': jax.random.uniform(k_b1, (ff_dim,), jnp.float32, -sc1, sc1), 'w2': jax.random.uniform(k_w2, (ff_dim, dim), jnp.float32, -sc2, sc2), 'b2': jax.random.uniform(k_b2, (dim,), jnp.float32, -sc2, sc2)}
    _L2_ffn_all = _L2_ffn_setup()
    _L2_ffn_in = {k: v for k, v in _L2_ffn_all.items() if k in ('w1', 'b1', 'w2', 'b2')}
    del _L2_ffn_all

    def _L3_xattn_setup():
        import jax, jax.numpy as jnp
        import numpy as np
        DIM, DIM_HEAD, HEADS, SCALE = (128, 64, 8, 8.0)
        INNER = DIM_HEAD * HEADS
        LN_EPS = 1e-05
        L2_EPS = 1e-12

        def layer_norm(x, w, b):
            mu = jnp.mean(x, axis=-1, keepdims=True)
            var = jnp.mean(jnp.square(x - mu), axis=-1, keepdims=True)
            return (x - mu) * jax.lax.rsqrt(var + LN_EPS) * w + b

        def l2norm(t):
            n = jnp.sqrt(jnp.sum(jnp.square(t), axis=-1, keepdims=True))
            return t / jnp.maximum(n, L2_EPS)
        key = jax.random.key(seed)
        ks = jax.random.split(key, 8)
        b, n, m = (8, 1024, 64)
        x = jax.random.normal(ks[0], (b, n, DIM), dtype=jnp.float32)
        latents = jax.random.normal(ks[1], (b, m, DIM), dtype=jnp.float32)
        mask = jax.random.randint(ks[2], (b, n), 0, 2) > 0
        Wq = jax.random.normal(ks[3], (DIM, INNER), dtype=jnp.float32) * DIM ** (-0.5)
        Wkv = jax.random.normal(ks[4], (DIM, 2 * INNER), dtype=jnp.float32) * DIM ** (-0.5)
        Wo = jax.random.normal(ks[5], (INNER, DIM), dtype=jnp.float32) * INNER ** (-0.5)
        return {'x': x, 'latents': latents, 'mask': mask, 'ln_x_w': jnp.ones((DIM,)), 'ln_x_b': jnp.zeros((DIM,)), 'ln_l_w': jnp.ones((DIM,)), 'ln_l_b': jnp.zeros((DIM,)), 'Wq': Wq, 'Wkv': Wkv, 'q_scale': jnp.ones((DIM_HEAD,)), 'k_scale': jnp.ones((DIM_HEAD,)), 'Wo': Wo, 'ln_o_w': jnp.ones((DIM,)), 'ln_o_b': jnp.zeros((DIM,))}
    _L3_xattn_all = _L3_xattn_setup()
    _L3_xattn_in = {k: v for k, v in _L3_xattn_all.items() if k in ('ln_x_w', 'ln_x_b', 'ln_l_w', 'ln_l_b', 'Wq', 'Wkv', 'q_scale', 'k_scale', 'Wo', 'ln_o_w', 'ln_o_b')}
    del _L3_xattn_all

    def _L3_ffn_setup():
        import jax, jax.numpy as jnp
        import numpy as np
        D_MODEL = 128
        HIDDEN = 512
        N_ROUTING = 2
        key = jax.random.key(seed)
        ks = jax.random.split(key, 10)
        s = 0.02
        x = jax.random.normal(ks[0], (4, 512, D_MODEL), dtype=jnp.float32)
        gate_w = jax.random.normal(ks[1], (N_ROUTING, D_MODEL), dtype=jnp.float32) * s
        w1 = jax.random.normal(ks[2], (N_ROUTING, D_MODEL, HIDDEN), dtype=jnp.float32) * s
        b1 = jax.random.normal(ks[3], (N_ROUTING, HIDDEN), dtype=jnp.float32) * s
        w2 = jax.random.normal(ks[4], (N_ROUTING, HIDDEN, D_MODEL), dtype=jnp.float32) * s
        b2 = jax.random.normal(ks[5], (N_ROUTING, D_MODEL), dtype=jnp.float32) * s
        sw1 = jax.random.normal(ks[6], (D_MODEL, HIDDEN), dtype=jnp.float32) * s
        sb1 = jax.random.normal(ks[7], (HIDDEN,), dtype=jnp.float32) * s
        sw2 = jax.random.normal(ks[8], (HIDDEN, D_MODEL), dtype=jnp.float32) * s
        sb2 = jax.random.normal(ks[9], (D_MODEL,), dtype=jnp.float32) * s
        return {'x': x, 'gate_w': gate_w, 'w1': w1, 'b1': b1, 'w2': w2, 'b2': b2, 'sw1': sw1, 'sb1': sb1, 'sw2': sw2, 'sb2': sb2}
    _L3_ffn_all = _L3_ffn_setup()
    _L3_ffn_in = {k: v for k, v in _L3_ffn_all.items() if k in ('gate_w', 'w1', 'b1', 'w2', 'b2', 'sw1', 'sb1', 'sw2', 'sb2')}
    del _L3_ffn_all
    return {'x': x, 'ctx_1024': ctx_1024, 'mask_BxS2_ik0': mask_BxS2_ik0, 'mask_BxS2_bk0': mask_BxS2_bk0, 'L0_xattn_Wq': _L0_xattn_in['Wq'], 'L0_xattn_bq': _L0_xattn_in['bq'], 'L0_xattn_Wk': _L0_xattn_in['Wk'], 'L0_xattn_bk': _L0_xattn_in['bk'], 'L0_ffn_gate_w': _L0_ffn_in['gate_w'], 'L0_ffn_gate_b': _L0_ffn_in['gate_b'], 'L0_ffn_w1': _L0_ffn_in['w1'], 'L0_ffn_b1': _L0_ffn_in['b1'], 'L0_ffn_w2': _L0_ffn_in['w2'], 'L0_ffn_b2': _L0_ffn_in['b2'], 'L1_xattn_Wq': _L1_xattn_in['Wq'], 'L1_xattn_bq': _L1_xattn_in['bq'], 'L1_xattn_Wk': _L1_xattn_in['Wk'], 'L1_xattn_bk': _L1_xattn_in['bk'], 'L1_xattn_Wv': _L1_xattn_in['Wv'], 'L1_xattn_bv': _L1_xattn_in['bv'], 'L1_xattn_Wo': _L1_xattn_in['Wo'], 'L1_xattn_bo': _L1_xattn_in['bo'], 'L1_ffn_gate_w': _L1_ffn_in['gate_w'], 'L1_ffn_gate_b': _L1_ffn_in['gate_b'], 'L1_ffn_w1': _L1_ffn_in['w1'], 'L1_ffn_b1': _L1_ffn_in['b1'], 'L1_ffn_w2': _L1_ffn_in['w2'], 'L1_ffn_b2': _L1_ffn_in['b2'], 'L2_xattn_w_q': _L2_xattn_in['w_q'], 'L2_xattn_w_k': _L2_xattn_in['w_k'], 'L2_xattn_w_v': _L2_xattn_in['w_v'], 'L2_xattn_w_o': _L2_xattn_in['w_o'], 'L2_ffn_w1': _L2_ffn_in['w1'], 'L2_ffn_b1': _L2_ffn_in['b1'], 'L2_ffn_w2': _L2_ffn_in['w2'], 'L2_ffn_b2': _L2_ffn_in['b2'], 'L3_xattn_ln_x_w': _L3_xattn_in['ln_x_w'], 'L3_xattn_ln_x_b': _L3_xattn_in['ln_x_b'], 'L3_xattn_ln_l_w': _L3_xattn_in['ln_l_w'], 'L3_xattn_ln_l_b': _L3_xattn_in['ln_l_b'], 'L3_xattn_Wq': _L3_xattn_in['Wq'], 'L3_xattn_Wkv': _L3_xattn_in['Wkv'], 'L3_xattn_q_scale': _L3_xattn_in['q_scale'], 'L3_xattn_k_scale': _L3_xattn_in['k_scale'], 'L3_xattn_Wo': _L3_xattn_in['Wo'], 'L3_xattn_ln_o_w': _L3_xattn_in['ln_o_w'], 'L3_xattn_ln_o_b': _L3_xattn_in['ln_o_b'], 'L3_ffn_gate_w': _L3_ffn_in['gate_w'], 'L3_ffn_w1': _L3_ffn_in['w1'], 'L3_ffn_b1': _L3_ffn_in['b1'], 'L3_ffn_w2': _L3_ffn_in['w2'], 'L3_ffn_b2': _L3_ffn_in['b2'], 'L3_ffn_sw1': _L3_ffn_in['sw1'], 'L3_ffn_sb1': _L3_ffn_in['sb1'], 'L3_ffn_sw2': _L3_ffn_in['sw2'], 'L3_ffn_sb2': _L3_ffn_in['sb2']}

def reference(x, ctx_1024, mask_BxS2_ik0, mask_BxS2_bk0, L0_xattn_Wq, L0_xattn_bq, L0_xattn_Wk, L0_xattn_bk, L0_ffn_gate_w, L0_ffn_gate_b, L0_ffn_w1, L0_ffn_b1, L0_ffn_w2, L0_ffn_b2, L1_xattn_Wq, L1_xattn_bq, L1_xattn_Wk, L1_xattn_bk, L1_xattn_Wv, L1_xattn_bv, L1_xattn_Wo, L1_xattn_bo, L1_ffn_gate_w, L1_ffn_gate_b, L1_ffn_w1, L1_ffn_b1, L1_ffn_w2, L1_ffn_b2, L2_xattn_w_q, L2_xattn_w_k, L2_xattn_w_v, L2_xattn_w_o, L2_ffn_w1, L2_ffn_b1, L2_ffn_w2, L2_ffn_b2, L3_xattn_ln_x_w, L3_xattn_ln_x_b, L3_xattn_ln_l_w, L3_xattn_ln_l_b, L3_xattn_Wq, L3_xattn_Wkv, L3_xattn_q_scale, L3_xattn_k_scale, L3_xattn_Wo, L3_xattn_ln_o_w, L3_xattn_ln_o_b, L3_ffn_gate_w, L3_ffn_w1, L3_ffn_b1, L3_ffn_w2, L3_ffn_b2, L3_ffn_sw1, L3_ffn_sb1, L3_ffn_sw2, L3_ffn_sb2):
    import jax
    import jax.numpy as jnp

    def _L0_xattn_ref(query, key, value, Wq, bq, Wk, bk, scale_factor, dropout_p):
        import jax, jax.numpy as jnp
        import numpy as np
        B, LQ, LKV, D = (8, 256, 256, 128)
        q = jnp.einsum('bld,ed->ble', query, Wq) + bq
        k = jnp.einsum('bld,ed->ble', key, Wk) + bk
        scores = jnp.einsum('bqd,bkd->bqk', q, k) / jnp.float32(scale_factor)
        attn = jax.nn.softmax(scores, axis=-1)
        return jnp.einsum('bqk,bkd->bqd', attn, value)

    def _L0_ffn_ref(x, gate_w, gate_b, w1, b1, w2, b2):
        import jax, jax.numpy as jnp
        import numpy as np
        B, S, D, H, E = (4, 256, 128, 512, 8)
        b, s, d = x.shape
        xf = x.reshape(-1, d)
        logits = xf @ gate_w.T + gate_b
        top1 = jnp.argmax(logits, axis=-1)
        out = jnp.zeros_like(xf)
        n_experts = w1.shape[0]
        for e in range(n_experts):
            h = jax.nn.relu(xf @ w1[e].T + b1[e])
            y = h @ w2[e].T + b2[e]
            out = out + jnp.where((top1 == e)[:, None], y, jnp.zeros((), y.dtype))
        return out.reshape(b, s, d)

    def _L1_xattn_ref(q, k, v, mask, Wq, bq, Wk, bk, Wv, bv, Wo, bo):
        import jax, jax.numpy as jnp
        import numpy as np
        D_MODEL = 128
        NUM_HEADS = 16
        D_K = D_MODEL // NUM_HEADS
        B, S, _ = q.shape

        def split(x):
            return x.reshape(B, -1, NUM_HEADS, D_K).transpose(0, 2, 1, 3)
        qh = split(q @ Wq.T + bq)
        kh = split(k @ Wk.T + bk)
        vh = split(v @ Wv.T + bv)
        scores = jnp.einsum('bhqd,bhkd->bhqk', qh, kh) / jnp.sqrt(jnp.float32(D_K))
        scores = jnp.where(mask[:, None, None, :] == 0, jnp.float32(-1000000000.0), scores)
        attn = jax.nn.softmax(scores, axis=-1)
        out = jnp.einsum('bhqk,bhkd->bhqd', attn, vh)
        out = out.transpose(0, 2, 1, 3).reshape(B, S, NUM_HEADS * D_K)
        return out @ Wo.T + bo

    def _L1_ffn_ref(x, gate_w, gate_b, w1, b1, w2, b2):
        import jax, jax.numpy as jnp
        import numpy as np
        B, S, H, F, E, K = (4, 256, 128, 512, 8, 2)
        Bb, Ss, Hh = x.shape
        xf = x.reshape(-1, Hh)
        gate = jax.nn.softmax(xf @ gate_w + gate_b)
        topv, topi = jax.lax.top_k(gate, K)
        topv = topv / topv.sum(-1, keepdims=True)
        combine = (jax.nn.one_hot(topi, gate.shape[-1], dtype=xf.dtype) * topv[..., None]).sum(1)

        def body(acc, p):
            w1e, b1e, w2e, b2e, ce = p
            h = jax.nn.relu(xf @ w1e + b1e)
            y = h @ w2e + b2e
            return (acc + y * ce[:, None], None)
        acc0 = jnp.zeros_like(xf)
        out, _ = jax.lax.scan(body, acc0, (w1, b1, w2, b2, combine.T))
        return out.reshape(Bb, Ss, Hh)

    def _L2_xattn_ref(query, kv_source, w_q, w_k, w_v, w_o):
        import jax, jax.numpy as jnp
        import numpy as np
        D_MODEL = 128
        N_HEADS = 16
        HEAD_DIM = D_MODEL // N_HEADS
        B, T_q, _ = query.shape
        T_kv = kv_source.shape[1]
        q = (query @ w_q.T).reshape(B, T_q, N_HEADS, HEAD_DIM)
        k = (kv_source @ w_k.T).reshape(B, T_kv, N_HEADS, HEAD_DIM)
        v = (kv_source @ w_v.T).reshape(B, T_kv, N_HEADS, HEAD_DIM)
        scale = HEAD_DIM ** (-0.5)
        attn = jax.nn.softmax(jnp.einsum('bqhd,bkhd->bhqk', q, k) * scale, axis=-1)
        out = jnp.einsum('bhqk,bkhd->bqhd', attn, v).reshape(B, T_q, D_MODEL)
        return out @ w_o.T

    def _L2_ffn_ref(x, w1, b1, w2, b2):
        import jax, jax.numpy as jnp
        import numpy as np
        MANT_BITS = 8
        _PWL_X = jnp.linspace(-4.0, 4.0, 33, dtype=jnp.float32)
        _PWL_Y = 0.5 * _PWL_X * (1.0 + jax.lax.erf(_PWL_X / jnp.sqrt(jnp.float32(2.0))))

        def float2fix(x, mantissa_bits):
            s = jnp.float32(2.0 ** mantissa_bits)
            q = jnp.round(x * s) / s
            return x + jax.lax.stop_gradient(q - x)

        def pwlin_gelu_basic(x, mantissa_bits_in, mantissa_bits_out):
            xq = float2fix(x, mantissa_bits_in)
            y = jnp.interp(xq, _PWL_X, _PWL_Y)
            y = jnp.where(xq > 4.0, xq, jnp.where(xq < -4.0, jnp.float32(0.0), y))
            return float2fix(y, mantissa_bits_out)
        h = jnp.einsum('bsd,df->bsf', x, w1) + b1
        h = float2fix(h, MANT_BITS)
        h = pwlin_gelu_basic(h, MANT_BITS, MANT_BITS)
        h = float2fix(h, MANT_BITS)
        out = jnp.einsum('bsf,fd->bsd', h, w2) + b2
        return float2fix(out, MANT_BITS)

    def _L3_xattn_ref(x, latents, mask, ln_x_w, ln_x_b, ln_l_w, ln_l_b, Wq, Wkv, q_scale, k_scale, Wo, ln_o_w, ln_o_b):
        import jax, jax.numpy as jnp
        import numpy as np
        DIM, DIM_HEAD, HEADS, SCALE = (128, 64, 8, 8.0)
        INNER = DIM_HEAD * HEADS
        LN_EPS = 1e-05
        L2_EPS = 1e-12

        def layer_norm(x, w, b):
            mu = jnp.mean(x, axis=-1, keepdims=True)
            var = jnp.mean(jnp.square(x - mu), axis=-1, keepdims=True)
            return (x - mu) * jax.lax.rsqrt(var + LN_EPS) * w + b

        def l2norm(t):
            n = jnp.sqrt(jnp.sum(jnp.square(t), axis=-1, keepdims=True))
            return t / jnp.maximum(n, L2_EPS)
        b, n, _ = x.shape
        m = latents.shape[1]
        x = layer_norm(x, ln_x_w, ln_x_b)
        latents = layer_norm(latents, ln_l_w, ln_l_b)
        q = latents @ Wq
        kv_input = jnp.concatenate([x, latents], axis=1)
        kv = kv_input @ Wkv
        k, v = jnp.split(kv, 2, axis=-1)

        def to_heads(t):
            return t.reshape(t.shape[0], t.shape[1], HEADS, DIM_HEAD).transpose(0, 2, 1, 3)
        q, k, v = map(to_heads, (q, k, v))
        q = l2norm(q) * q_scale
        k = l2norm(k) * k_scale
        sim = jnp.einsum('bhid,bhjd->bhij', q, k) * SCALE
        full_mask = jnp.concatenate([mask, jnp.ones((b, m), dtype=bool)], axis=1)[:, None, None, :]
        max_neg = -jnp.finfo(sim.dtype).max
        sim = jnp.where(full_mask, sim, max_neg)
        attn = jax.nn.softmax(sim.astype(jnp.float32), axis=-1).astype(sim.dtype)
        out = jnp.einsum('bhij,bhjd->bhid', attn, v)
        out = out.transpose(0, 2, 1, 3).reshape(b, m, INNER)
        return layer_norm(out @ Wo, ln_o_w, ln_o_b)

    def _L3_ffn_ref(x, gate_w, w1, b1, w2, b2, sw1, sb1, sw2, sb2):
        import jax, jax.numpy as jnp
        import numpy as np
        D_MODEL = 128
        HIDDEN = 512
        N_ROUTING = 2
        B, S, D = x.shape
        xf = x.reshape(-1, D)
        gate_scores = xf @ gate_w.T
        gate_probs = jax.nn.softmax(gate_scores, axis=-1)
        top1 = jnp.argmax(gate_probs, axis=-1)
        one_hot = jax.nn.one_hot(top1, N_ROUTING, dtype=xf.dtype)
        masked = xf[None, :, :] * one_hot.T[:, :, None]
        h = jax.nn.relu(jnp.einsum('end,edh->enh', masked, w1) + b1[:, None, :])
        expert_out = jnp.einsum('enh,ehd->end', h, w2) + b2[:, None, :]
        routing_output = expert_out.sum(axis=0)
        shared = jax.nn.relu(xf @ sw1 + sb1) @ sw2 + sb2
        return (routing_output + shared).reshape(B, S, D)
    x = x + _L0_xattn_ref(_layernorm(x, axis=-1), ctx_1024, ctx_1024, L0_xattn_Wq, L0_xattn_bq, L0_xattn_Wk, L0_xattn_bk, 32, 0)
    x = x + _L0_ffn_ref(_layernorm(x, axis=-1), L0_ffn_gate_w, L0_ffn_gate_b, L0_ffn_w1, L0_ffn_b1, L0_ffn_w2, L0_ffn_b2)
    x = x + _L1_xattn_ref(_layernorm(x, axis=-1), ctx_1024, ctx_1024, mask_BxS2_ik0, L1_xattn_Wq, L1_xattn_bq, L1_xattn_Wk, L1_xattn_bk, L1_xattn_Wv, L1_xattn_bv, L1_xattn_Wo, L1_xattn_bo)
    x = x + _L1_ffn_ref(_layernorm(x, axis=-1), L1_ffn_gate_w, L1_ffn_gate_b, L1_ffn_w1, L1_ffn_b1, L1_ffn_w2, L1_ffn_b2)
    x = x + _L2_xattn_ref(_layernorm(x, axis=-1), ctx_1024, L2_xattn_w_q, L2_xattn_w_k, L2_xattn_w_v, L2_xattn_w_o)
    x = x + _L2_ffn_ref(_layernorm(x, axis=-1), L2_ffn_w1, L2_ffn_b1, L2_ffn_w2, L2_ffn_b2)
    x = x + _L3_xattn_ref(ctx_1024, _layernorm(x, axis=-1), mask_BxS2_bk0, L3_xattn_ln_x_w, L3_xattn_ln_x_b, L3_xattn_ln_l_w, L3_xattn_ln_l_b, L3_xattn_Wq, L3_xattn_Wkv, L3_xattn_q_scale, L3_xattn_k_scale, L3_xattn_Wo, L3_xattn_ln_o_w, L3_xattn_ln_o_b)
    x = x + _L3_ffn_ref(_layernorm(x, axis=-1), L3_ffn_gate_w, L3_ffn_w1, L3_ffn_b1, L3_ffn_w2, L3_ffn_b2, L3_ffn_sw1, L3_ffn_sb1, L3_ffn_sw2, L3_ffn_sb2)
    return x

_drawn_inputs = setup_inputs


def setup_inputs(seed=0):
    import zlib

    import numpy as np

    out = dict(_drawn_inputs(seed))
    spreads = {'L1_ffn_gate_b': (0.0, 0.1),
     'L1_ffn_b1': (0.0, 0.1),
     'L1_ffn_b2': (0.0, 0.1),
     'L3_xattn_ln_x_w': (1.0, 0.2),
     'L3_xattn_ln_x_b': (0.0, 0.1),
     'L3_xattn_ln_l_w': (1.0, 0.2),
     'L3_xattn_ln_l_b': (0.0, 0.1),
     'L3_xattn_q_scale': (1.0, 0.2),
     'L3_xattn_k_scale': (1.0, 0.2),
     'L3_xattn_ln_o_w': (1.0, 0.2),
     'L3_xattn_ln_o_b': (0.0, 0.1)}
    factors = {'L0_xattn_bq': 6.651,
     'L0_xattn_bk': 8.0,
     'L1_xattn_bk': 8.0,
     'L2_ffn_b1': 5.168,
     'L2_ffn_b2': 3.437,
     'L3_ffn_b1': 8.0,
     'L3_ffn_b2': 3.381,
     'L3_ffn_sb1': 8.0,
     'L3_ffn_sb2': 4.591}
    for name, (base, spread) in spreads.items():
        noise = np.random.default_rng([zlib.crc32(name.encode()), seed]).standard_normal(out[name].shape)
        drawn = base * np.exp(spread * noise) if base else spread * noise
        out[name] = jnp.asarray(drawn.astype(out[name].dtype))
    for name, factor in factors.items():
        out[name] = (out[name] * factor).astype(out[name].dtype)
    return out
```

```python
from contextlib import ExitStack

import concourse.bass as bass
from concourse import mybir

F32 = mybir.dt.float32
F32R = mybir.dt.float32r
I32 = mybir.dt.int32
ALU = mybir.AluOpType
ACT = mybir.ActivationFunctionType
AX = mybir.AxisListType

B, SQ, D = 32, 56, 128
SK = 1500
KT = 12
KP = SK // KT
TOK = B * SQ
NCH = 4
CH = TOK // NCH
NKC = 3
KC = SK // NKC
E, HID = 8, 512
HT = HID // D
TT = TOK // D
H16, DK = 16, 8
HQ = H16 * SQ
RT = HQ // D
H8, DH = 8, 64
HQ3 = H8 * SQ
LN_EPS, L2_EPS = 1e-5, 1e-12
MAGIC = 12582912.0
MASKED = -1e9
NEVER = -1e30


class Shared:
    norms = scaled_steps = products = loads = 0


def bcast(ap, n, at):
    shape = list(ap.shape)
    return ap.unsqueeze(at).broadcast_to(shape[:at] + [n] + shape[at:])


def pipelined(eng, prepare, consume):
    prepare(0, 0, 0)
    prepare(1, 1, 0)
    consume(0, 0, 0)
    prepare(2, 0, 1)
    consume(1, 1, 0)
    with eng.Fori(1, B // 2 - 1) as j:
        prepare(j * 2 + 1, 1, j)
        consume(j * 2, 0, j)
        prepare(j * 2 + 2, 0, j + 1)
        consume(j * 2 + 1, 1, j)
    prepare(B - 1, 1, B // 2 - 1)
    consume(B - 2, 0, B // 2 - 1)
    consume(B - 1, 1, B // 2 - 1)


def one_ahead(eng, first, step, last):
    first(0, 0, 0)
    step(0, 0, 0)
    with eng.Fori(0, B // 2 - 1) as j:
        step(j * 2 + 1, 1, j)
        step(j * 2 + 2, 0, j + 1)
    last(B - 1, 1, B // 2 - 1)


def following(u, i):
    return (1 - u, i) if u == 0 else (0, i + 1)


def nothing(b, u, i):
    pass


def wait(eng, sem, value):
    if not isinstance(value, int) or value > 0:
        eng.wait_ge(sem, value)


def plain(eng, s):
    eng.wait_ge(s.x_loaded, 16)


def start_at_one(nc, sems):
    with nc.Block() as block:
        @block.sync
        def _(sp):
            for sem in sems:
                sp.sem_inc(sem, 1)


def clear(nc, sems):
    with nc.Block() as block:
        @block.gpsimd
        def _(pool):
            for sem in sems:
                pool.sem_clear(sem)


def batch_of(b):
    return bass.ds(b * SQ, SQ)


def setup(nc, s, a):
    zeroed, consts_made = s.zeroed, s.consts_made
    with nc.Block() as block:
        @block.sync
        def _(sp):
            sp.dma_start(s.x_T[:, :], a["x_T"]).then_inc(s.x_loaded, 16)
            sp.wait_ge(s.x_loaded, 16)

        @block.gpsimd
        def _(pool):
            nc.gpsimd.memset(s.ident[:, :], 0.0).then_inc(zeroed, 1)
            pool.wait_ge(zeroed, 1)
            nc.gpsimd.affine_select(out=s.ident[:, :], in_=s.ident[:, :], compare_op=ALU.not_equal, fill=1.0,
                                    base=0, pattern=[[-1, D]], channel_multiplier=1).then_inc(consts_made, 1)

        @block.vector
        def _(dve):
            nc.vector.memset(s.ones[:, :], 1.0).then_inc(consts_made, 1)
            nc.vector.memset(s.average[:, :], 1.0 / D).then_inc(consts_made, 1)
            nc.vector.memset(s.eps[:, :], LN_EPS).then_inc(consts_made, 1)


def layer_norm(nc, s, name, src, dst, weight=None, bias=None, add_to=None):
    n0, scaled0 = s.norms * NCH, s.scaled_steps
    steps = 1 + (weight is not None) + (add_to is not None)
    s.norms += 1
    s.scaled_steps += steps * NCH
    with ExitStack() as ctx:
        squares = ctx.enter_context(nc.sbuf_tensor(f"{name}_squares", [D, NCH, CH], F32))
        std = ctx.enter_context(nc.sbuf_tensor(f"{name}_std", [D, NCH, CH], F32))
        block = ctx.enter_context(nc.Block())

        def cols(t, c):
            return t[:, c * CH:(c + 1) * CH]

        @block.tensor
        def _(pe):
            for c in range(NCH):
                nc.tensor.matmul(s.ps[:, c, 0:CH], s.average[:, :], cols(src, c), start=True, stop=True)\
                    .then_inc(s.means_made, 1)
            for c in range(NCH):
                pe.wait_ge(s.squared, n0 + c + 1)
                nc.tensor.matmul(s.ps[:, NCH + c, 0:CH], s.average[:, :], squares[:, c, :], start=True, stop=True)\
                    .then_inc(s.vars_made, 1)

        @block.gpsimd
        def _(pool):
            for c in range(NCH):
                pool.wait_ge(s.centred, n0 + c + 1)
                nc.gpsimd.tensor_tensor(squares[:, c, :], cols(dst, c), cols(dst, c), ALU.mult).then_inc(s.squared, 1)

        @block.scalar
        def _(act):
            for c in range(NCH):
                act.wait_ge(s.vars_made, n0 + c + 1)
                nc.scalar.activation(std[:, c, :], s.ps[:, NCH + c, 0:CH], ACT.Sqrt, bias=s.eps[:, 0:1])\
                    .then_inc(s.std_made, 1)

        @block.vector
        def _(dve):
            for c in range(NCH):
                dve.wait_ge(s.means_made, n0 + c + 1)
                nc.vector.tensor_tensor(cols(dst, c), cols(src, c), s.ps[:, c, 0:CH], ALU.subtract)\
                    .then_inc(s.centred, 1)
            for c in range(NCH):
                dve.wait_ge(s.std_made, n0 + c + 1)
                nc.vector.reciprocal(std[:, c, :], std[:, c, :]).then_inc(s.inverted, 1)
                dve.wait_ge(s.inverted, n0 + c + 1)
                dve.wait_ge(s.squared, n0 + c + 1)
                nc.vector.tensor_tensor(cols(dst, c), cols(dst, c), std[:, c, :], ALU.mult).then_inc(s.scaled, 1)
                if weight is not None:
                    dve.wait_ge(s.scaled, scaled0 + c * steps + 1)
                    nc.vector.tensor_scalar(cols(dst, c), cols(dst, c), weight, bias, ALU.mult, ALU.add)\
                        .then_inc(s.scaled, 1)
                if add_to is not None:
                    dve.wait_ge(s.scaled, scaled0 + c * steps + 2)
                    nc.vector.tensor_tensor(cols(add_to, c), cols(add_to, c), cols(dst, c), ALU.add)\
                        .then_inc(s.scaled, 1)


def project(nc, s, pairs):
    n0 = s.products
    s.products += len(pairs) * NCH
    with nc.Block() as block:
        @block.tensor
        def _(pe):
            n = 0
            for i, (dst, w, src, bias, scale) in enumerate(pairs):
                if i:
                    pe.wait_ge(s.product_taken, n0 + n)
                for c in range(NCH):
                    nc.tensor.matmul(s.ps[0:w.shape[1], n % 8, 0:CH], w, src[:, c * CH:(c + 1) * CH],
                                     start=True, stop=True).then_inc(s.product_made, 1)
                    n += 1

        @block.vector
        def _(dve):
            n = 0
            for dst, w, src, bias, scale in pairs:
                for c in range(NCH):
                    dve.wait_ge(s.product_made, n0 + n + 1)
                    nc.vector.tensor_scalar(dst[:, c * CH:(c + 1) * CH], s.ps[0:w.shape[1], n % 8, 0:CH],
                                            0.0 if bias is None else bias, scale, ALU.add, ALU.mult)\
                        .then_inc(s.product_taken, 1)
                    n += 1


def load(nc, s, pairs):
    s.loads += len(pairs)
    with nc.Block() as block:
        @block.sync
        def _(sp):
            for dst, src in pairs:
                sp.dma_start(dst, src).then_inc(s.loaded, 16)
            sp.wait_ge(s.loaded, 16 * s.loads)


def start_moe_loads(nc, s, a, layer, moe_loaded):
    with nc.Block() as block:
        @block.sync
        def _(sp):
            sp.dma_start(s.w1[:, :], a[f"{layer}_w1"]).then_inc(moe_loaded, 16)
            sp.dma_start(s.w2[:, :], a[f"{layer}_w2"]).then_inc(moe_loaded, 16)


def attention_one_head(nc, s, a):
    with ExitStack() as ctx:
        def sb(name, shape, dt=F32):
            return ctx.enter_context(nc.sbuf_tensor(f"a0_{name}", shape, dt))

        sems = []

        def sem(name):
            sems.append(ctx.enter_context(nc.semaphore(f"a0_{name}")))
            return sems[-1]

        wq, wk, bias = sb("wq", [D, D]), sb("wk", [D, D]), sb("bias", [D, 2])
        q, qk, qbk = sb("q", [D, TOK]), sb("qk", [D, TOK]), sb("qbk", [1, TOK])
        q_b = [sb(f"q_b{u}", [D, SQ]) for u in range(2)]
        q_r = [sb(f"q_r{u}", [D, SQ], F32R) for u in range(2)]
        ctx_N = [sb(f"ctx_N{u}", [KP, KT, D]) for u in range(2)]
        ctx_T = [sb(f"ctx_T{u}", [D, KT, KP]) for u in range(2)]
        ctx_R = [sb(f"ctx_R{u}", [D, SK], F32R) for u in range(2)]
        max_col = sb("max_col", [SQ, 2])
        shift = sb("shift", [1, 2, SQ])
        probs = [sb(f"probs{u}", [KP, KT, SQ]) for u in range(2)]
        prob_sum = sb("prob_sum", [KP, 2, SQ])
        inv, delta = sb("inv", [D, 2, SQ]), sb("delta", [D, 2, SQ])

        load(nc, s, [(wq[:, :], a["L0_WqT"]), (wk[:, :], a["L0_Wk"]), (bias[:, 0:1], a["L0_bq"]),
                           (bias[:, 1:2], a["L0_bk"])])
        project(nc, s, [(q, wq[:, :], s.xn, bias[:, 0:1], 1.0 / 32), (qk, wk[:, :], q, None, 1.0),
                               (qbk, bias[:, 1:2], q, None, 1.0)])

        loaded = [sem("even_loaded"), sem("odd_loaded")]
        q_taken, rounded, rows_made, max_made, max_turned, shift_made = (
            sem(n) for n in ("q_taken", "rounded", "rows_made", "max_made", "max_turned", "shift_made"))
        scores_made, probs_made, summed, out_made, inverted, scaled, added = (
            sem(n) for n in ("scores_made", "probs_made", "summed", "out_made", "inverted", "scaled", "added"))
        HALF = KT // 2
        batches = ExitStack()
        block = batches.enter_context(nc.Block())

        @block.sync
        def _(sp):
            def fetch(b, u):
                wait(sp, out_made, b - 1)
                sp.dma_start(ctx_T[u][:, :, :], a["ctx_T"][bass.ds(b, 1)].rearrange("a d (t p) -> (a d) t p", t=KT))\
                    .then_inc(loaded[u], 16)
                sp.dma_start(ctx_N[u][:, :, :], a["ctx_N"][bass.ds(b, 1)].rearrange("a (p t) d -> (a p) t d", t=KT))\
                    .then_inc(loaded[u], 16)
            fetch(0, 0)
            fetch(1, 1)
            with sp.Fori(1, B // 2) as j:
                fetch(j * 2, 0)
                fetch(j * 2 + 1, 1)

        @block.gpsimd
        def _(pool):
            def prepare(b, u, i):
                wait(pool, scores_made, b - 1)
                nc.gpsimd.tensor_copy(q_b[u][:, :], qk[:, batch_of(b)]).then_inc(q_taken, 1)
                nc.gpsimd.tensor_copy(q_r[u][:, :], qk[:, batch_of(b)]).then_inc(q_taken, 1)
            pipelined(pool, prepare, nothing)

        @block.tensor
        def _(pe):
            def prepare(b, u, i):
                pe.wait_ge(rounded, b + 1)
                pe.wait_ge(q_taken, b * 2 + 2)
                wait(pe, max_made, b)
                for k in range(NKC):
                    mm = nc.tensor.matmul(s.ps[0:SQ, k, 0:KC], q_r[u][:, :], ctx_R[u][:, k * KC:(k + 1) * KC],
                                          start=True, stop=True)
                mm.then_inc(rows_made, 1)

            def consume(b, u, i):
                plain(pe, s)
                pe.wait_ge(max_made, b + 1)
                wait(pe, added, b)
                nc.tensor.transpose(s.ps[0:1, 7, 0:SQ], max_col[:, u:u + 1], s.ident[0:SQ, 0:SQ])\
                    .then_inc(max_turned, 1)
                wait(pe, probs_made, b - 1)
                for h in range(2):
                    for t in range(HALF):
                        nc.tensor.matmul(s.ps[0:KP, 3 + 2 * u + h, t * SQ:(t + 1) * SQ], ctx_T[u][:, h * HALF + t, :],
                                         q_b[u][:, :], start=(t == 0), stop=False, skip_group_check=True)
                pe.wait_ge(shift_made, b + 1)
                for h in range(2):
                    mm = nc.tensor.matmul(s.ps[0:KP, 3 + 2 * u + h, 0:HALF * SQ], s.ones[0:1, 0:KP],
                                          bcast(shift[:, u, :], HALF, 1), start=False, stop=True,
                                          skip_group_check=True)
                mm.then_inc(scores_made, 1)
                pe.wait_ge(probs_made, b + 1)
                for t in range(KT):
                    nc.tensor.matmul(s.ps[:, 7, 64:64 + SQ], ctx_N[u][:, t, :], probs[u][:, t, :],
                                     start=(t == 0), stop=False, skip_group_check=True)
                pe.wait_ge(summed, b + 1)
                nc.tensor.matmul(s.ps[:, 7, 128:128 + SQ], s.ones[0:KP, :], prob_sum[:, u, :],
                                 start=False, stop=True, skip_group_check=True).then_inc(out_made, 1)

            pipelined(pe, prepare, consume)

        @block.scalar
        def _(act):
            def consume(b, u, i):
                act.wait_ge(scores_made, b + 1)
                wait(act, out_made, b - 1)
                wait(act, summed, b - 1)
                nc.scalar.activation(probs[u][:, :, :].rearrange("p (h t) q -> p h (t q)", h=2),
                                     s.ps[0:KP, 3 + 2 * u:5 + 2 * u, 0:HALF * SQ], ACT.Exp).then_inc(probs_made, 1)
            pipelined(act, nothing, consume)

        @block.vector
        def _(dve):
            def prepare(b, u, i):
                dve.wait_ge(loaded[u], i * 32 + 32)
                wait(dve, rows_made, b - 1)
                nc.vector.tensor_copy(ctx_R[u][:, :].rearrange("d (t p) -> d t p", t=KT), ctx_T[u][:, :, :])\
                    .then_inc(rounded, 1)
                dve.wait_ge(rows_made, b + 1)
                wait(dve, max_turned, b - 1)
                nc.vector.tensor_reduce(max_col[:, u:u + 1], s.ps[0:SQ, 0:NKC, 0:KC], AX.XY, ALU.max)\
                    .then_inc(max_made, 1)

            def consume(b, u, i):
                dve.wait_ge(max_turned, b + 1)
                wait(dve, scores_made, b - 1)
                nc.vector.tensor_tensor(delta[0:1, u, :], s.ps[0:1, 7, 0:SQ], qbk[0:1, batch_of(b)], ALU.add)\
                    .then_inc(inverted, 1)
                dve.wait_ge(inverted, b * 2 + 1)
                nc.vector.tensor_tensor(shift[:, u, :], qbk[0:1, batch_of(b)], delta[0:1, u, :], ALU.subtract)\
                    .then_inc(shift_made, 1)
                dve.wait_ge(probs_made, b + 1)
                wait(dve, out_made, b - 1)
                nc.vector.tensor_reduce(prob_sum[:, u, :], probs[u][:, :, :].rearrange("p t q -> p q t"), AX.X,
                                        ALU.add).then_inc(summed, 1)
                dve.wait_ge(out_made, b + 1)
                nc.vector.reciprocal(inv[:, u, :], s.ps[:, 7, 128:128 + SQ]).then_inc(inverted, 1)
                dve.wait_ge(inverted, b * 2 + 2)
                nc.vector.tensor_tensor(delta[:, u, :], s.ps[:, 7, 64:64 + SQ], inv[:, u, :], ALU.mult)\
                    .then_inc(scaled, 1)
                dve.wait_ge(scaled, b + 1)
                nc.vector.tensor_tensor(s.x_T[:, batch_of(b)], s.x_T[:, batch_of(b)], delta[:, u, :], ALU.add)\
                    .then_inc(added, 1)

            pipelined(dve, prepare, consume)

        batches.close()
        clear(nc, sems)


def mixture(nc, s, a, layer, moe_loaded, top2):
    with ExitStack() as ctx:
        def sb(name, shape, dt=F32):
            return ctx.enter_context(nc.sbuf_tensor(f"{layer}f_{name}", shape, dt))

        sems = []

        def sem(name):
            sems.append(ctx.enter_context(nc.semaphore(f"{layer}f_{name}")))
            return sems[-1]

        gate_w, gate_b = sb("gate_w", [D, E]), sb("gate_b", [1, E])
        b1, neg_b1, b2 = sb("b1", [D, E, HT]), sb("neg_b1", [D, E, HT]), sb("b2", [E, D])
        b1_blocks = sb("b1_blocks", [D, E, HT, E])
        rank = sb("rank", [D, E])
        logits, best, eq, won, second, gates = (sb(n, [D, TT, E]) for n in
                                                ("logits", "best", "eq", "won", "second", "gates"))
        row_max, row_rank = sb("row_max", [D, TT]), sb("row_rank", [D, TT])
        weight_hi, weight_lo = sb("weight_hi", [E, TOK], F32R), sb("weight_lo", [E, TOK], F32R)
        weight_T = sb("weight_T", [E, TOK])
        pick = sb("pick", [E, E, D], F32R)
        expert_bias = sb("expert_bias", [E, D])
        spread = sb("spread", [D, 2, CH])
        hidden = sb("hidden", [D, 4, CH])

        load(nc, s, [(gate_w[:, :], a[f"{layer}_gate_w"]), (gate_b[:, :], a[f"{layer}_gate_b"]),
                                  (b1[:, :, :].rearrange("p e j -> p (e j)"), a[f"{layer}_b1"]),
                                  (b2[:, :], a[f"{layer}_b2"])])

        logits_made, gates_ready, step, exps_made, bias_made, rank_made = (
            sem(n) for n in ("logits_made", "gates_ready", "step", "exps_made", "bias_made", "rank_made"))
        with nc.Block() as block:
            @block.tensor
            def _(pe):
                for t in range(TT):
                    nc.tensor.matmul(s.ps[:, 7, t * E:(t + 1) * E], s.xn[:, t * D:(t + 1) * D], gate_w[:, :],
                                     start=(t == 0), stop=False, skip_group_check=True)
                    mm = nc.tensor.matmul(s.ps[:, 7, t * E:(t + 1) * E], s.ones[0:1, :], gate_b[:, :],
                                          start=False, stop=True, skip_group_check=True)
                mm.then_inc(logits_made, 1)
                pe.wait_ge(moe_loaded, 32)
                pe.wait_ge(bias_made, 2)
                for n in range(E * HT):
                    mm = nc.tensor.matmul(s.ps[0:E, 6, 0:D], b1_blocks[:, n // HT, n % HT, :],
                                          s.w2[:, n * D:(n + 1) * D], start=(n == 0), stop=(n == E * HT - 1))
                mm.then_inc(logits_made, 1)
                pe.wait_ge(gates_ready, 1)
                for t in range(TT):
                    mm = nc.tensor.transpose(s.ps[0:E, t // 4, (t % 4) * D:(t % 4 + 1) * D], gates[:, t, :], s.ident[:, :])
                mm.then_inc(logits_made, 1)

            @block.scalar
            def _(act):
                if top2:
                    act.wait_ge(exps_made, 1)
                    nc.scalar.activation(best[:, :, :], best[:, :, :], ACT.Exp).then_inc(exps_made, 1)

            @block.gpsimd
            def _(pool):
                nc.gpsimd.memset(b1_blocks[:, :, :, :], 0.0).then_inc(bias_made, 1)
                for e in range(E):
                    nc.gpsimd.memset(rank[:, e:e + 1], float(E - e)).then_inc(rank_made, 1)

            @block.vector
            def _(dve):
                count = [0]

                def chain(ins):
                    count[0] += 1
                    ins.then_inc(step, 1)
                    dve.wait_ge(step, count[0])

                dve.wait_ge(bias_made, 1)
                for e in range(E):
                    ins = nc.vector.tensor_copy(b1_blocks[:, e, :, e], b1[:, e, :])
                ins.then_inc(bias_made, 1)
                chain(nc.vector.tensor_scalar(neg_b1[:, :, :], b1[:, :, :], -1.0, None, ALU.mult))
                chain(nc.vector.tensor_copy(pick[:, :, :], bcast(s.ident[0:E, 0:E], D, 2)))
                dve.wait_ge(rank_made, E)
                dve.wait_ge(logits_made, 1)
                chain(nc.vector.tensor_copy(logits[:, :, :].rearrange("p t e -> p (t e)"), s.ps[:, 7, 0:TT * E]))

                def choose(values, chosen):
                    chain(nc.vector.tensor_reduce(row_max[:, :], values[:, :, :], AX.X, ALU.max))
                    chain(nc.vector.tensor_tensor(eq[:, :, :], values[:, :, :], bcast(row_max[:, :], E, 2), ALU.is_equal))
                    chain(nc.vector.tensor_tensor(eq[:, :, :], eq[:, :, :], bcast(rank[:, :], TT, 1), ALU.mult))
                    chain(nc.vector.tensor_reduce(row_rank[:, :], eq[:, :, :], AX.X, ALU.max))
                    chain(nc.vector.tensor_tensor(chosen[:, :, :], eq[:, :, :], bcast(row_rank[:, :], E, 2), ALU.is_equal))

                choose(logits, won)
                if top2:
                    nc.vector.tensor_tensor(best[:, :, :], logits[:, :, :], bcast(row_max[:, :], E, 2), ALU.subtract)\
                        .then_inc(exps_made, 1)
                    chain(nc.vector.scalar_tensor_tensor(logits[:, :, :], won[:, :, :], -1e38, logits[:, :, :],
                                                         ALU.mult, ALU.add))
                    dve.wait_ge(exps_made, 2)
                    choose(logits, second)
                    chain(nc.vector.tensor_tensor(won[:, :, :], won[:, :, :], second[:, :, :], ALU.add))
                    chain(nc.vector.tensor_tensor(won[:, :, :], won[:, :, :], best[:, :, :], ALU.mult))
                    chain(nc.vector.tensor_reduce(row_max[:, :], won[:, :, :], AX.X, ALU.add))
                    chain(nc.vector.reciprocal(row_max[:, :], row_max[:, :]))
                    chain(nc.vector.tensor_tensor(won[:, :, :], won[:, :, :], bcast(row_max[:, :], E, 2), ALU.mult))
                nc.vector.tensor_copy(gates[:, :, :], won[:, :, :]).then_inc(gates_ready, 1)
                dve.wait_ge(logits_made, 2)
                chain(nc.vector.tensor_tensor(expert_bias[:, :], s.ps[0:E, 6, 0:D], b2[:, :], ALU.add))
                dve.wait_ge(logits_made, 3)
                for k in range(4):
                    n = min(4, TT - 4 * k) * D
                    chain(nc.vector.tensor_copy(weight_T[:, 4 * k * D:4 * k * D + n], s.ps[0:E, k, 0:n]))
                chain(nc.vector.tensor_copy(weight_hi[:, :], weight_T[:, :]))
                chain(nc.vector.tensor_tensor(weight_lo[:, :], weight_T[:, :], weight_hi[:, :].bitcast(F32), ALU.subtract))

        hidden_made, hidden_taken, out_made, out_taken, spread_made, spread_taken = (
            sem(n) for n in ("hidden_made", "hidden_taken", "out_made", "out_taken", "spread_made", "spread_taken"))
        start_at_one(nc, [spread_taken, hidden_taken, out_taken, out_made])
        NT = E * HT
        with nc.Block() as block:
            @block.tensor
            def _(pe):
                with pe.Fori(0, NCH) as c:
                    def spread_weights(e):
                        mm = nc.tensor.matmul(s.ps[:, 5 + e % 2, 0:CH], pick[:, e, :], weight_hi[:, bass.ds(c * CH, CH)],
                                              start=True, stop=not top2)
                        if top2:
                            mm = nc.tensor.matmul(s.ps[:, 5 + e % 2, 0:CH], pick[:, e, :],
                                                  weight_lo[:, bass.ds(c * CH, CH)], start=False, stop=True)
                        mm.then_inc(spread_made, 1)

                    def first_product(n):
                        if n % HT == 0:
                            pe.wait_ge(spread_taken, 1 + c * E + max(n // HT - 1, 0))
                        if n >= 4:
                            pe.wait_ge(hidden_taken, 1 + c * NT + n - 3)
                        else:
                            pe.wait_ge(hidden_taken, 1 + c * NT)
                        nc.tensor.matmul(s.ps[:, n % 4, 0:CH], s.w1[:, n * D:(n + 1) * D],
                                         s.xn[:, bass.ds(c * CH, CH)], start=True, stop=True).then_inc(hidden_made, 1)

                    def second_product(n):
                        pe.wait_ge(hidden_taken, 1 + c * NT + n + 1)
                        mm = nc.tensor.matmul(s.ps[:, 4, 0:CH], s.w2[:, n * D:(n + 1) * D], hidden[:, n % 4, :],
                                              start=False, stop=(n == NT - 1))
                        mm.then_inc(out_made, 1)

                    pe.wait_ge(out_taken, 1 + c)
                    nc.tensor.matmul(s.ps[:, 4, 0:CH], expert_bias[:, :], weight_T[:, bass.ds(c * CH, CH)],
                                     start=True, stop=False)
                    for n in range(NT + 2):
                        if n < NT:
                            first_product(n)
                            if n % HT == 0:
                                spread_weights(n // HT)
                        if n >= 2:
                            second_product(n - 2)

            @block.scalar
            def _(act):
                with act.Fori(0, NCH) as c:
                    for e in range(E):
                        act.wait_ge(spread_made, c * E + e + 1)
                        if e >= 2:
                            act.wait_ge(hidden_taken, 1 + c * NT + (e - 1) * HT)
                        else:
                            act.wait_ge(hidden_taken, 1 + c * NT)
                        nc.scalar.activation(spread[:, e % 2, :], s.ps[:, 5 + e % 2, 0:CH], ACT.Copy)\
                            .then_inc(spread_taken, 1)

            @block.vector
            def _(dve):
                with dve.Fori(0, NCH) as c:
                    for n in range(NT):
                        e = n // HT
                        dve.wait_ge(hidden_made, c * NT + n + 1)
                        dve.wait_ge(spread_taken, 1 + c * E + e + 1)
                        if n >= 4:
                            dve.wait_ge(out_made, 1 + c * NT + n - 3)
                        else:
                            dve.wait_ge(out_made, 1 + c * NT)
                        nc.vector.scalar_tensor_tensor(hidden[:, n % 4, :], s.ps[:, n % 4, 0:CH],
                                                       neg_b1[:, e, n % HT:n % HT + 1], spread[:, e % 2, :],
                                                       ALU.max, ALU.mult).then_inc(hidden_taken, 1)
                    dve.wait_ge(out_made, 1 + c * NT + NT)
                    nc.vector.tensor_tensor(s.x_T[:, bass.ds(c * CH, CH)], s.x_T[:, bass.ds(c * CH, CH)],
                                            s.ps[:, 4, 0:CH], ALU.add).then_inc(out_taken, 1)

        clear(nc, sems)


def attention_16_heads(nc, s, a, layer, masked, biased):
    with ExitStack() as ctx:
        def sb(name, shape, dt=F32):
            return ctx.enter_context(nc.sbuf_tensor(f"{layer}a_{name}", shape, dt))

        def sem(name):
            return ctx.enter_context(nc.semaphore(f"{layer}a_{name}"))

        wq, wk, wv, wo = (sb(n, [D, D]) for n in ("wq", "wk", "wv", "wo_nat"))
        wo_quad = sb("wo_quad", [D, 4, D])
        bias = sb("bias", [D, 4])
        bv_quad = sb("bv_quad", [D, 4])
        head_mask = sb("head_mask", [D, H16])
        sum_rows = sb("sum_rows", [D, 4, 32])
        ones_2 = sb("ones_2", [2, D], F32R)
        q = sb("q", [D, TOK])
        q_lo = sb("q_lo", [D, TOK])
        heads_out = sb("heads_out", [D, 4, TOK])
        ctx_T = [sb(f"ctx_T{u}", [D, KT, KP]) for u in range(2)]
        k_full = sb("k_full", [D, SK])
        k_hi = [sb(f"k_hi{u}", [D, SK], F32R) for u in range(2)]
        k_lo = [sb(f"k_lo{u}", [D, SK], F32R) for u in range(2)]
        v = [sb(f"v{u}", [KP, KT, H16, DK + 1]) for u in range(2)]
        qd_hi = [sb(f"qd_hi{u}", [D, HQ], F32R) for u in range(2)]
        qd_lo = [sb(f"qd_lo{u}", [D, HQ], F32R) for u in range(2)]
        chunk_max = sb("chunk_max", [D, 2, RT, NKC])
        max_col = sb("max_col", [D, 2, RT])
        max_hi, max_lo = sb("max_hi", [RT, 2, D], F32R), sb("max_lo", [RT, 2, D], F32R)
        shift = [sb(f"shift{u}", [2, HQ], F32R) for u in range(2)]
        probs = [sb(f"probs{u}", [KP, HQ]) for u in range(2)]
        acc = sb("acc", [D, 4 * SQ])
        inv = sb("inv", [D, 4 * SQ])
        if masked:
            mask_i = sb("mask_i", [D, SK], I32)
            mask_n = [sb(f"mask_n{u}", [KP, KT], I32) for u in range(2)]
            neg_row, valid_row = sb("neg_row", [D, SK]), sb("valid_row", [D, SK])
            neg_col = sb("neg_col", [KP, 2, KT])
            carrier = sb("carrier", [1, RT * NKC])

        prep_loaded, zeroed, cut, prep = sem("prep_loaded"), sem("zeroed"), sem("cut"), sem("prep")
        with nc.Block() as block:
            @block.gpsimd
            def _(pool):
                nc.gpsimd.memset(wo_quad[:, :, :], 0.0).then_inc(zeroed, 1)
                nc.gpsimd.memset(bv_quad[:, :], 0.0).then_inc(zeroed, 1)
                nc.gpsimd.memset(bias[:, :], 0.0).then_inc(zeroed, 1)
                nc.gpsimd.memset(acc[:, :], 0.0).then_inc(zeroed, 1)
                for u in range(2):
                    nc.gpsimd.memset(v[u][:, :, :, DK:DK + 1], 1.0).then_inc(zeroed, 1)
                nc.gpsimd.memset(head_mask[:, :], 1.0).then_inc(zeroed, 1)
                pool.wait_ge(zeroed, 7)
                nc.gpsimd.affine_select(out=head_mask[:, :], in_=head_mask[:, :], compare_op=ALU.is_ge, fill=0.0,
                                        base=0, pattern=[[-DK, H16]], channel_multiplier=1).then_inc(cut, 1)
                pool.wait_ge(cut, 1)
                nc.gpsimd.affine_select(out=head_mask[:, :], in_=head_mask[:, :], compare_op=ALU.is_ge, fill=0.0,
                                        base=DK - 1, pattern=[[DK, H16]], channel_multiplier=-1).then_inc(cut, 1)

            @block.vector
            def _(dve):
                nc.vector.tensor_copy(ones_2[:, :], s.ones[0:2, :]).then_inc(prep, 1)
                nc.vector.tensor_copy(sum_rows[:, :, :], bcast(s.ident[:, DK:D:32], 32, 2)).then_inc(prep, 1)

            @block.sync
            def _(sp):
                sp.dma_start(wq[:, :], a[f"{layer}_WqT"]).then_inc(prep_loaded, 16)
                sp.dma_start(wk[:, :], a[f"{layer}_WkT"]).then_inc(prep_loaded, 16)
                sp.dma_start(wv[:, :], a[f"{layer}_WvT"]).then_inc(prep_loaded, 16)
                sp.wait_ge(zeroed, 7)
                n = 3
                for j in range(4):
                    sp.dma_start(wo_quad[32 * j:32 * j + DK, :, :],
                                 a[f"{layer}_WoT"][j])\
                        .then_inc(prep_loaded, 16)
                    n += 1
                    if biased:
                        sp.dma_start(bv_quad[32 * j:32 * j + DK, :],
                                     a[f"{layer}_bv"][j])\
                            .then_inc(prep_loaded, 16)
                        n += 1
                if biased:
                    for k, name in enumerate(("bq", "bk", "bo")):
                        sp.dma_start(bias[:, k:k + 1], a[f"{layer}_{name}"]).then_inc(prep_loaded, 16)
                        n += 1
                sp.wait_ge(prep_loaded, 16 * n)

        project(nc, s, [(q, wq[:, :], s.xn, bias[:, 0:1], float(DK) ** -0.5)])

        loaded = [sem("even_loaded"), sem("odd_loaded")]
        (q_split, qd_made, masks_made, k_hi_made, k_lo_made, scratch_dve, scratch_act, k_rows,
         max_made, max_turned, max_split, row_moved, scores_made, probs_made, probs_used, acc_taken, sums_made,
         inverted, normed, products) = (
            sem(n) for n in ("q_split", "qd_made", "masks_made", "k_hi_made", "k_lo_made", "scratch_dve", "scratch_act", "k_rows", "max_made", "max_turned", "max_split",
                             "row_moved", "scores_made", "probs_made", "probs_used", "acc_taken", "sums_made",
                             "inverted", "normed", "products"))
        NV = 3
        ROWS = RT * NKC
        ND = NKC + ROWS
        NL = 3 if masked else 1
        batches = ExitStack()
        block = batches.enter_context(nc.Block())

        @block.sync
        def _(sp):
            def fetch(b, u):
                wait(sp, products, b * (NKC + NV) - (NKC + NV))
                sp.dma_start(ctx_T[u][:, :, :], a["ctx_T"][bass.ds(b, 1)].rearrange("a d (t p) -> (a d) t p", t=KT))\
                    .then_inc(loaded[u], 16)
                if masked:
                    wait(sp, masks_made, b * 3)
                    sp.dma_start(mask_i[:, :], a["mask_T"][bass.ds(b, 1)].broadcast_to([D, SK]))\
                        .then_inc(loaded[u], 16)
                    sp.dma_start(mask_n[u][:, :], a["mask_N"][bass.ds(b, 1)].rearrange("a (p t) -> (a p) t", t=KT))\
                        .then_inc(loaded[u], 16)

            def move_rows(b, u):
                sp.wait_ge(max_split, b * 2 + 2)
                wait(sp, scores_made, b * KT - KT)
                for k, part in enumerate((max_hi, max_lo)):
                    sp.dma_start(shift[u][k:k + 1, :].bitcast(F32), part[:, u, :].bitcast(F32)).then_inc(row_moved, 16)

            fetch(0, 0)
            fetch(1, 1)
            move_rows(0, 0)
            fetch(2, 0)
            move_rows(1, 1)
            fetch(3, 1)
            move_rows(2, 0)
            with sp.Fori(1, B // 2 - 1) as j:
                fetch(j * 2 + 2, 0)
                move_rows(j * 2 + 1, 1)
                fetch(j * 2 + 3, 1)
                move_rows(j * 2 + 2, 0)
            move_rows(B - 1, 1)

        @block.gpsimd
        def _(pool):
            def prepare(b, u, i):
                pool.wait_ge(q_split, 4)
                wait(pool, scores_made, b * KT - KT)
                for part, dst in ((q, qd_hi[u]), (q_lo, qd_lo[u])):
                    nc.gpsimd.tensor_tensor(dst[:, :].rearrange("p (h q) -> p h q", h=H16),
                                            bcast(part[:, batch_of(b)], H16, 1), bcast(head_mask[:, :], SQ, 2),
                                            ALU.mult).then_inc(qd_made, 1)
                for k in range(NKC):
                    pool.wait_ge(k_hi_made, b * NKC + k + 1)
                    cols = slice(k * KC, (k + 1) * KC)
                    nc.gpsimd.tensor_tensor(k_lo[u][:, cols], k_full[:, cols], k_hi[u][:, cols].bitcast(F32),
                                            ALU.subtract).then_inc(k_lo_made, 1)

            def step(b, u, i):
                prepare(b + 1, *following(u, i))
            one_ahead(pool, prepare, step, nothing)

        @block.tensor
        def _(pe):
            def keys_product(b, u, i, k):
                if k == 0:
                    pe.wait_ge(loaded[u], i * (16 * NL) + 16 * NL)
                wait(pe, scratch_dve, b * ND + (1 if k == 2 else 0))
                nc.tensor.matmul(s.ps[:, 4 + k % 2, 0:KC], wk[:, :],
                                 ctx_T[u][:, :, :].rearrange("d t p -> d (t p)")[:, k * KC:(k + 1) * KC],
                                 start=True, stop=True).then_inc(products, 1)

            def values_product(b, u, i, g):
                if g < 2:
                    pe.wait_ge(scratch_dve, b * ND + 2 + g)
                else:
                    pe.wait_ge(scratch_act, b * NV + 1)
                for t in range(4):
                    mm = nc.tensor.matmul(s.ps[0:KP, 4 + (g + 1) % 2, t * D:(t + 1) * D], ctx_T[u][:, 4 * g + t, :],
                                          wv[:, :], start=True, stop=True, skip_group_check=True)
                mm.then_inc(products, 1)

            def score_rows(b, u, i, n):
                t, k = n // NKC, n % NKC
                if n == 0:
                    pe.wait_ge(qd_made, b * 2 + 2)
                if n < 2:
                    pe.wait_ge(scratch_act, b * NV + 2 + n)
                else:
                    pe.wait_ge(scratch_dve, b * ND + NKC + n - 1)
                if t == 0:
                    pe.wait_ge(k_hi_made, b * NKC + k + 1)
                nc.tensor.matmul(s.ps[:, 4 + n % 2, 0:KC], qd_hi[u][:, t * D:(t + 1) * D],
                                 k_hi[u][:, k * KC:(k + 1) * KC], start=True, stop=True).then_inc(k_rows, 1)

            slots = [[(keys_product, 0), (keys_product, 1)], [(keys_product, 2), (values_product, 0)],
                     [(values_product, 1), (values_product, 2)]]
            slots += [[(score_rows, n) for n in range(m, m + 3)] for m in range(0, ROWS, 3)]

            def turn(b, u):
                pe.wait_ge(max_made, b + 1)
                wait(pe, normed, b - 1)
                nc.tensor.transpose(s.ps[0:RT, 7, 0:D], max_col[:, u, :], s.ident[:, :]).then_inc(max_turned, 1)

            def values(b, u, t):
                pe.wait_ge(probs_made, b * KT + t + 1)
                if t == 0:
                    wait(pe, acc_taken, b * 4)
                for h in range(H16):
                    j, c = h % 4, h // 4
                    mm = nc.tensor.matmul(s.ps[32 * j:32 * j + DK + 1, 6, c * SQ:(c + 1) * SQ], v[u][:, t, h, :],
                                          probs[t % 2][:, h * SQ:(h + 1) * SQ], start=(t == 0 and c == 0),
                                          stop=(t == KT - 1), skip_group_check=True)
                mm.then_inc(probs_used, 1)

            def spread_sums(b, split):
                pe.wait_ge(acc_taken, b * 4 + 4)
                pe.wait_ge(max_split, split)
                nc.tensor.matmul(s.ps[:, 7, 256:256 + 4 * SQ], sum_rows[:, :, :].rearrange("p j i -> p (j i)"),
                                 acc[:, :], start=True, stop=True).then_inc(sums_made, 1)

            def step(b, u, i, last=False):
                pe.wait_ge(k_lo_made, b * NKC + NKC)
                for t in range(KT):
                    ahead = [] if last or t >= len(slots) else slots[t]
                    wait(pe, probs_made, b * KT + t - 1)
                    tile = slice(t * KP, (t + 1) * KP)
                    for w, m in ((k_hi[u], qd_hi[u]), (k_hi[u], qd_lo[u]), (k_lo[u], qd_hi[u])):
                        for h in range(2):
                            nc.tensor.matmul(s.ps[0:KP, 2 * (t % 2) + h, 0:HQ // 2], w[:, tile],
                                             m[:, h * (HQ // 2):(h + 1) * (HQ // 2)],
                                             start=(w is k_hi[u] and m is qd_hi[u]), stop=False)
                    if t == 0:
                        pe.wait_ge(row_moved, b * 32 + 32)
                    for h in range(2):
                        mm = nc.tensor.matmul(s.ps[0:KP, 2 * (t % 2) + h, 0:HQ // 2], ones_2[:, 0:KP],
                                              shift[u][:, h * (HQ // 2):(h + 1) * (HQ // 2)], start=False, stop=True)
                    mm.then_inc(scores_made, 1)
                    for product, n in ahead[:2]:
                        product(b + 1, *following(u, i), n)
                    if t:
                        values(b, u, t - 1)
                    for product, n in ahead[2:]:
                        product(b + 1, *following(u, i), n)
                    if t == 2 and not (isinstance(b, int) and b == 0):
                        spread_sums(b - 1, b * 2 + 2)
                    if t == KT - 2 and not last:
                        turn(b + 1, 1 - u)
                values(b, u, KT - 1)

            def first(b, u, i):
                for slot in slots:
                    for product, n in slot:
                        product(b, u, i, n)
                turn(b, u)

            def end(b, u, i):
                step(b, u, i, last=True)
                spread_sums(b, b * 2 + 2)
            one_ahead(pe, first, step, end)

        @block.scalar
        def _(act):
            def take_keys(b, u, k):
                act.wait_ge(scratch_dve, b * ND + k + 1)
                wait(act, scores_made, b * KT - KT)
                cols = slice(k * KC, (k + 1) * KC)
                nc.scalar.activation(k_hi[u][:, cols], k_full[:, cols], ACT.Copy).then_inc(k_hi_made, 1)

            def take_values(b, u, g):
                if g == 0:
                    wait(act, probs_used, b * KT - KT)
                act.wait_ge(products, b * (NKC + NV) + NKC + g + 1)
                nc.scalar.activation(v[u][:, 4 * g:4 * g + 4, :, 0:DK],
                                     s.ps[0:KP, 4 + (g + 1) % 2, :].rearrange("p (t h d) -> p t h d", t=4, h=H16),
                                     ACT.Copy).then_inc(scratch_act, 1)

            slots = [[(take_keys, 0), (take_keys, 1)], [(take_keys, 2), (take_values, 0)],
                     [(take_values, 1), (take_values, 2)]]

            def first(b, u, i):
                for slot in slots:
                    for take, n in slot:
                        take(b, u, n)

            def step(b, u, i, last=False):
                for t in range(KT):
                    act.wait_ge(scores_made, b * KT + t + 1)
                    wait(act, probs_used, b * KT + t - 1)
                    if masked and t == 0:
                        act.wait_ge(masks_made, b * 3 + 3)
                    nc.scalar.activation(probs[t % 2][:, :].rearrange("p (h c) -> p h c", h=2),
                                         s.ps[0:KP, 2 * (t % 2):2 * (t % 2) + 2, 0:HQ // 2], ACT.Exp,
                                         bias=neg_col[:, u, t:t + 1] if masked else 0.0).then_inc(probs_made, 1)
                    for take, n in [] if last or t >= len(slots) else slots[t]:
                        take(b + 1, 1 - u, n)
                act.wait_ge(probs_used, b * KT + KT)
                wait(act, normed, b)
                for j in range(4):
                    rows = slice(32 * j, 32 * j + DK + 1)
                    nc.scalar.activation(acc[rows, :], s.ps[rows, 6, 0:4 * SQ], ACT.Copy).then_inc(acc_taken, 1)

            def end(b, u, i):
                step(b, u, i, last=True)
            one_ahead(act, first, step, end)

        @block.vector
        def _(dve):
            for h in range(2):
                half = slice(h * TOK // 2, (h + 1) * TOK // 2)
                nc.vector.tensor_copy(qd_hi[h][:, :], q[:, half]).then_inc(q_split, 1)
                dve.wait_ge(q_split, 2 * h + 1)
                nc.vector.tensor_tensor(q_lo[:, half], q[:, half], qd_hi[h][:, :].bitcast(F32), ALU.subtract)\
                    .then_inc(q_split, 1)

            def prepare(b, u, i, before=None):
                if masked:
                    dve.wait_ge(loaded[u], i * (16 * NL) + 16 * NL)
                    nc.vector.tensor_scalar(neg_row[:, :], mask_i[:, :], 0.0, MASKED, ALU.is_equal, ALU.mult)\
                        .then_inc(masks_made, 1)
                    nc.vector.tensor_scalar(valid_row[:, :], mask_i[:, :], 0.0, None, ALU.not_equal)\
                        .then_inc(masks_made, 1)
                    wait(dve, probs_made, b * KT - KT)
                    nc.vector.tensor_scalar(neg_col[:, u, :], mask_n[u][:, :], 0.0, MASKED, ALU.is_equal, ALU.mult)\
                        .then_inc(masks_made, 1)
                    dve.wait_ge(masks_made, b * 3 + 3)
                for k in range(NKC):
                    cols = slice(k * KC, (k + 1) * KC)
                    dve.wait_ge(products, b * (NKC + NV) + k + 1)
                    wait(dve, k_lo_made, b * NKC)
                    if masked:
                        nc.vector.scalar_tensor_tensor(k_full[:, cols], s.ps[:, 4 + k % 2, 0:KC], bias[:, 1:2],
                                                       valid_row[:, cols], ALU.add, ALU.mult).then_inc(scratch_dve, 1)
                    else:
                        nc.vector.tensor_scalar(k_full[:, cols], s.ps[:, 4 + k % 2, 0:KC], bias[:, 1:2], None, ALU.add)\
                            .then_inc(scratch_dve, 1)
                if before is not None:
                    norm(before)
                for n in range(ROWS):
                    t, k = n // NKC, n % NKC
                    dve.wait_ge(k_rows, b * ROWS + n + 1)
                    if masked:
                        nc.vector.memset(carrier[:, n:n + 1], 0.0)
                        nc.vector.tensor_tensor_reduce(s.ps[:, 4 + n % 2, 0:KC], s.ps[:, 4 + n % 2, 0:KC], neg_row[:, k * KC:(k + 1) * KC],
                                                       1.0, -3e38, ALU.add, ALU.max, chunk_max[:, u, t, k:k + 1])\
                            .then_inc(scratch_dve, 1)
                    else:
                        nc.vector.tensor_reduce(chunk_max[:, u, t, k:k + 1], s.ps[:, 4 + n % 2, 0:KC], AX.X, ALU.max)\
                            .then_inc(scratch_dve, 1)
                dve.wait_ge(scratch_dve, b * ND + ND)
                wait(dve, max_turned, b - 1)
                nc.vector.tensor_reduce(max_col[:, u, :], chunk_max[:, u, :, :], AX.X, ALU.max, negate=True)\
                    .then_inc(max_made, 1)

            def split(b, u):
                dve.wait_ge(max_turned, b + 1)
                wait(dve, row_moved, b * 32 - 32)
                nc.vector.tensor_copy(max_hi[:, u, :], s.ps[0:RT, 7, 0:D]).then_inc(max_split, 1)
                dve.wait_ge(max_split, b * 2 + 1)
                nc.vector.tensor_tensor(max_lo[:, u, :], s.ps[0:RT, 7, 0:D], max_hi[:, u, :].bitcast(F32), ALU.subtract)\
                    .then_inc(max_split, 1)

            def norm(b):
                dve.wait_ge(sums_made, b + 1)
                nc.vector.reciprocal(inv[:, :], s.ps[:, 7, 256:256 + 4 * SQ]).then_inc(inverted, 1)
                dve.wait_ge(inverted, b + 1)
                nc.vector.tensor_tensor(heads_out[:, :, batch_of(b)], acc[:, :].rearrange("p (c q) -> p c q", c=4),
                                        inv[:, :].rearrange("p (c q) -> p c q", c=4), ALU.mult).then_inc(normed, 1)

            def first(b, u, i):
                prepare(b, u, i)
                split(b, u)

            def step(b, u, i):
                prepare(b + 1, *following(u, i), before=None if isinstance(b, int) and b == 0 else b - 1)
                split(b + 1, 1 - u)

            def end(b, u, i):
                norm(b - 1)
                norm(b)
            one_ahead(dve, first, step, end)

        batches.close()
        output_projection(nc, s, layer, heads_out, wo_quad, bv_quad, bias[:, 2:3])

def output_projection(nc, s, name, heads_out, wo_quad, bv_quad, bias):
    with ExitStack() as ctx:
        biased, product_made, added = (ctx.enter_context(nc.semaphore(f"{name}_{n}"))
                                       for n in ("biased", "product_made", "added"))
        block = ctx.enter_context(nc.Block())

        @block.tensor
        def _(pe):
            for c in range(NCH):
                pe.wait_ge(biased, c + 1)
                for g in range(4):
                    mm = nc.tensor.matmul(s.ps[:, c, 0:CH], wo_quad[:, g, :], heads_out[:, g, c * CH:(c + 1) * CH],
                                          start=(g == 0), stop=(g == 3))
                mm.then_inc(product_made, 1)

        @block.gpsimd
        def _(pool):
            for c in range(NCH):
                cols = heads_out[:, :, c * CH:(c + 1) * CH]
                nc.gpsimd.tensor_tensor(cols, cols, bcast(bv_quad[:, :], CH, 2), ALU.add).then_inc(biased, 1)

        @block.vector
        def _(dve):
            for c in range(NCH):
                dve.wait_ge(product_made, c + 1)
                nc.vector.scalar_tensor_tensor(s.x_T[:, c * CH:(c + 1) * CH], s.ps[:, c, 0:CH], bias,
                                               s.x_T[:, c * CH:(c + 1) * CH], ALU.add, ALU.add).then_inc(added, 1)


def quantized(nc, s, a):
    with ExitStack() as ctx:
        def sb(name, shape, dt=F32):
            return ctx.enter_context(nc.sbuf_tensor(f"q2_{name}", shape, dt))

        def sem(name):
            return ctx.enter_context(nc.semaphore(f"q2_{name}"))

        w1, w2, b1, b2 = sb("w1", [D, HID]), sb("w2", [D, HT, D]), sb("b1", [D, HT]), sb("b2", [D, 1])
        quarter = sb("quarter", [D, 1])
        h, clamped, cell, y0, y1, hq = (sb(n, [D, HT, CH]) for n in ("h", "clamped", "cell", "y0", "y1", "hq"))
        out = sb("out", [D, CH])
        load(nc, s, [(w1[:, :], a["L2_w1"]), (w2[:, :, :].rearrange("p j o -> p (j o)"), a["L2_w2"]),
                           (b1[:, :], a["L2_b1"]), (b2[:, :], a["L2_b2"])])
        ready, hidden_made, scaled, step, cells, ends, sloped, out_made = (
            sem(n) for n in ("ready", "hidden_made", "scaled", "step", "cells", "ends", "sloped", "out_made"))
        start_at_one(nc, [scaled, step, out_made])
        STEPS = 12
        block = ctx.enter_context(nc.Block())

        @block.tensor
        def _(pe):
            with pe.Fori(0, NCH) as c:
                pe.wait_ge(scaled, 1 + c * HT)
                for j in range(HT):
                    nc.tensor.matmul(s.ps[:, j, 0:CH], w1[:, j * D:(j + 1) * D], s.xn[:, bass.ds(c * CH, CH)],
                                     start=True, stop=True).then_inc(hidden_made, 1)
                pe.wait_ge(step, 1 + c * STEPS + 9)
                for j in range(HT):
                    mm = nc.tensor.matmul(s.ps[:, 4, 0:CH], w2[:, j, :], hq[:, j, :], start=(j == 0), stop=(j == HT - 1))
                mm.then_inc(out_made, 1)

        @block.scalar
        def _(act):
            act.wait_ge(ready, 3)
            with act.Fori(0, NCH) as c:
                act.wait_ge(step, 1 + c * STEPS)
                for j in range(HT):
                    act.wait_ge(hidden_made, c * HT + j + 1)
                    nc.scalar.activation(h[:, j, :], s.ps[:, j, 0:CH], ACT.Identity, bias=b1[:, j:j + 1], scale=256.0)\
                        .then_inc(scaled, 1)
                act.wait_ge(step, 1 + c * STEPS + 4)
                nc.scalar.activation(y0[:, :, :], cell[:, :, :], ACT.Gelu, scale=0.25).then_inc(ends, 1)
                nc.scalar.activation(y1[:, :, :], cell[:, :, :], ACT.Gelu, bias=quarter[:, 0:1], scale=0.25)\
                    .then_inc(ends, 1)

        @block.gpsimd
        def _(pool):
            with pool.Fori(0, NCH) as c:
                pool.wait_ge(ends, c * 2 + 2)
                nc.gpsimd.tensor_tensor(y1[:, :, :], y1[:, :, :], y0[:, :, :], ALU.subtract).then_inc(sloped, 1)
                pool.wait_ge(sloped, c * 2 + 1)
                pool.wait_ge(step, 1 + c * STEPS + 5)
                nc.gpsimd.tensor_tensor(y1[:, :, :], y1[:, :, :], clamped[:, :, :], ALU.mult).then_inc(sloped, 1)

        @block.vector
        def _(dve):
            nc.vector.memset(quarter[:, :], 0.25).then_inc(ready, 1)
            nc.vector.tensor_scalar(b1[:, :], b1[:, :], 256.0, None, ALU.mult).then_inc(ready, 1)
            nc.vector.tensor_scalar(b2[:, :], b2[:, :], 256.0, None, ALU.mult).then_inc(ready, 1)
            with dve.Fori(0, NCH) as c:
                count = [0]

                def chain(ins):
                    count[0] += 1
                    ins.then_inc(step, 1)
                    dve.wait_ge(step, 1 + c * STEPS + count[0])

                dve.wait_ge(scaled, 1 + c * HT + HT)
                chain(nc.vector.tensor_scalar(h[:, :, :], h[:, :, :], MAGIC, MAGIC, ALU.add, ALU.subtract))
                chain(nc.vector.tensor_scalar(clamped[:, :, :], h[:, :, :], -1024.0, 1024.0, ALU.max, ALU.min))
                chain(nc.vector.tensor_scalar(cell[:, :, :], clamped[:, :, :], 1.0 / 64, -0.5 + 1.0 / 128,
                                              ALU.mult, ALU.add))
                chain(nc.vector.tensor_scalar(cell[:, :, :], cell[:, :, :], MAGIC, MAGIC, ALU.add, ALU.subtract))
                chain(nc.vector.scalar_tensor_tensor(clamped[:, :, :], cell[:, :, :], -64.0, clamped[:, :, :],
                                                     ALU.mult, ALU.add))
                chain(nc.vector.tensor_scalar(h[:, :, :], h[:, :, :], -1024.0, 0.0, ALU.add, ALU.max))
                dve.wait_ge(sloped, c * 2 + 2)
                chain(nc.vector.scalar_tensor_tensor(y0[:, :, :], y1[:, :, :], 1.0 / 64, y0[:, :, :], ALU.mult, ALU.add))
                chain(nc.vector.scalar_tensor_tensor(h[:, :, :], y0[:, :, :], 256.0, h[:, :, :], ALU.mult, ALU.add))
                dve.wait_ge(out_made, 1 + c)
                chain(nc.vector.tensor_scalar(hq[:, :, :], h[:, :, :], MAGIC, MAGIC, ALU.add, ALU.subtract))
                dve.wait_ge(out_made, 1 + c + 1)
                chain(nc.vector.tensor_scalar(out[:, :], s.ps[:, 4, 0:CH], b2[:, 0:1], None, ALU.add))
                chain(nc.vector.tensor_scalar(out[:, :], out[:, :], MAGIC, MAGIC, ALU.add, ALU.subtract))
                chain(nc.vector.scalar_tensor_tensor(s.x_T[:, bass.ds(c * CH, CH)], out[:, :], 1.0 / 256,
                                                     s.x_T[:, bass.ds(c * CH, CH)], ALU.mult, ALU.add))


def routed(nc, s, a):
    NE = 3
    with ExitStack() as ctx:
        def sb(name, shape, dt=F32):
            return ctx.enter_context(nc.sbuf_tensor(f"r3_{name}", shape, dt))

        def sem(name):
            return ctx.enter_context(nc.semaphore(f"r3_{name}"))

        w1, w2, b1, b2 = sb("w1", [D, NE, HID]), sb("w2", [D, NE * HT, D]), sb("b1", [D, NE * HT]), sb("b2", [D, NE])
        gate, gates = sb("gate", [D, 2]), sb("gates", [D, 2, D])
        bias = sb("bias", [D, 1])
        second = sb("second", [D, CH])
        routed_x = sb("routed_x", [D, 2, CH])
        hidden = sb("hidden", [D, 4, CH])
        load(nc, s, [(w1[:, 0:2, :], a["L3_w1"]), (w1[:, 2, :], a["L3_sw1"]),
                           (w2[:, 0:2 * HT, :], a["L3_w2"]), (w2[:, 2 * HT:, :], a["L3_sw2"]),
                           (b1[:, 0:2 * HT], a["L3_b1"]), (b1[:, 2 * HT:], a["L3_sb1"]),
                           (b2[:, 0:2], a["L3_b2"]), (b2[:, 2:3], a["L3_sb2"]), (gate[:, :], a["L3_gate_w"])])
        ready, gates_made, second_taken, route, hidden_made, hidden_taken, out_made, out_taken = (
            sem(n) for n in ("ready", "gates_made", "second_taken", "route", "hidden_made", "hidden_taken",
                             "out_made", "out_taken"))
        start_at_one(nc, [route, second_taken, out_taken, hidden_taken, out_made, hidden_made])
        NT = NE * HT
        block = ctx.enter_context(nc.Block())

        @block.tensor
        def _(pe):
            pe.wait_ge(ready, 2)
            with pe.Fori(0, NCH) as c:
                chunk = s.xn[:, bass.ds(c * CH, CH)]
                pe.wait_ge(route, 1 + c * 3)
                pe.wait_ge(second_taken, 1 + c)
                for g in range(2):
                    nc.tensor.matmul(s.ps[:, 5 + g, 0:CH], gates[:, g, :], chunk, start=True, stop=True)\
                        .then_inc(gates_made, 1)
                pe.wait_ge(out_taken, 1 + c)
                order = [2, 0, 1]
                for n in range(NT + 2):
                    if n < NT:
                        e, j = order[n // HT], n % HT
                        if n >= 4:
                            pe.wait_ge(hidden_taken, 1 + c * NT + n - 3)
                        else:
                            pe.wait_ge(hidden_taken, 1 + c * NT)
                        if e < 2 and j == 0:
                            pe.wait_ge(route, 1 + c * 3 + 2 + e)
                        nc.tensor.matmul(s.ps[:, n % 4, 0:CH], w1[:, e, j * D:(j + 1) * D],
                                         chunk if e == 2 else routed_x[:, e, :], start=True, stop=True)\
                            .then_inc(hidden_made, 1)
                    if n >= 2:
                        m = n - 2
                        pe.wait_ge(hidden_taken, 1 + c * NT + m + 1)
                        nc.tensor.matmul(s.ps[:, 4, 0:CH], w2[:, order[m // HT] * HT + m % HT, :], hidden[:, m % 4, :],
                                         start=(m == 0), stop=(m == NT - 1)).then_inc(out_made, 1)

        @block.scalar
        def _(act):
            with act.Fori(0, NCH) as c:
                act.wait_ge(gates_made, c * 2 + 2)
                act.wait_ge(route, 1 + c * 3)
                nc.scalar.activation(second[:, :], s.ps[:, 6, 0:CH], ACT.Copy).then_inc(second_taken, 1)
                for n in range(NT):
                    e, j = [2, 0, 1][n // HT], n % HT
                    act.wait_ge(hidden_made, 1 + c * NT + n + 1)
                    if n >= 4:
                        act.wait_ge(out_made, 1 + c * NT + n - 3)
                    else:
                        act.wait_ge(out_made, 1 + c * NT)
                    nc.scalar.activation(hidden[:, n % 4, :], s.ps[:, n % 4, 0:CH], ACT.Relu,
                                         bias=b1[:, e * HT + j:e * HT + j + 1]).then_inc(hidden_taken, 1)

        @block.vector
        def _(dve):
            nc.vector.tensor_copy(gates[:, :, :], bcast(gate[:, :], D, 2)).then_inc(ready, 1)
            nc.vector.tensor_reduce(bias[:, :], b2[:, :], AX.X, ALU.add).then_inc(ready, 1)
            dve.wait_ge(ready, 2)
            with dve.Fori(0, NCH) as c:
                chunk = s.xn[:, bass.ds(c * CH, CH)]
                dve.wait_ge(second_taken, 1 + c + 1)
                dve.wait_ge(hidden_made, 1 + c * NT)
                nc.vector.tensor_tensor(routed_x[:, 1, :], s.ps[:, 5, 0:CH], second[:, :], ALU.is_ge).then_inc(route, 1)
                dve.wait_ge(route, 1 + c * 3 + 1)
                nc.vector.tensor_tensor(routed_x[:, 0, :], routed_x[:, 1, :], chunk, ALU.mult).then_inc(route, 1)
                dve.wait_ge(route, 1 + c * 3 + 2)
                nc.vector.tensor_tensor(routed_x[:, 1, :], chunk, routed_x[:, 0, :], ALU.subtract).then_inc(route, 1)
                dve.wait_ge(out_made, 1 + c * NT + NT)
                nc.vector.scalar_tensor_tensor(s.x_T[:, bass.ds(c * CH, CH)], s.ps[:, 4, 0:CH], bias[:, 0:1],
                                               s.x_T[:, bass.ds(c * CH, CH)], ALU.add, ALU.add).then_inc(out_taken, 1)


def attention_latents(nc, s, a):
    with ExitStack() as ctx:
        def sb(name, shape, dt=F32):
            return ctx.enter_context(nc.sbuf_tensor(f"l3_{name}", shape, dt))

        def sem(name):
            return ctx.enter_context(nc.semaphore(f"l3_{name}"))

        NP = 4
        affine = sb("affine", [D, 6])
        latents = sb("latents", [D, TOK])
        q = sb("q", [D, NP, TOK])
        wq, wk, wkT, wv = sb("wq", [D, HID]), sb("wk", [D, HID]), sb("wkT", [D, NP, D]), sb("wv", [D, HID])
        wo = sb("wo", [D, NP, D])
        bx_rows = sb("bx_rows", [D, D])
        y = sb("y", [D, TOK])
        neg_rows = sb("neg_rows", [B, SK], F32R)
        rows_stored = sem("rows_stored")
        load(nc, s, [(affine[:, k:k + 1], a[f"L3_{n}"]) for k, n in
                           enumerate(("ln_x_w", "ln_x_b", "ln_l_w", "ln_l_b", "ln_o_w", "ln_o_b"))] +
             [(wq[:, :], a["L3_Wq"]), (wk[:, :], a["L3_Wk"]), (wkT[:, :, :], a["L3_WkT"]), (wv[:, :], a["L3_Wv"]),
              (wo[:, :, :], a["L3_Wo"]), (bx_rows[:, :], a["L3_bx_row"].broadcast_to([D, D]))])
        layer_norm(nc, s, "l3l", s.xn, latents, affine[:, 2:3], affine[:, 3:4])

        with ExitStack() as sub:
            def tmp(name, shape, dt=F32):
                return sub.enter_context(nc.sbuf_tensor(f"l3_{name}", shape, dt))

            masks = tmp("masks", [B, SK], mybir.dt.uint8)
            scales = tmp("scales", [D, 2])
            head_sel, head_selT = tmp("head_sel", [D, NP, H8]), tmp("head_selT", [H8, NP, D])
            squares = tmp("squares", [D, NP, CH])
            inv = tmp("q_inv", [H8, CH])
            load(nc, s, [(masks[:, :], a["mask_rows"]), (scales[0:DH, 0:1], a["L3_q_scale"]),
                                (scales[DH:D, 0:1], a["L3_q_scale"]), (scales[0:DH, 1:2], a["L3_k_scale"]),
                                (scales[DH:D, 1:2], a["L3_k_scale"])])
            made, step, q_made, squared, norms_made, std, spread_made = (
                sub.enter_context(nc.semaphore(f"l3q_{n}")) for n in
                ("made", "step", "q_made", "squared", "norms_made", "std", "spread_made"))
            with nc.Block() as block:
                @block.gpsimd
                def _(pool):
                    nc.gpsimd.memset(head_sel[:, :, :], 1.0).then_inc(made, 1)
                    nc.gpsimd.memset(head_selT[:, :, :], 1.0).then_inc(made, 1)
                    pool.wait_ge(made, 2)
                    nc.gpsimd.affine_select(out=head_sel[:, :, :], in_=head_sel[:, :, :], compare_op=ALU.is_ge, fill=0.0,
                                            base=0, pattern=[[D, NP], [-DH, H8]], channel_multiplier=1).then_inc(made, 1)
                    nc.gpsimd.affine_select(out=head_selT[:, :, :], in_=head_selT[:, :, :], compare_op=ALU.is_ge,
                                            fill=0.0, base=0, pattern=[[D, NP], [1, D]], channel_multiplier=-DH)\
                        .then_inc(made, 1)
                    pool.wait_ge(made, 4)
                    nc.gpsimd.affine_select(out=head_sel[:, :, :], in_=head_sel[:, :, :], compare_op=ALU.is_ge, fill=0.0,
                                            base=DH - 1, pattern=[[-D, NP], [DH, H8]], channel_multiplier=-1)\
                        .then_inc(made, 1)
                    nc.gpsimd.affine_select(out=head_selT[:, :, :], in_=head_selT[:, :, :], compare_op=ALU.is_ge,
                                            fill=0.0, base=DH - 1, pattern=[[-D, NP], [-1, D]],
                                            channel_multiplier=DH).then_inc(made, 1)

                @block.tensor
                def _(pe):
                    pe.wait_ge(made, 6)
                    for c in range(NCH):
                        if c:
                            pe.wait_ge(q_made, 4 * c)
                        for j in range(NP):
                            mm = nc.tensor.matmul(s.ps[:, j, 0:CH], wq[:, j * D:(j + 1) * D],
                                                  latents[:, c * CH:(c + 1) * CH], start=True, stop=True)
                        mm.then_inc(norms_made, 1)
                        pe.wait_ge(squared, c + 1)
                        for j in range(NP):
                            mm = nc.tensor.matmul(s.ps[0:H8, 4, 0:CH], head_sel[:, j, :], squares[:, j, :],
                                                  start=(j == 0), stop=(j == NP - 1))
                        mm.then_inc(norms_made, 1)
                        pe.wait_ge(step, 2 + 3 * c + 2)
                        for j in range(NP):
                            if j:
                                pe.wait_ge(q_made, 4 * c + j)
                            nc.tensor.matmul(s.ps[:, 5, 0:CH], head_selT[:, j, :], inv[:, :], start=True, stop=True)\
                                .then_inc(spread_made, 1)

                @block.scalar
                def _(act):
                    for c in range(NCH):
                        act.wait_ge(norms_made, 2 * c + 1)
                        nc.scalar.activation(squares[:, :, :], s.ps[:, 0:NP, 0:CH], ACT.Square).then_inc(squared, 1)
                        act.wait_ge(norms_made, 2 * c + 2)
                        if c:
                            act.wait_ge(spread_made, 4 * c)
                        nc.scalar.activation(inv[:, :], s.ps[0:H8, 4, 0:CH], ACT.Sqrt).then_inc(std, 1)

                @block.vector
                def _(dve):
                    nc.vector.tensor_scalar(neg_rows[:, :], masks[:, :], 0.0, NEVER, ALU.is_equal, ALU.mult)\
                        .then_inc(step, 1)
                    nc.vector.scalar_tensor_tensor(scales[:, 0:1], scales[:, 0:1], 8.0, scales[:, 1:2], ALU.mult,
                                                   ALU.mult).then_inc(step, 1)
                    for c in range(NCH):
                        dve.wait_ge(squared, c + 1)
                        dve.wait_ge(std, c + 1)
                        nc.vector.tensor_scalar(inv[:, :], inv[:, :], L2_EPS, None, ALU.max).then_inc(step, 1)
                        dve.wait_ge(step, 2 + 3 * c + 1)
                        nc.vector.reciprocal(inv[:, :], inv[:, :]).then_inc(step, 1)
                        nc.vector.tensor_scalar(q[:, :, c * CH:(c + 1) * CH], s.ps[:, 0:NP, 0:CH], scales[:, 0:1],
                                                None, ALU.mult).then_inc(step, 1)
                        dve.wait_ge(step, 2 + 3 * c + 3)
                        for j in range(NP):
                            dve.wait_ge(spread_made, 4 * c + j + 1)
                            cols = q[:, j, c * CH:(c + 1) * CH]
                            nc.vector.tensor_tensor(cols, cols, s.ps[:, 5, 0:CH], ALU.mult).then_inc(q_made, 1)

        with nc.Block() as block:
            @block.sync
            def _(sp):
                sp.dma_start(a["neg_scratch"].bitcast(F32), neg_rows[:, :].bitcast(F32)).then_inc(rows_stored, 16)
                sp.wait_ge(rows_stored, 16)

        ctx_N = [sb(f"ctx_N{u}", [KP, KT, D]) for u in range(2)]
        neg = [sb(f"neg{u}", [1, SK], F32R) for u in range(2)]
        stats, moments, rstd = sb("stats", [KP, KT, 6]), sb("moments", [KP, 3, KT]), sb("rstd", [KP, KT])
        xnT = sb("xnT", [D, SK + SQ])
        lat_N = sb("lat_N", [SQ, D])
        squares = sb("k_squares", [KP, 2, HID])
        norms = sb("norms", [KP, KT + 1, H8])
        inv_norms = sb("inv_norms", [KP, KT + 1, H8])
        q_blocks = sb("q_blocks", [D, NP, 2, SQ])
        G = sb("G", [D, HQ3])
        S = sb("S", [KP, KT + 1, HQ3])
        top = sb("top", [KP, HQ3])
        neg_max = sb("neg_max", [2 * SQ, NP])
        diag = sb("diag", [2 * SQ, NP, 2 * SQ])
        shift = sb("shift", [KP, HQ3])
        prob_sum = sb("prob_sum", [KP, HQ3])
        inv, mixed, mixed_b = sb("inv", [D, HQ3]), sb("mixed", [D, HQ3]), sb("mixed_b", [D, HQ3])
        heads = sb("heads", [D, NP, SQ])
        ones_row = sb("ones_row", [1, HQ3], F32R)
        loaded = [sem("even_loaded"), sem("odd_loaded")]
        (init, blocks_zeroed, lat_copied, qb_made, stats_made, mean_made, std_made, rstd_made, z_made, turned, xnT_made, lat_turned, lat_made,
         k_made, squared, reduced, root_made, inv_made, G_made, G_taken, raw_made, S_made, topped, top_turned,
         maxed, diag_made, spread_made, shift_made, shifted, exps_made, summed, mixed_made, sums_made, evac,
         heads_made, heads_taken, y_made, y_taken) = (
            sem(n) for n in (
                "init", "blocks_zeroed", "lat_copied", "qb_made", "stats_made", "mean_made", "std_made", "rstd_made", "z_made", "turned", "xnT_made",
                "lat_turned", "lat_made", "k_made", "squared", "reduced", "root_made", "inv_made", "G_made", "G_taken",
                "raw_made", "S_made", "topped", "top_turned", "maxed", "diag_made", "spread_made", "shift_made",
                "shifted", "exps_made", "summed", "mixed_made", "sums_made", "evac", "heads_made", "heads_taken",
                "y_made", "y_taken"))
        T = KT + 1
        NG = KT // 4

        def rows(t):
            return KP if t < KT else SQ

        batches = ExitStack()
        block = batches.enter_context(nc.Block())

        def staged(eng, first, step, last):
            first(0, 0, 0)
            step(0, 0, 0)
            with eng.Fori(0, B // 2 - 1) as j:
                step(j * 2 + 1, 1, j)
                step(j * 2 + 2, 0, j + 1)
            last(B - 1, 1, B // 2 - 1)

        @block.sync
        def _(sp):
            def fetch(b, u, i):
                wait(sp, loaded[u], i * 32)
                wait(sp, mixed_made, b - 1)
                sp.dma_start(ctx_N[u][:, :, :], a["ctx_N"][bass.ds(b, 1)].rearrange("a (p t) d -> (a p) t d", t=KT))\
                    .then_inc(loaded[u], 16)
                sp.dma_start(neg[u][:, :].bitcast(F32), a["neg_scratch"][bass.ds(b, 1)].bitcast(F32)).then_inc(loaded[u], 16)
            fetch(0, 0, 0)
            fetch(1, 1, 0)
            with sp.Fori(1, B // 2) as j:
                fetch(j * 2, 0, j)
                fetch(j * 2 + 1, 1, j)

        @block.gpsimd
        def _(pool):
            def prepare(b, u, i):
                wait(pool, raw_made, b * T)
                nc.gpsimd.tensor_copy(xnT[:, SK:], latents[:, batch_of(b)]).then_inc(lat_copied, 1)
                wait(pool, G_made, b)
                pool.wait_ge(lat_copied, b + 1)
                for half in range(2):
                    r = slice(half * DH, (half + 1) * DH)
                    nc.gpsimd.tensor_copy(q_blocks[r, :, half, :], q[r, :, batch_of(b)]).then_inc(qb_made, 1)
                    pool.wait_ge(qb_made, b * 2 + half + 1)

            def finish(b, u, i):
                pool.wait_ge(shift_made, b + 1)
                for t in range(T):
                    r = rows(t)
                    nc.gpsimd.tensor_tensor(S[0:r, t, :], S[0:r, t, :], shift[0:r, :], ALU.add).then_inc(shifted, 1)

            nc.gpsimd.memset(q_blocks[:, :, :, :], 0.0).then_inc(blocks_zeroed, 1)
            pool.wait_ge(blocks_zeroed, 1)

            def step(b, u, i):
                prepare(b + 1, 1 - u, i)
                finish(b, u, i)
            staged(pool, prepare, step, finish)

        @block.tensor
        def _(pe):
            def prepare(b, u, i):
                pe.wait_ge(z_made, b + 1)
                for g in range(NG):
                    if g < 2:
                        wait(pe, squared, b * T)
                    else:
                        pe.wait_ge(xnT_made, b * NG + 1)
                    for t in range(4):
                        mm = nc.tensor.transpose(s.ps[:, g % 2, t * KP:(t + 1) * KP], ctx_N[u][:, 4 * g + t, :],
                                                 s.ident[0:KP, 0:KP])
                    mm.then_inc(turned, 1)
                plain(pe, s)
                pe.wait_ge(lat_copied, b + 1)
                wait(pe, heads_taken, b - 1)
                nc.tensor.transpose(s.ps[0:SQ, 5, 0:D], xnT[:, SK:], s.ident[:, :]).then_inc(lat_turned, 1)
                pe.wait_ge(xnT_made, b * NG + NG)
                for t in range(T):
                    if t >= 2:
                        pe.wait_ge(squared, b * T + t - 1)
                    nc.tensor.matmul(s.ps[0:rows(t), t % 2, 0:HID], xnT[:, t * KP:t * KP + rows(t)], wk[:, :],
                                     start=True, stop=True).then_inc(k_made, 1)
                pe.wait_ge(qb_made, b * 2 + 2)
                wait(pe, maxed, b)
                for j in range(NP):
                    mm = nc.tensor.matmul(s.ps[:, 4, j * 2 * SQ:(j + 1) * 2 * SQ], wkT[:, j, :],
                                          q_blocks[:, j, :, :].rearrange("p h q -> p (h q)"), start=True, stop=True,
                                          skip_group_check=True)
                mm.then_inc(G_made, 1)

            def project_out(b, u, i):
                pe.wait_ge(evac, b * 4 + 4)
                if not isinstance(b, int) or b < B - 1:
                    pe.wait_ge(lat_made, b + 2)
                for h in range(H8):
                    r = slice((h % 2) * DH, (h % 2 + 1) * DH)
                    mm = nc.tensor.matmul(s.ps[r, 5, (h // 2) * SQ:(h // 2 + 1) * SQ], wv[:, h * DH:(h + 1) * DH],
                                          mixed[:, h * SQ:(h + 1) * SQ], start=(h < 2), stop=True,
                                          skip_group_check=True)
                mm.then_inc(heads_made, 1)
                pe.wait_ge(heads_taken, b + 1)
                for j in range(NP):
                    mm = nc.tensor.matmul(s.ps[:, 3, 0:SQ], wo[:, j, :], heads[:, j, :], start=(j == 0), stop=(j == NP - 1))
                mm.then_inc(y_made, 1)

            def finish(b, u, i):
                pe.wait_ge(topped, b * KT + KT)
                for j in range(NP):
                    mm = nc.tensor.transpose(s.ps[0:2 * SQ, 4, j * KP:(j + 1) * KP], top[:, j * 2 * SQ:(j + 1) * 2 * SQ],
                                             s.ident[0:KP, 0:KP])
                mm.then_inc(top_turned, 1)
                pe.wait_ge(diag_made, b + 1)
                nc.tensor.matmul(s.ps[0:KP, 5, 0:HQ3], s.ones[0:2 * SQ, 0:KP], diag[:, :, :].rearrange("p j q -> p (j q)"),
                                 start=True, stop=True).then_inc(spread_made, 1)
                for t in range(KT):
                    pe.wait_ge(exps_made, b * T + t + 1)
                    mm = nc.tensor.matmul(s.ps[:, 6, 0:HQ3], ctx_N[u][:, t, :], S[:, t, :], start=(t == 0), stop=(t == KT - 1))
                mm.then_inc(mixed_made, 1)
                pe.wait_ge(exps_made, b * T + T)
                nc.tensor.matmul(s.ps[:, 7, 0:HQ3], lat_N[:, :], S[0:SQ, KT, :], start=True, stop=False)
                nc.tensor.matmul(s.ps[:, 2, 0:HQ3], s.ones[0:SQ, :], S[0:SQ, KT, :], start=True, stop=False)
                pe.wait_ge(summed, b + 1)
                nc.tensor.matmul(s.ps[:, 7, 0:HQ3], bx_rows[0:KP, :], prob_sum[:, :], start=False, stop=True)
                nc.tensor.matmul(s.ps[:, 2, 0:HQ3], s.ones[0:KP, :], prob_sum[:, :], start=False, stop=True)\
                    .then_inc(sums_made, 1)

            def scores(b, u, i):
                pe.wait_ge(G_taken, b + 1)
                for t in range(T):
                    r = rows(t)
                    if t >= 2:
                        pe.wait_ge(S_made, b * T + t - 1)
                    elif t == 0:
                        wait(pe, evac, b * 4)
                    else:
                        wait(pe, y_taken, b)
                    mm = nc.tensor.matmul(s.ps[0:r, 2 + t % 2, 0:HQ3], xnT[:, t * KP:t * KP + r], G[:, :], start=True,
                                          stop=(t == KT))
                    if t < KT:
                        mm = nc.tensor.matmul(s.ps[0:r, 2 + t % 2, 0:HQ3], neg[u][0:1, t * KP:(t + 1) * KP],
                                              ones_row[:, :], start=False, stop=True)
                    mm.then_inc(raw_made, 1)

            def first(b, u, i):
                pe.wait_ge(loaded[0], 32)
                pe.wait_ge(init, 3)
                prepare(b, u, i)
                scores(b, u, i)

            def step(b, u, i):
                finish(b, u, i)
                prepare(b + 1, 1 - u, i)
                project_out(b, u, i)
                pe.wait_ge(loaded[1 - u], i * 32 + (32 if u == 0 else 64))
                scores(b + 1, 1 - u, i)

            def last(b, u, i):
                finish(b, u, i)
                project_out(b, u, i)
            staged(pe, first, step, last)

        @block.scalar
        def _(act):
            def std(b):
                act.wait_ge(stats_made, b * (KT + 4) + KT + 4)
                nc.scalar.activation(rstd[:, :], moments[:, 1, :], ACT.Sqrt, bias=s.eps[0:KP, 0:1], scale=1.0 / D).then_inc(std_made, 1)

            def prepare(b, u, i):
                wait(act, raw_made, b * T)
                for g in range(NG):
                    act.wait_ge(turned, b * NG + g + 1)
                    nc.scalar.activation(xnT[:, g * 4 * KP:(g + 1) * 4 * KP], s.ps[:, g % 2, 0:4 * KP], ACT.Identity,
                                         bias=affine[:, 1:2], scale=affine[:, 0:1]).then_inc(xnT_made, 1)
                act.wait_ge(lat_turned, b + 1)
                wait(act, sums_made, b)
                nc.scalar.activation(lat_N[:, :], s.ps[0:SQ, 5, 0:D], ACT.Copy).then_inc(lat_made, 1)
                for t in range(T):
                    act.wait_ge(k_made, b * T + t + 1)
                    wait(act, reduced, b * T + t - 1)
                    nc.scalar.activation(squares[0:rows(t), t % 2, :], s.ps[0:rows(t), t % 2, 0:HID], ACT.Square)\
                        .then_inc(squared, 1)
                act.wait_ge(G_made, b + 1)
                nc.scalar.activation(G[:, :], s.ps[:, 4, 0:HQ3], ACT.Copy).then_inc(G_taken, 1)
                act.wait_ge(reduced, b * T + T)
                nc.scalar.activation(inv_norms[:, :, :], norms[:, :, :], ACT.Sqrt).then_inc(root_made, 1)

            def take_heads(b, u, i):
                act.wait_ge(heads_made, b + 1)
                nc.scalar.activation(heads[:, :, :].rearrange("p j q -> p (j q)"), s.ps[:, 5, 0:NP * SQ], ACT.Copy)\
                    .then_inc(heads_taken, 1)

            def finish(b, u, i):
                act.wait_ge(spread_made, b + 1)
                nc.scalar.activation(shift[:, :], s.ps[0:KP, 5, 0:HQ3], ACT.Copy).then_inc(shift_made, 1)

            def exps(b, u, i):
                for t in range(T):
                    act.wait_ge(shifted, b * T + t + 1)
                    nc.scalar.activation(S[0:rows(t), t, :], S[0:rows(t), t, :], ACT.Exp).then_inc(exps_made, 1)

            def first(b, u, i):
                std(b)
                prepare(b, u, i)

            def step(b, u, i):
                finish(b, u, i)
                std(b + 1)
                exps(b, u, i)
                prepare(b + 1, 1 - u, i)
                take_heads(b, u, i)

            def last(b, u, i):
                finish(b, u, i)
                exps(b, u, i)
                take_heads(b, u, i)
            staged(act, first, step, last)

        @block.vector
        def _(dve):
            nc.vector.memset(norms[:, :, :], 1.0).then_inc(init, 1)
            nc.vector.tensor_copy(ones_row[:, :], s.ones[0:1, 0:1].broadcast_to([1, HQ3])).then_inc(init, 1)
            nc.vector.memset(top[:, :], 0.0).then_inc(init, 1)
            dve.wait_ge(init, 3)

            def normalize(b, u, count):
                dve.wait_ge(loaded[u], count)
                for t in range(KT):
                    nc.vector.bn_stats(stats[:, t, :], ctx_N[u][:, t, :]).then_inc(stats_made, 1)
                dve.wait_ge(stats_made, b * (KT + 4) + KT)
                nc.vector.tensor_tensor(moments[:, 0, :], stats[:, :, 1], stats[:, :, 4], ALU.add).then_inc(stats_made, 1)
                nc.vector.tensor_tensor(moments[:, 1, :], stats[:, :, 1], stats[:, :, 4], ALU.subtract).then_inc(stats_made, 1)
                nc.vector.tensor_tensor(moments[:, 2, :], stats[:, :, 2], stats[:, :, 5], ALU.add).then_inc(stats_made, 1)
                dve.wait_ge(stats_made, b * (KT + 4) + KT + 3)
                nc.vector.tensor_scalar(moments[:, 0, :], moments[:, 0, :], 0.5, None, ALU.mult).then_inc(mean_made, 1)
                nc.vector.tensor_tensor(moments[:, 1, :], moments[:, 1, :], moments[:, 1, :], ALU.mult).then_inc(mean_made, 1)
                dve.wait_ge(mean_made, b * 2 + 2)
                nc.vector.scalar_tensor_tensor(moments[:, 1, :], moments[:, 1, :], D / 4.0, moments[:, 2, :], ALU.mult,
                                               ALU.add).then_inc(stats_made, 1)
                dve.wait_ge(std_made, b + 1)
                nc.vector.reciprocal(rstd[:, :], rstd[:, :]).then_inc(rstd_made, 1)
                dve.wait_ge(rstd_made, b + 1)
                for t in range(KT):
                    ins = nc.vector.tensor_scalar(ctx_N[u][:, t, :], ctx_N[u][:, t, :], moments[:, 0, t:t + 1],
                                                  rstd[:, t:t + 1], ALU.subtract, ALU.mult)
                ins.then_inc(z_made, 1)

            def maxima(b, u, i):
                dve.wait_ge(top_turned, b + 1)
                nc.vector.tensor_reduce(neg_max[:, :], s.ps[0:2 * SQ, 4, 0:NP * KP].rearrange("p (j k) -> p j k", j=NP),
                                        AX.X, ALU.max, negate=True).then_inc(maxed, 1)
                dve.wait_ge(maxed, b + 1)
                nc.vector.tensor_tensor(diag[:, :, :], bcast(s.ident[0:2 * SQ, 0:2 * SQ], NP, 1),
                                        bcast(neg_max[:, :], 2 * SQ, 2), ALU.mult).then_inc(diag_made, 1)

            def finish(b, u, i):
                dve.wait_ge(exps_made, b * T + KT)
                nc.vector.tensor_reduce(prob_sum[:, :], S[:, 0:KT, :].rearrange("p t c -> p c t"), AX.X, ALU.add)\
                    .then_inc(summed, 1)
                dve.wait_ge(sums_made, b + 1)
                nc.vector.reciprocal(inv[:, :], s.ps[:, 2, 0:HQ3]).then_inc(evac, 1)
                dve.wait_ge(evac, b * 4 + 1)
                nc.vector.scalar_tensor_tensor(mixed[:, :], s.ps[:, 6, 0:HQ3], affine[:, 0:1], inv[:, :], ALU.mult,
                                               ALU.mult).then_inc(evac, 1)
                nc.vector.tensor_tensor(mixed_b[:, :], s.ps[:, 7, 0:HQ3], inv[:, :], ALU.mult).then_inc(evac, 1)
                dve.wait_ge(evac, b * 4 + 3)
                nc.vector.tensor_tensor(mixed[:, :], mixed[:, :], mixed_b[:, :], ALU.add).then_inc(evac, 1)

            def take_output(b, u, i):
                dve.wait_ge(y_made, b + 1)
                nc.vector.tensor_copy(y[:, batch_of(b)], s.ps[:, 3, 0:SQ]).then_inc(y_taken, 1)

            def first(b, u, i):
                normalize(b, u, 32)
                norms_part(b)
                scores_part(b)

            def step(b, u, i):
                maxima(b, u, i)
                normalize(b + 1, 1 - u, i * 32 + (32 if u == 0 else 64))
                finish(b, u, i)
                norms_part(b + 1)
                take_output(b, u, i)
                scores_part(b + 1)

            def norms_part(b):
                for t in range(T):
                    r = rows(t)
                    dve.wait_ge(squared, b * T + t + 1)
                    nc.vector.tensor_reduce(norms[0:r, t, :], squares[0:r, t % 2, :].rearrange("p (h d) -> p h d", h=H8),
                                            AX.X, ALU.add).then_inc(reduced, 1)
                dve.wait_ge(root_made, b + 1)
                nc.vector.tensor_scalar(inv_norms[:, :, :], inv_norms[:, :, :], L2_EPS, None, ALU.max).then_inc(inv_made, 1)
                dve.wait_ge(inv_made, b * 2 + 1)
                nc.vector.reciprocal(inv_norms[:, :, :], inv_norms[:, :, :]).then_inc(inv_made, 1)
                dve.wait_ge(inv_made, b * 2 + 2)

            def scores_part(b):
                for t in range(T):
                    r = rows(t)
                    dve.wait_ge(raw_made, b * T + t + 1)
                    nc.vector.tensor_tensor(S[0:r, t, :].rearrange("p (h q) -> p h q", h=H8),
                                            s.ps[0:r, 2 + t % 2, 0:HQ3].rearrange("p (h q) -> p h q", h=H8),
                                            bcast(inv_norms[0:r, t, :], SQ, 2), ALU.mult).then_inc(S_made, 1)
                    if t:
                        dve.wait_ge(S_made, b * T + t + 1)
                        if t > 1:
                            dve.wait_ge(topped, b * KT + t - 1)
                        nc.vector.tensor_tensor(top[0:r, :], S[0:r, 0, :] if t == 1 else top[0:r, :], S[0:r, t, :],
                                                ALU.max).then_inc(topped, 1)

            def last(b, u, i):
                maxima(b, u, i)
                finish(b, u, i)
                take_output(b, u, i)
            staged(dve, first, step, last)

        batches.close()
        layer_norm(nc, s, "l3o", y, s.xn, affine[:, 4:5], affine[:, 5:6], add_to=s.x_T)


def build(nc, a, out_T):
    with ExitStack() as ctx:
        def sb(name, shape, dt=F32):
            return ctx.enter_context(nc.sbuf_tensor(name, shape, dt))

        def sem(name):
            return ctx.enter_context(nc.semaphore(name))

        s = Shared()
        s.ps = ctx.enter_context(nc.psum_tensor("ps", [D, 8, 512], F32))
        s.x_T, s.xn, s.ident, s.ones = sb("x_T", [D, TOK]), sb("xn", [D, TOK]), sb("ident", [D, D]), sb("ones", [D, D])
        s.average, s.eps = sb("average", [D, D]), sb("eps", [D, 1])
        s.w1, s.w2 = sb("moe_w1", [D, E * HID]), sb("moe_w2", [D, E * HT * D])
        s.means_made, s.centred, s.squared, s.vars_made, s.std_made, s.inverted, s.scaled = (
            sem(n) for n in ("means_made", "centred", "squared", "vars_made", "std_made", "inverted", "scaled"))
        s.product_made, s.product_taken, s.loaded, s.x_loaded, s.zeroed, s.consts_made = (
            sem(n) for n in ("product_made", "product_taken", "loaded", "x_loaded", "zeroed", "consts_made"))
        moe_loaded = {"L0": sem("L0_moe_loaded"), "L1": sem("L1_moe_loaded")}
        stored = sem("stored")

        def norm(name):
            layer_norm(nc, s, name, s.x_T, s.xn)

        setup(nc, s, a)
        start_moe_loads(nc, s, a, "L0", moe_loaded["L0"])
        stages = [
            lambda: attention_one_head(nc, s, a),
            lambda: mixture(nc, s, a, "L0", moe_loaded["L0"], top2=False),
            lambda: (start_moe_loads(nc, s, a, "L1", moe_loaded["L1"]),
                     attention_16_heads(nc, s, a, "L1", masked=True, biased=True)),
            lambda: mixture(nc, s, a, "L1", moe_loaded["L1"], top2=True),
            lambda: attention_16_heads(nc, s, a, "L2", masked=False, biased=False),
            lambda: quantized(nc, s, a),
            lambda: attention_latents(nc, s, a),
            lambda: routed(nc, s, a),
        ]
        for n, stage in enumerate(stages):
            norm(f"norm{n}")
            stage()

        with nc.Block() as block:
            @block.sync
            def _(sp):
                sp.dma_start(out_T, s.x_T[:, :]).then_inc(stored, 16)
                sp.wait_ge(stored, 16)


def _layouts(i, np):
    def by_tile(m):
        m = m.reshape((B, KP, KT) + m.shape[2:])
        return np.ascontiguousarray(np.moveaxis(m, (2, 1), (-2, -1))).reshape((B,) + m.shape[3:] + (SK,))

    a = {"x_T": i["x"].reshape(TOK, D).T, "ctx_N": i["ctx_1024"], "ctx_T": by_tile(i["ctx_1024"]),
         "mask_T": by_tile(i["mask_BxS2_ik0"]), "mask_N": i["mask_BxS2_ik0"],
         "mask_rows": by_tile(i["mask_BxS2_bk0"]),
         "L0_WqT": i["L0_xattn_Wq"].T, "L0_Wk": i["L0_xattn_Wk"], "L0_bq": i["L0_xattn_bq"][:, None],
         "L0_bk": i["L0_xattn_bk"][:, None]}
    for n in ("Wq", "Wk", "Wv", "Wo"):
        a[f"L1_{n}T"] = i[f"L1_xattn_{n}"].T
        a[f"L2_{n}T"] = i[f"L2_xattn_w_{n[1]}"].T
        a[f"L1_b{n[1]}"] = i[f"L1_xattn_b{n[1]}"][:, None]
    for n in ("L1_WoT", "L2_WoT", "L1_bv"):
        a[n] = a[n].reshape(4, 4, DK, -1).transpose(1, 2, 0, 3)
    a["L1_bv"] = a["L1_bv"].reshape(4, DK, 4)
    a["L0_gate_w"] = i["L0_ffn_gate_w"].T
    a["L1_gate_w"] = i["L1_ffn_gate_w"]
    a["L0_w1"] = i["L0_ffn_w1"].transpose(2, 0, 1).reshape(D, E * HID)
    a["L0_w2"] = i["L0_ffn_w2"].reshape(E, D, HT, D).transpose(3, 0, 2, 1).reshape(D, E * HT * D)
    a["L1_w1"] = i["L1_ffn_w1"].transpose(1, 0, 2).reshape(D, E * HID)
    a["L1_w2"] = i["L1_ffn_w2"].reshape(E, HT, D, D).transpose(2, 0, 1, 3).reshape(D, E * HT * D)
    for n in ("L0", "L1"):
        a[f"{n}_gate_b"] = i[f"{n}_ffn_gate_b"][None, :]
        a[f"{n}_b1"] = i[f"{n}_ffn_b1"].reshape(E * HT, D).T
        a[f"{n}_b2"] = i[f"{n}_ffn_b2"]
    a["L2_w1"] = i["L2_ffn_w1"]
    a["L2_w2"] = i["L2_ffn_w2"].reshape(HT, D, D).transpose(1, 0, 2).reshape(D, HT * D)
    a["L2_b1"] = i["L2_ffn_b1"].reshape(HT, D).T
    a["L2_b2"] = i["L2_ffn_b2"][:, None]
    for n in ("ln_x_w", "ln_x_b", "ln_l_w", "ln_l_b", "ln_o_w", "ln_o_b", "q_scale", "k_scale"):
        a[f"L3_{n}"] = i[f"L3_xattn_{n}"][:, None]
    a["L3_bx_row"] = i["L3_xattn_ln_x_b"][None, :]
    a["L3_Wq"] = i["L3_xattn_Wq"]
    a["L3_Wk"] = i["L3_xattn_Wkv"][:, :HID]
    a["L3_Wv"] = i["L3_xattn_Wkv"][:, HID:]
    a["L3_WkT"] = i["L3_xattn_Wkv"][:, :HID].T.reshape(HT, D, D).transpose(1, 0, 2)
    a["L3_Wo"] = i["L3_xattn_Wo"].reshape(HT, D, D).transpose(1, 0, 2)
    a["L3_gate_w"] = i["L3_ffn_gate_w"].T
    a["L3_w1"] = i["L3_ffn_w1"].transpose(1, 0, 2)
    a["L3_sw1"] = i["L3_ffn_sw1"]
    a["L3_w2"] = i["L3_ffn_w2"].reshape(2 * HT, D, D).transpose(1, 0, 2)
    a["L3_sw2"] = i["L3_ffn_sw2"].reshape(HT, D, D).transpose(1, 0, 2)
    a["L3_b1"] = i["L3_ffn_b1"].reshape(2 * HT, D).T
    a["L3_sb1"] = i["L3_ffn_sb1"].reshape(HT, D).T
    a["L3_b2"] = i["L3_ffn_b2"].T
    a["L3_sb2"] = i["L3_ffn_sb2"][:, None]
    return {k: np.ascontiguousarray(v) for k, v in a.items()}


def kernel(**inputs):
    import numpy as np
    import concourse.bacc as bacc
    from concourse.bass_utils import run_bass_kernel_spmd

    arrays = _layouts({k: np.asarray(v) for k, v in inputs.items()}, np)
    nc = bacc.Bacc("TRN2", target_bir_lowering=False, num_devices=1)
    a = {k: nc.dram_tensor(f"in_{k}", v.shape, mybir.dt.from_np(v.dtype), kind="ExternalInput").ap()
         for k, v in arrays.items()}
    a["neg_scratch"] = nc.dram_tensor("neg_scratch", [B, SK], F32R, kind="Internal").ap()
    out_T = nc.dram_tensor("out_T", [D, TOK], F32, kind="ExternalOutput").ap()
    build(nc, a, out_T)
    r = run_bass_kernel_spmd(nc, [{f"in_{k}": v for k, v in arrays.items()}], core_ids=[0])
    return np.ascontiguousarray(r.results[0]["out_T"].T).reshape(B, SQ, D)
```

```python
from contextlib import ExitStack

import concourse.bass as bass
from concourse import mybir

F32 = mybir.dt.float32
F32R = mybir.dt.float32r
I32 = mybir.dt.int32
ALU = mybir.AluOpType
ACT = mybir.ActivationFunctionType
AX = mybir.AxisListType

B, SQ, D = 32, 56, 128
SK = 1500
KT = 12
KP = SK // KT
TOK = B * SQ
NCH = 4
CH = TOK // NCH
NKC = 3
KC = SK // NKC
E, HID = 8, 512
HT = HID // D
TT = TOK // D
H16, DK = 16, 8
HQ = H16 * SQ
RT = HQ // D
H8, DH = 8, 64
HQ3 = H8 * SQ
LN_EPS, L2_EPS = 1e-5, 1e-12
MAGIC = 12582912.0
MASKED = -1e9
NEVER = -1e30


class Shared:
    norms = scaled_steps = products = loads = 0


def bcast(ap, n, at):
    shape = list(ap.shape)
    return ap.unsqueeze(at).broadcast_to(shape[:at] + [n] + shape[at:])


def one_ahead(eng, first, step, last):
    first(0, 0, 0)
    step(0, 0, 0)
    step(1, 1, 0)
    with eng.Fori(1, B // 2 - 1) as j:
        step(j * 2, 0, j)
        step(j * 2 + 1, 1, j)
    step(B - 2, 0, B // 2 - 1)
    last(B - 1, 1, B // 2 - 1)


def following(u, i):
    return (1 - u, i) if u == 0 else (0, i + 1)


def nothing(b, u, i):
    pass


def wait(eng, sem, value):
    if not isinstance(value, int) or value > 0:
        eng.wait_ge(sem, value)


def plain(eng, s):
    eng.wait_ge(s.x_loaded, 16)


def start_at_one(nc, sems):
    with nc.Block() as block:
        @block.sync
        def _(sp):
            for sem in sems:
                sp.sem_inc(sem, 1)


def clear(nc, sems):
    with nc.Block() as block:
        @block.gpsimd
        def _(pool):
            for sem in sems:
                pool.sem_clear(sem)


def batch_of(b):
    return bass.ds(b * SQ, SQ)


def setup(nc, s, a):
    zeroed, consts_made = s.zeroed, s.consts_made
    with nc.Block() as block:
        @block.sync
        def _(sp):
            sp.dma_start(s.x_T[:, :], a["x_T"]).then_inc(s.x_loaded, 16)
            sp.wait_ge(s.x_loaded, 16)

        @block.gpsimd
        def _(pool):
            nc.gpsimd.memset(s.ident[:, :], 0.0).then_inc(zeroed, 1)
            pool.wait_ge(zeroed, 1)
            nc.gpsimd.affine_select(out=s.ident[:, :], in_=s.ident[:, :], compare_op=ALU.not_equal, fill=1.0,
                                    base=0, pattern=[[-1, D]], channel_multiplier=1).then_inc(consts_made, 1)

        @block.vector
        def _(dve):
            nc.vector.memset(s.ones[:, :], 1.0).then_inc(consts_made, 1)
            nc.vector.memset(s.average[:, :], 1.0 / D).then_inc(consts_made, 1)
            nc.vector.memset(s.eps[:, :], LN_EPS).then_inc(consts_made, 1)


def layer_norm(nc, s, name, src, dst, weight=None, bias=None, add_to=None):
    n0, scaled0 = s.norms * NCH, s.scaled_steps
    steps = 1 + (weight is not None) + (add_to is not None)
    s.norms += 1
    s.scaled_steps += steps * NCH
    with ExitStack() as ctx:
        squares = ctx.enter_context(nc.sbuf_tensor(f"{name}_squares", [D, NCH, CH], F32))
        std = ctx.enter_context(nc.sbuf_tensor(f"{name}_std", [D, NCH, CH], F32))
        block = ctx.enter_context(nc.Block())

        def cols(t, c):
            return t[:, c * CH:(c + 1) * CH]

        @block.tensor
        def _(pe):
            for c in range(NCH):
                nc.tensor.matmul(s.ps[:, c, 0:CH], s.average[:, :], cols(src, c), start=True, stop=True)\
                    .then_inc(s.means_made, 1)
            for c in range(NCH):
                pe.wait_ge(s.squared, n0 + c + 1)
                nc.tensor.matmul(s.ps[:, NCH + c, 0:CH], s.average[:, :], squares[:, c, :], start=True, stop=True)\
                    .then_inc(s.vars_made, 1)

        @block.gpsimd
        def _(pool):
            for c in range(NCH):
                pool.wait_ge(s.centred, n0 + c + 1)
                nc.gpsimd.tensor_tensor(squares[:, c, :], cols(dst, c), cols(dst, c), ALU.mult).then_inc(s.squared, 1)

        @block.scalar
        def _(act):
            for c in range(NCH):
                act.wait_ge(s.vars_made, n0 + c + 1)
                nc.scalar.activation(std[:, c, :], s.ps[:, NCH + c, 0:CH], ACT.Sqrt, bias=s.eps[:, 0:1])\
                    .then_inc(s.std_made, 1)

        @block.vector
        def _(dve):
            for c in range(NCH):
                dve.wait_ge(s.means_made, n0 + c + 1)
                nc.vector.tensor_tensor(cols(dst, c), cols(src, c), s.ps[:, c, 0:CH], ALU.subtract)\
                    .then_inc(s.centred, 1)
            for c in range(NCH):
                dve.wait_ge(s.std_made, n0 + c + 1)
                nc.vector.reciprocal(std[:, c, :], std[:, c, :]).then_inc(s.inverted, 1)
                dve.wait_ge(s.inverted, n0 + c + 1)
                dve.wait_ge(s.squared, n0 + c + 1)
                nc.vector.tensor_tensor(cols(dst, c), cols(dst, c), std[:, c, :], ALU.mult).then_inc(s.scaled, 1)
                if weight is not None:
                    dve.wait_ge(s.scaled, scaled0 + c * steps + 1)
                    nc.vector.tensor_scalar(cols(dst, c), cols(dst, c), weight, bias, ALU.mult, ALU.add)\
                        .then_inc(s.scaled, 1)
                if add_to is not None:
                    dve.wait_ge(s.scaled, scaled0 + c * steps + 2)
                    nc.vector.tensor_tensor(cols(add_to, c), cols(add_to, c), cols(dst, c), ALU.add)\
                        .then_inc(s.scaled, 1)


def project(nc, s, pairs):
    n0 = s.products
    s.products += len(pairs) * NCH
    with nc.Block() as block:
        @block.tensor
        def _(pe):
            n = 0
            for i, (dst, w, src, bias, scale) in enumerate(pairs):
                if i:
                    pe.wait_ge(s.product_taken, n0 + n)
                for c in range(NCH):
                    nc.tensor.matmul(s.ps[0:w.shape[1], n % 8, 0:CH], w, src[:, c * CH:(c + 1) * CH],
                                     start=True, stop=True).then_inc(s.product_made, 1)
                    n += 1

        @block.vector
        def _(dve):
            n = 0
            for dst, w, src, bias, scale in pairs:
                for c in range(NCH):
                    dve.wait_ge(s.product_made, n0 + n + 1)
                    nc.vector.tensor_scalar(dst[:, c * CH:(c + 1) * CH], s.ps[0:w.shape[1], n % 8, 0:CH],
                                            0.0 if bias is None else bias, scale, ALU.add, ALU.mult)\
                        .then_inc(s.product_taken, 1)
                    n += 1


def load(nc, s, pairs):
    s.loads += len(pairs)
    with nc.Block() as block:
        @block.sync
        def _(sp):
            for dst, src in pairs:
                sp.dma_start(dst, src).then_inc(s.loaded, 16)
            sp.wait_ge(s.loaded, 16 * s.loads)


def start_moe_loads(nc, s, a, layer, moe_loaded):
    with nc.Block() as block:
        @block.sync
        def _(sp):
            sp.dma_start(s.w1[:, :], a[f"{layer}_w1"]).then_inc(moe_loaded, 16)
            sp.dma_start(s.w2[:, :], a[f"{layer}_w2"]).then_inc(moe_loaded, 16)


def attention_one_head(nc, s, a):
    with ExitStack() as ctx:
        def sb(name, shape, dt=F32):
            return ctx.enter_context(nc.sbuf_tensor(f"a0_{name}", shape, dt))

        sems = []

        def sem(name):
            sems.append(ctx.enter_context(nc.semaphore(f"a0_{name}")))
            return sems[-1]

        wq, wk, bias = sb("wq", [D, D]), sb("wk", [D, D]), sb("bias", [D, 2])
        q, qk, qbk = sb("q", [D, TOK]), sb("qk", [D, TOK]), sb("qbk", [1, TOK])
        q_b = [sb(f"q_b{u}", [D, SQ]) for u in range(2)]
        q_r = [sb(f"q_r{u}", [D, SQ], F32R) for u in range(2)]
        ctx_N = [sb(f"ctx_N{u}", [KP, KT, D]) for u in range(2)]
        ctx_T = [sb(f"ctx_T{u}", [D, KT, KP]) for u in range(2)]
        ctx_R = [sb(f"ctx_R{u}", [D, SK], F32R) for u in range(2)]
        max_col = sb("max_col", [SQ, 2])
        shift = sb("shift", [1, 2, SQ])
        probs = [sb(f"probs{u}", [KP, KT, SQ]) for u in range(2)]
        prob_sum = sb("prob_sum", [KP, 2, SQ])
        raised = sb("raised", [1, SQ])
        inv, delta = sb("inv", [D, SQ]), sb("delta", [D, SQ])

        load(nc, s, [(wq[:, :], a["L0_WqT"]), (wk[:, :], a["L0_Wk"]), (bias[:, 0:1], a["L0_bq"]),
                           (bias[:, 1:2], a["L0_bk"])])
        project(nc, s, [(q, wq[:, :], s.xn, bias[:, 0:1], 1.0 / 32), (qk, wk[:, :], q, None, 1.0),
                               (qbk, bias[:, 1:2], q, None, 1.0)])

        T_loaded = [sem("even_T_loaded"), sem("odd_T_loaded")]
        N_loaded = [sem("even_N_loaded"), sem("odd_N_loaded")]
        q_taken, rounded, rows_made, max_made, max_turned, shift_made = (
            sem(n) for n in ("q_taken", "rounded", "rows_made", "max_made", "max_turned", "shift_made"))
        scores_made, probs_made, summed, out_made, max_raised, inverted, scaled, added = (
            sem(n) for n in ("scores_made", "probs_made", "summed", "out_made", "max_raised", "inverted", "scaled", "added"))
        HALF = KT // 2
        batches = ExitStack()
        block = batches.enter_context(nc.Block())

        @block.sync
        def _(sp):
            def fetch(b, u):
                wait(sp, scores_made, b - 1)
                sp.dma_start(ctx_T[u][:, :, :], a["ctx_T"][bass.ds(b, 1)].rearrange("a d (t p) -> (a d) t p", t=KT))\
                    .then_inc(T_loaded[u], 16)
                wait(sp, out_made, b - 1)
                sp.dma_start(ctx_N[u][:, :, :], a["ctx_N"][bass.ds(b, 1)].rearrange("a (p t) d -> (a p) t d", t=KT))\
                    .then_inc(N_loaded[u], 16)
            fetch(0, 0)
            fetch(1, 1)
            with sp.Fori(1, B // 2) as j:
                fetch(j * 2, 0)
                fetch(j * 2 + 1, 1)

        @block.gpsimd
        def _(pool):
            def take_queries(b, u, i):
                wait(pool, scores_made, b - 1)
                nc.gpsimd.tensor_copy(q_b[u][:, :], qk[:, batch_of(b)]).then_inc(q_taken, 1)
                nc.gpsimd.tensor_copy(q_r[u][:, :], qk[:, batch_of(b)]).then_inc(q_taken, 1)

            def step(b, u, i):
                take_queries(b + 1, *following(u, i))
            one_ahead(pool, take_queries, step, nothing)

        @block.tensor
        def _(pe):
            def score_rows(b, u):
                pe.wait_ge(rounded, b + 1)
                pe.wait_ge(q_taken, b * 2 + 2)
                wait(pe, shift_made, b)
                for k in range(NKC):
                    mm = nc.tensor.matmul(s.ps[0:SQ, k, 0:KC], q_r[u][:, :], ctx_R[u][:, k * KC:(k + 1) * KC],
                                          start=True, stop=True)
                mm.then_inc(rows_made, 1)

            def turn_maxima(b, u):
                plain(pe, s)
                pe.wait_ge(max_made, b + 1)
                pe.wait_ge(rows_made, b + 1)
                nc.tensor.transpose(s.ps[0:1, 0, 0:SQ], max_col[:, u:u + 1], s.ident[0:SQ, 0:SQ])\
                    .then_inc(max_turned, 1)

            def scores(b, u):
                wait(pe, probs_made, b - 1)
                for h in range(2):
                    for t in range(HALF):
                        nc.tensor.matmul(s.ps[0:KP, 3 + 2 * u + h, t * SQ:(t + 1) * SQ], ctx_T[u][:, h * HALF + t, :],
                                         q_b[u][:, :], start=(t == 0), stop=False, skip_group_check=True)
                pe.wait_ge(shift_made, b + 1)
                for h in range(2):
                    mm = nc.tensor.matmul(s.ps[0:KP, 3 + 2 * u + h, 0:HALF * SQ], s.ones[0:1, 0:KP],
                                          bcast(shift[:, u, :], HALF, 1), start=False, stop=True,
                                          skip_group_check=True)
                mm.then_inc(scores_made, 1)

            def outputs(b, u, i):
                pe.wait_ge(N_loaded[u], i * 16 + 16)
                pe.wait_ge(probs_made, b + 1)
                wait(pe, scaled, b)
                for t in range(KT):
                    nc.tensor.matmul(s.ps[:, 7, 64:64 + SQ], ctx_N[u][:, t, :], probs[u][:, t, :],
                                     start=(t == 0), stop=False, skip_group_check=True)
                pe.wait_ge(summed, b + 1)
                nc.tensor.matmul(s.ps[:, 7, 128:128 + SQ], s.ones[0:KP, :], prob_sum[:, u, :],
                                 start=False, stop=True, skip_group_check=True).then_inc(out_made, 1)

            def first(b, u, i):
                score_rows(b, u)
                turn_maxima(b, u)

            def step(b, u, i):
                scores(b, u)
                score_rows(b + 1, 1 - u)
                if not (isinstance(b, int) and b == 0):
                    outputs(b - 1, 1 - u, i - 1 if u == 0 else i)
                turn_maxima(b + 1, 1 - u)

            def last(b, u, i):
                scores(b, u)
                outputs(b - 1, 1 - u, i)
                outputs(b, u, i)
            one_ahead(pe, first, step, last)

        @block.scalar
        def _(act):
            def exps(b, u, i):
                act.wait_ge(scores_made, b + 1)
                wait(act, out_made, b - 1)
                wait(act, summed, b - 1)
                nc.scalar.activation(probs[u][:, :, :].rearrange("p (h t) q -> p h (t q)", h=2),
                                     s.ps[0:KP, 3 + 2 * u:5 + 2 * u, 0:HALF * SQ], ACT.Exp).then_inc(probs_made, 1)
            one_ahead(act, nothing, exps, exps)

        @block.vector
        def _(dve):
            def round_keys(b, u, i):
                dve.wait_ge(T_loaded[u], i * 16 + 16)
                wait(dve, rows_made, b - 1)
                nc.vector.tensor_copy(ctx_R[u][:, :].rearrange("d (t p) -> d t p", t=KT), ctx_T[u][:, :, :])\
                    .then_inc(rounded, 1)

            def maxima(b, u):
                dve.wait_ge(rows_made, b + 1)
                wait(dve, max_turned, b - 1)
                nc.vector.tensor_reduce(max_col[:, u:u + 1], s.ps[0:SQ, 0:NKC, 0:KC], AX.XY, ALU.max)\
                    .then_inc(max_made, 1)

            def shifts(b, u):
                dve.wait_ge(max_turned, b + 1)
                wait(dve, scores_made, b - 1)
                nc.vector.tensor_tensor(raised[:, :], s.ps[0:1, 0, 0:SQ], qbk[0:1, batch_of(b)], ALU.add)\
                    .then_inc(max_raised, 1)
                dve.wait_ge(max_raised, b + 1)
                nc.vector.tensor_tensor(shift[:, u, :], qbk[0:1, batch_of(b)], raised[:, :], ALU.subtract)\
                    .then_inc(shift_made, 1)

            def sums(b, u):
                dve.wait_ge(probs_made, b + 1)
                wait(dve, out_made, b - 1)
                nc.vector.tensor_reduce(prob_sum[:, u, :], probs[u][:, :, :].rearrange("p t q -> p q t"), AX.X,
                                        ALU.add).then_inc(summed, 1)

            def outputs(b):
                dve.wait_ge(out_made, b + 1)
                nc.vector.reciprocal(inv[:, :], s.ps[:, 7, 128:128 + SQ]).then_inc(inverted, 1)
                dve.wait_ge(inverted, b + 1)
                wait(dve, added, b)
                nc.vector.tensor_tensor(delta[:, :], s.ps[:, 7, 64:64 + SQ], inv[:, :], ALU.mult).then_inc(scaled, 1)
                dve.wait_ge(scaled, b + 1)
                nc.vector.tensor_tensor(s.x_T[:, batch_of(b)], s.x_T[:, batch_of(b)], delta[:, :], ALU.add)\
                    .then_inc(added, 1)

            def first(b, u, i):
                round_keys(b, u, i)
                maxima(b, u)
                shifts(b, u)

            def step(b, u, i):
                later = not (isinstance(b, int) and b == 0)
                round_keys(b + 1, *following(u, i))
                if later:
                    sums(b - 1, 1 - u)
                maxima(b + 1, 1 - u)
                if later:
                    outputs(b - 1)
                shifts(b + 1, 1 - u)

            def last(b, u, i):
                sums(b - 1, 1 - u)
                outputs(b - 1)
                sums(b, u)
                outputs(b)
            one_ahead(dve, first, step, last)

        batches.close()
        clear(nc, sems)


def mixture(nc, s, a, layer, moe_loaded, top2):
    with ExitStack() as ctx:
        def sb(name, shape, dt=F32):
            return ctx.enter_context(nc.sbuf_tensor(f"{layer}f_{name}", shape, dt))

        sems = []

        def sem(name):
            sems.append(ctx.enter_context(nc.semaphore(f"{layer}f_{name}")))
            return sems[-1]

        gate_w, gate_b = sb("gate_w", [D, E]), sb("gate_b", [1, E])
        b1, neg_b1, b2 = sb("b1", [D, E, HT]), sb("neg_b1", [D, E, HT]), sb("b2", [E, D])
        b1_blocks = sb("b1_blocks", [D, E, HT, E])
        rank = sb("rank", [D, E])
        logits, best, eq, won, second, gates = (sb(n, [D, TT, E]) for n in
                                                ("logits", "best", "eq", "won", "second", "gates"))
        row_max, row_rank = sb("row_max", [D, TT]), sb("row_rank", [D, TT])
        weight_hi, weight_lo = sb("weight_hi", [E, TOK], F32R), sb("weight_lo", [E, TOK], F32R)
        weight_T = sb("weight_T", [E, TOK])
        pick = sb("pick", [E, E, D], F32R)
        expert_bias = sb("expert_bias", [E, D])
        spread = sb("spread", [D, 2, CH])
        hidden = sb("hidden", [D, 4, CH])

        load(nc, s, [(gate_w[:, :], a[f"{layer}_gate_w"]), (gate_b[:, :], a[f"{layer}_gate_b"]),
                                  (b1[:, :, :].rearrange("p e j -> p (e j)"), a[f"{layer}_b1"]),
                                  (b2[:, :], a[f"{layer}_b2"])])

        logits_made, gates_ready, step, exps_made, bias_made, rank_made = (
            sem(n) for n in ("logits_made", "gates_ready", "step", "exps_made", "bias_made", "rank_made"))
        with nc.Block() as block:
            @block.tensor
            def _(pe):
                for t in range(TT):
                    nc.tensor.matmul(s.ps[:, 7, t * E:(t + 1) * E], s.xn[:, t * D:(t + 1) * D], gate_w[:, :],
                                     start=(t == 0), stop=False, skip_group_check=True)
                    mm = nc.tensor.matmul(s.ps[:, 7, t * E:(t + 1) * E], s.ones[0:1, :], gate_b[:, :],
                                          start=False, stop=True, skip_group_check=True)
                mm.then_inc(logits_made, 1)
                pe.wait_ge(moe_loaded, 32)
                pe.wait_ge(bias_made, 2)
                for n in range(E * HT):
                    mm = nc.tensor.matmul(s.ps[0:E, 6, 0:D], b1_blocks[:, n // HT, n % HT, :],
                                          s.w2[:, n * D:(n + 1) * D], start=(n == 0), stop=(n == E * HT - 1))
                mm.then_inc(logits_made, 1)
                pe.wait_ge(gates_ready, 1)
                for t in range(TT):
                    mm = nc.tensor.transpose(s.ps[0:E, t // 4, (t % 4) * D:(t % 4 + 1) * D], gates[:, t, :], s.ident[:, :])
                mm.then_inc(logits_made, 1)

            @block.scalar
            def _(act):
                if top2:
                    act.wait_ge(exps_made, 1)
                    nc.scalar.activation(best[:, :, :], best[:, :, :], ACT.Exp).then_inc(exps_made, 1)

            @block.gpsimd
            def _(pool):
                nc.gpsimd.memset(b1_blocks[:, :, :, :], 0.0).then_inc(bias_made, 1)
                for e in range(E):
                    nc.gpsimd.memset(rank[:, e:e + 1], float(E - e)).then_inc(rank_made, 1)

            @block.vector
            def _(dve):
                count = [0]

                def chain(ins):
                    count[0] += 1
                    ins.then_inc(step, 1)
                    dve.wait_ge(step, count[0])

                dve.wait_ge(bias_made, 1)
                for e in range(E):
                    ins = nc.vector.tensor_copy(b1_blocks[:, e, :, e], b1[:, e, :])
                ins.then_inc(bias_made, 1)
                chain(nc.vector.tensor_scalar(neg_b1[:, :, :], b1[:, :, :], -1.0, None, ALU.mult))
                chain(nc.vector.tensor_copy(pick[:, :, :], bcast(s.ident[0:E, 0:E], D, 2)))
                dve.wait_ge(rank_made, E)
                dve.wait_ge(logits_made, 1)
                chain(nc.vector.tensor_copy(logits[:, :, :].rearrange("p t e -> p (t e)"), s.ps[:, 7, 0:TT * E]))

                def choose(values, chosen):
                    chain(nc.vector.tensor_reduce(row_max[:, :], values[:, :, :], AX.X, ALU.max))
                    chain(nc.vector.tensor_tensor(eq[:, :, :], values[:, :, :], bcast(row_max[:, :], E, 2), ALU.is_equal))
                    chain(nc.vector.tensor_tensor(eq[:, :, :], eq[:, :, :], bcast(rank[:, :], TT, 1), ALU.mult))
                    chain(nc.vector.tensor_reduce(row_rank[:, :], eq[:, :, :], AX.X, ALU.max))
                    chain(nc.vector.tensor_tensor(chosen[:, :, :], eq[:, :, :], bcast(row_rank[:, :], E, 2), ALU.is_equal))

                choose(logits, won)
                if top2:
                    nc.vector.tensor_tensor(best[:, :, :], logits[:, :, :], bcast(row_max[:, :], E, 2), ALU.subtract)\
                        .then_inc(exps_made, 1)
                    chain(nc.vector.scalar_tensor_tensor(logits[:, :, :], won[:, :, :], -1e38, logits[:, :, :],
                                                         ALU.mult, ALU.add))
                    dve.wait_ge(exps_made, 2)
                    choose(logits, second)
                    chain(nc.vector.tensor_tensor(won[:, :, :], won[:, :, :], second[:, :, :], ALU.add))
                    chain(nc.vector.tensor_tensor(won[:, :, :], won[:, :, :], best[:, :, :], ALU.mult))
                    chain(nc.vector.tensor_reduce(row_max[:, :], won[:, :, :], AX.X, ALU.add))
                    chain(nc.vector.reciprocal(row_max[:, :], row_max[:, :]))
                    chain(nc.vector.tensor_tensor(won[:, :, :], won[:, :, :], bcast(row_max[:, :], E, 2), ALU.mult))
                nc.vector.tensor_copy(gates[:, :, :], won[:, :, :]).then_inc(gates_ready, 1)
                dve.wait_ge(logits_made, 2)
                chain(nc.vector.tensor_tensor(expert_bias[:, :], s.ps[0:E, 6, 0:D], b2[:, :], ALU.add))
                dve.wait_ge(logits_made, 3)
                for k in range(4):
                    n = min(4, TT - 4 * k) * D
                    chain(nc.vector.tensor_copy(weight_T[:, 4 * k * D:4 * k * D + n], s.ps[0:E, k, 0:n]))
                chain(nc.vector.tensor_copy(weight_hi[:, :], weight_T[:, :]))
                chain(nc.vector.tensor_tensor(weight_lo[:, :], weight_T[:, :], weight_hi[:, :].bitcast(F32), ALU.subtract))

        hidden_made, hidden_taken, out_made, out_taken, spread_made, spread_taken = (
            sem(n) for n in ("hidden_made", "hidden_taken", "out_made", "out_taken", "spread_made", "spread_taken"))
        start_at_one(nc, [spread_taken, hidden_taken, out_taken, out_made])
        NT = E * HT
        with nc.Block() as block:
            @block.tensor
            def _(pe):
                with pe.Fori(0, NCH) as c:
                    def spread_weights(e):
                        mm = nc.tensor.matmul(s.ps[:, 5 + e % 2, 0:CH], pick[:, e, :], weight_hi[:, bass.ds(c * CH, CH)],
                                              start=True, stop=not top2)
                        if top2:
                            mm = nc.tensor.matmul(s.ps[:, 5 + e % 2, 0:CH], pick[:, e, :],
                                                  weight_lo[:, bass.ds(c * CH, CH)], start=False, stop=True)
                        mm.then_inc(spread_made, 1)

                    def first_product(n):
                        if n % HT == 0:
                            pe.wait_ge(spread_taken, 1 + c * E + max(n // HT - 1, 0))
                        if n >= 4:
                            pe.wait_ge(hidden_taken, 1 + c * NT + n - 3)
                        else:
                            pe.wait_ge(hidden_taken, 1 + c * NT)
                        nc.tensor.matmul(s.ps[:, n % 4, 0:CH], s.w1[:, n * D:(n + 1) * D],
                                         s.xn[:, bass.ds(c * CH, CH)], start=True, stop=True).then_inc(hidden_made, 1)

                    def second_product(n):
                        pe.wait_ge(hidden_taken, 1 + c * NT + n + 1)
                        mm = nc.tensor.matmul(s.ps[:, 4, 0:CH], s.w2[:, n * D:(n + 1) * D], hidden[:, n % 4, :],
                                              start=False, stop=(n == NT - 1))
                        mm.then_inc(out_made, 1)

                    pe.wait_ge(out_taken, 1 + c)
                    nc.tensor.matmul(s.ps[:, 4, 0:CH], expert_bias[:, :], weight_T[:, bass.ds(c * CH, CH)],
                                     start=True, stop=False)
                    for n in range(NT + 2):
                        if n < NT:
                            first_product(n)
                            if n % HT == 0:
                                spread_weights(n // HT)
                        if n >= 2:
                            second_product(n - 2)

            @block.scalar
            def _(act):
                with act.Fori(0, NCH) as c:
                    for e in range(E):
                        act.wait_ge(spread_made, c * E + e + 1)
                        if e >= 2:
                            act.wait_ge(hidden_taken, 1 + c * NT + (e - 1) * HT)
                        else:
                            act.wait_ge(hidden_taken, 1 + c * NT)
                        nc.scalar.activation(spread[:, e % 2, :], s.ps[:, 5 + e % 2, 0:CH], ACT.Copy)\
                            .then_inc(spread_taken, 1)

            @block.vector
            def _(dve):
                with dve.Fori(0, NCH) as c:
                    for n in range(NT):
                        e = n // HT
                        dve.wait_ge(hidden_made, c * NT + n + 1)
                        dve.wait_ge(spread_taken, 1 + c * E + e + 1)
                        if n >= 4:
                            dve.wait_ge(out_made, 1 + c * NT + n - 3)
                        else:
                            dve.wait_ge(out_made, 1 + c * NT)
                        nc.vector.scalar_tensor_tensor(hidden[:, n % 4, :], s.ps[:, n % 4, 0:CH],
                                                       neg_b1[:, e, n % HT:n % HT + 1], spread[:, e % 2, :],
                                                       ALU.max, ALU.mult).then_inc(hidden_taken, 1)
                    dve.wait_ge(out_made, 1 + c * NT + NT)
                    nc.vector.tensor_tensor(s.x_T[:, bass.ds(c * CH, CH)], s.x_T[:, bass.ds(c * CH, CH)],
                                            s.ps[:, 4, 0:CH], ALU.add).then_inc(out_taken, 1)

        clear(nc, sems)


def attention_16_heads(nc, s, a, layer, masked, biased):
    with ExitStack() as ctx:
        def sb(name, shape, dt=F32):
            return ctx.enter_context(nc.sbuf_tensor(f"{layer}a_{name}", shape, dt))

        def sem(name):
            return ctx.enter_context(nc.semaphore(f"{layer}a_{name}"))

        wq, wk, wv, wo = (sb(n, [D, D]) for n in ("wq", "wk", "wv", "wo_nat"))
        wo_quad = sb("wo_quad", [D, 4, D])
        bias = sb("bias", [D, 4])
        bv_quad = sb("bv_quad", [D, 4])
        head_mask = sb("head_mask", [D, H16])
        sum_rows = sb("sum_rows", [D, 4, 32])
        ones_2 = sb("ones_2", [2, D], F32R)
        q = sb("q", [D, TOK])
        q_lo = sb("q_lo", [D, TOK])
        heads_out = sb("heads_out", [D, 4, TOK])
        ctx_T = [sb(f"ctx_T{u}", [D, KT, KP]) for u in range(2)]
        k_full = sb("k_full", [D, SK])
        k_hi = [sb(f"k_hi{u}", [D, SK], F32R) for u in range(2)]
        k_lo = [sb(f"k_lo{u}", [D, SK], F32R) for u in range(2)]
        v = [sb(f"v{u}", [KP, KT, H16, DK + 1]) for u in range(2)]
        qd_hi = [sb(f"qd_hi{u}", [D, HQ], F32R) for u in range(2)]
        qd_lo = [sb(f"qd_lo{u}", [D, HQ], F32R) for u in range(2)]
        chunk_max = sb("chunk_max", [D, 2, RT, NKC])
        max_col = sb("max_col", [D, 2, RT])
        max_hi, max_lo = sb("max_hi", [RT, 2, D], F32R), sb("max_lo", [RT, 2, D], F32R)
        shift = [sb(f"shift{u}", [2, HQ], F32R) for u in range(2)]
        probs = [sb(f"probs{u}", [KP, HQ]) for u in range(2)]
        acc = sb("acc", [D, 4 * SQ])
        inv = sb("inv", [D, 4 * SQ])
        if masked:
            mask_i = sb("mask_i", [D, SK], I32)
            mask_n = [sb(f"mask_n{u}", [KP, KT], I32) for u in range(2)]
            neg_row, valid_row = sb("neg_row", [D, SK]), sb("valid_row", [D, SK])
            neg_col = sb("neg_col", [KP, 2, KT])
            carrier = sb("carrier", [1, RT * NKC])

        prep_loaded, zeroed, cut, prep = sem("prep_loaded"), sem("zeroed"), sem("cut"), sem("prep")
        with nc.Block() as block:
            @block.gpsimd
            def _(pool):
                nc.gpsimd.memset(wo_quad[:, :, :], 0.0).then_inc(zeroed, 1)
                nc.gpsimd.memset(bv_quad[:, :], 0.0).then_inc(zeroed, 1)
                nc.gpsimd.memset(bias[:, :], 0.0).then_inc(zeroed, 1)
                nc.gpsimd.memset(acc[:, :], 0.0).then_inc(zeroed, 1)
                for u in range(2):
                    nc.gpsimd.memset(v[u][:, :, :, DK:DK + 1], 1.0).then_inc(zeroed, 1)
                nc.gpsimd.memset(head_mask[:, :], 1.0).then_inc(zeroed, 1)
                pool.wait_ge(zeroed, 7)
                nc.gpsimd.affine_select(out=head_mask[:, :], in_=head_mask[:, :], compare_op=ALU.is_ge, fill=0.0,
                                        base=0, pattern=[[-DK, H16]], channel_multiplier=1).then_inc(cut, 1)
                pool.wait_ge(cut, 1)
                nc.gpsimd.affine_select(out=head_mask[:, :], in_=head_mask[:, :], compare_op=ALU.is_ge, fill=0.0,
                                        base=DK - 1, pattern=[[DK, H16]], channel_multiplier=-1).then_inc(cut, 1)

            @block.vector
            def _(dve):
                nc.vector.tensor_copy(ones_2[:, :], s.ones[0:2, :]).then_inc(prep, 1)
                nc.vector.tensor_copy(sum_rows[:, :, :], bcast(s.ident[:, DK:D:32], 32, 2)).then_inc(prep, 1)

            @block.sync
            def _(sp):
                sp.dma_start(wq[:, :], a[f"{layer}_WqT"]).then_inc(prep_loaded, 16)
                sp.dma_start(wk[:, :], a[f"{layer}_WkT"]).then_inc(prep_loaded, 16)
                sp.dma_start(wv[:, :], a[f"{layer}_WvT"]).then_inc(prep_loaded, 16)
                sp.wait_ge(zeroed, 7)
                n = 3
                for j in range(4):
                    sp.dma_start(wo_quad[32 * j:32 * j + DK, :, :],
                                 a[f"{layer}_WoT"][j])\
                        .then_inc(prep_loaded, 16)
                    n += 1
                    if biased:
                        sp.dma_start(bv_quad[32 * j:32 * j + DK, :],
                                     a[f"{layer}_bv"][j])\
                            .then_inc(prep_loaded, 16)
                        n += 1
                if biased:
                    for k, name in enumerate(("bq", "bk", "bo")):
                        sp.dma_start(bias[:, k:k + 1], a[f"{layer}_{name}"]).then_inc(prep_loaded, 16)
                        n += 1
                sp.wait_ge(prep_loaded, 16 * n)

        project(nc, s, [(q, wq[:, :], s.xn, bias[:, 0:1], float(DK) ** -0.5)])

        loaded = [sem("even_loaded"), sem("odd_loaded")]
        (q_split, qd_made, masks_made, k_hi_made, k_lo_made, scratch_dve, scratch_act, k_rows,
         max_made, max_turned, max_split, row_moved, scores_made, probs_made, probs_used, acc_taken, sums_made,
         inverted, normed, products) = (
            sem(n) for n in ("q_split", "qd_made", "masks_made", "k_hi_made", "k_lo_made", "scratch_dve", "scratch_act", "k_rows", "max_made", "max_turned", "max_split",
                             "row_moved", "scores_made", "probs_made", "probs_used", "acc_taken", "sums_made",
                             "inverted", "normed", "products"))
        NV = 3
        ROWS = RT * NKC
        ND = NKC + ROWS
        NL = 3 if masked else 1
        batches = ExitStack()
        block = batches.enter_context(nc.Block())

        @block.sync
        def _(sp):
            def fetch(b, u):
                wait(sp, products, b * (NKC + NV) - (NKC + NV))
                sp.dma_start(ctx_T[u][:, :, :], a["ctx_T"][bass.ds(b, 1)].rearrange("a d (t p) -> (a d) t p", t=KT))\
                    .then_inc(loaded[u], 16)
                if masked:
                    wait(sp, masks_made, b * 3)
                    sp.dma_start(mask_i[:, :], a["mask_T"][bass.ds(b, 1)].broadcast_to([D, SK]))\
                        .then_inc(loaded[u], 16)
                    sp.dma_start(mask_n[u][:, :], a["mask_N"][bass.ds(b, 1)].rearrange("a (p t) -> (a p) t", t=KT))\
                        .then_inc(loaded[u], 16)

            def move_rows(b, u):
                sp.wait_ge(max_split, b * 2 + 2)
                wait(sp, scores_made, b * KT - KT)
                for k, part in enumerate((max_hi, max_lo)):
                    sp.dma_start(shift[u][k:k + 1, :].bitcast(F32), part[:, u, :].bitcast(F32)).then_inc(row_moved, 16)

            fetch(0, 0)
            fetch(1, 1)
            move_rows(0, 0)
            fetch(2, 0)
            move_rows(1, 1)
            fetch(3, 1)
            move_rows(2, 0)
            with sp.Fori(1, B // 2 - 1) as j:
                fetch(j * 2 + 2, 0)
                move_rows(j * 2 + 1, 1)
                fetch(j * 2 + 3, 1)
                move_rows(j * 2 + 2, 0)
            move_rows(B - 1, 1)

        @block.gpsimd
        def _(pool):
            def prepare(b, u, i):
                pool.wait_ge(q_split, 4)
                wait(pool, scores_made, b * KT - KT)
                for part, dst in ((q, qd_hi[u]), (q_lo, qd_lo[u])):
                    nc.gpsimd.tensor_tensor(dst[:, :].rearrange("p (h q) -> p h q", h=H16),
                                            bcast(part[:, batch_of(b)], H16, 1), bcast(head_mask[:, :], SQ, 2),
                                            ALU.mult).then_inc(qd_made, 1)
                for k in range(NKC):
                    pool.wait_ge(k_hi_made, b * NKC + k + 1)
                    cols = slice(k * KC, (k + 1) * KC)
                    nc.gpsimd.tensor_tensor(k_lo[u][:, cols], k_full[:, cols], k_hi[u][:, cols].bitcast(F32),
                                            ALU.subtract).then_inc(k_lo_made, 1)

            def step(b, u, i):
                prepare(b + 1, *following(u, i))
            one_ahead(pool, prepare, step, nothing)

        @block.tensor
        def _(pe):
            def keys_product(b, u, i, k):
                if k == 0:
                    pe.wait_ge(loaded[u], i * (16 * NL) + 16 * NL)
                wait(pe, scratch_dve, b * ND + (1 if k == 2 else 0))
                nc.tensor.matmul(s.ps[:, 4 + k % 2, 0:KC], wk[:, :],
                                 ctx_T[u][:, :, :].rearrange("d t p -> d (t p)")[:, k * KC:(k + 1) * KC],
                                 start=True, stop=True).then_inc(products, 1)

            def values_product(b, u, i, g):
                if g < 2:
                    pe.wait_ge(scratch_dve, b * ND + 2 + g)
                else:
                    pe.wait_ge(scratch_act, b * NV + 1)
                for t in range(4):
                    mm = nc.tensor.matmul(s.ps[0:KP, 4 + (g + 1) % 2, t * D:(t + 1) * D], ctx_T[u][:, 4 * g + t, :],
                                          wv[:, :], start=True, stop=True, skip_group_check=True)
                mm.then_inc(products, 1)

            def score_rows(b, u, i, n):
                t, k = n // NKC, n % NKC
                if n == 0:
                    pe.wait_ge(qd_made, b * 2 + 2)
                if n < 2:
                    pe.wait_ge(scratch_act, b * NV + 2 + n)
                else:
                    pe.wait_ge(scratch_dve, b * ND + NKC + n - 1)
                if t == 0:
                    pe.wait_ge(k_hi_made, b * NKC + k + 1)
                nc.tensor.matmul(s.ps[:, 4 + n % 2, 0:KC], qd_hi[u][:, t * D:(t + 1) * D],
                                 k_hi[u][:, k * KC:(k + 1) * KC], start=True, stop=True).then_inc(k_rows, 1)

            slots = [[(keys_product, 0), (keys_product, 1)], [(keys_product, 2), (values_product, 0)],
                     [(values_product, 1), (values_product, 2)]]
            slots += [[(score_rows, n) for n in range(m, m + 3)] for m in range(0, ROWS, 3)]

            def turn(b, u):
                pe.wait_ge(max_made, b + 1)
                wait(pe, normed, b - 1)
                nc.tensor.transpose(s.ps[0:RT, 7, 0:D], max_col[:, u, :], s.ident[:, :]).then_inc(max_turned, 1)

            def values(b, u, t):
                pe.wait_ge(probs_made, b * KT + t + 1)
                if t == 0:
                    wait(pe, acc_taken, b * 4)
                for h in range(H16):
                    j, c = h % 4, h // 4
                    mm = nc.tensor.matmul(s.ps[32 * j:32 * j + DK + 1, 6, c * SQ:(c + 1) * SQ], v[u][:, t, h, :],
                                          probs[t % 2][:, h * SQ:(h + 1) * SQ], start=(t == 0 and c == 0),
                                          stop=(t == KT - 1), skip_group_check=True)
                mm.then_inc(probs_used, 1)

            def spread_sums(b, split):
                pe.wait_ge(acc_taken, b * 4 + 4)
                pe.wait_ge(max_split, split)
                nc.tensor.matmul(s.ps[:, 7, 256:256 + 4 * SQ], sum_rows[:, :, :].rearrange("p j i -> p (j i)"),
                                 acc[:, :], start=True, stop=True).then_inc(sums_made, 1)

            def step(b, u, i, last=False):
                pe.wait_ge(k_lo_made, b * NKC + NKC)
                for t in range(KT):
                    ahead = [] if last or t >= len(slots) else slots[t]
                    wait(pe, probs_made, b * KT + t - 1)
                    tile = slice(t * KP, (t + 1) * KP)
                    for w, m in ((k_hi[u], qd_hi[u]), (k_hi[u], qd_lo[u]), (k_lo[u], qd_hi[u])):
                        for h in range(2):
                            nc.tensor.matmul(s.ps[0:KP, 2 * (t % 2) + h, 0:HQ // 2], w[:, tile],
                                             m[:, h * (HQ // 2):(h + 1) * (HQ // 2)],
                                             start=(w is k_hi[u] and m is qd_hi[u]), stop=False)
                    if t == 0:
                        pe.wait_ge(row_moved, b * 32 + 32)
                    for h in range(2):
                        mm = nc.tensor.matmul(s.ps[0:KP, 2 * (t % 2) + h, 0:HQ // 2], ones_2[:, 0:KP],
                                              shift[u][:, h * (HQ // 2):(h + 1) * (HQ // 2)], start=False, stop=True)
                    mm.then_inc(scores_made, 1)
                    for product, n in ahead[:2]:
                        product(b + 1, *following(u, i), n)
                    if t:
                        values(b, u, t - 1)
                    for product, n in ahead[2:]:
                        product(b + 1, *following(u, i), n)
                    if t == 2 and not (isinstance(b, int) and b == 0):
                        spread_sums(b - 1, b * 2 + 2)
                    if t == KT - 2 and not last:
                        turn(b + 1, 1 - u)
                values(b, u, KT - 1)

            def first(b, u, i):
                for slot in slots:
                    for product, n in slot:
                        product(b, u, i, n)
                turn(b, u)

            def end(b, u, i):
                step(b, u, i, last=True)
                spread_sums(b, b * 2 + 2)
            one_ahead(pe, first, step, end)

        @block.scalar
        def _(act):
            def take_keys(b, u, k):
                act.wait_ge(scratch_dve, b * ND + k + 1)
                wait(act, scores_made, b * KT - KT)
                cols = slice(k * KC, (k + 1) * KC)
                nc.scalar.activation(k_hi[u][:, cols], k_full[:, cols], ACT.Copy).then_inc(k_hi_made, 1)

            def take_values(b, u, g):
                if g == 0:
                    wait(act, probs_used, b * KT - KT)
                act.wait_ge(products, b * (NKC + NV) + NKC + g + 1)
                nc.scalar.activation(v[u][:, 4 * g:4 * g + 4, :, 0:DK],
                                     s.ps[0:KP, 4 + (g + 1) % 2, :].rearrange("p (t h d) -> p t h d", t=4, h=H16),
                                     ACT.Copy).then_inc(scratch_act, 1)

            slots = [[(take_keys, 0), (take_keys, 1)], [(take_keys, 2), (take_values, 0)],
                     [(take_values, 1), (take_values, 2)]]

            def first(b, u, i):
                for slot in slots:
                    for take, n in slot:
                        take(b, u, n)

            def step(b, u, i, last=False):
                for t in range(KT):
                    act.wait_ge(scores_made, b * KT + t + 1)
                    wait(act, probs_used, b * KT + t - 1)
                    if masked and t == 0:
                        act.wait_ge(masks_made, b * 3 + 3)
                    nc.scalar.activation(probs[t % 2][:, :].rearrange("p (h c) -> p h c", h=2),
                                         s.ps[0:KP, 2 * (t % 2):2 * (t % 2) + 2, 0:HQ // 2], ACT.Exp,
                                         bias=neg_col[:, u, t:t + 1] if masked else 0.0).then_inc(probs_made, 1)
                    for take, n in [] if last or t >= len(slots) else slots[t]:
                        take(b + 1, 1 - u, n)
                act.wait_ge(probs_used, b * KT + KT)
                wait(act, normed, b)
                for j in range(4):
                    rows = slice(32 * j, 32 * j + DK + 1)
                    nc.scalar.activation(acc[rows, :], s.ps[rows, 6, 0:4 * SQ], ACT.Copy).then_inc(acc_taken, 1)

            def end(b, u, i):
                step(b, u, i, last=True)
            one_ahead(act, first, step, end)

        @block.vector
        def _(dve):
            for h in range(2):
                half = slice(h * TOK // 2, (h + 1) * TOK // 2)
                nc.vector.tensor_copy(qd_hi[h][:, :], q[:, half]).then_inc(q_split, 1)
                dve.wait_ge(q_split, 2 * h + 1)
                nc.vector.tensor_tensor(q_lo[:, half], q[:, half], qd_hi[h][:, :].bitcast(F32), ALU.subtract)\
                    .then_inc(q_split, 1)

            def prepare(b, u, i, before=None):
                if masked:
                    dve.wait_ge(loaded[u], i * (16 * NL) + 16 * NL)
                    nc.vector.tensor_scalar(neg_row[:, :], mask_i[:, :], 0.0, MASKED, ALU.is_equal, ALU.mult)\
                        .then_inc(masks_made, 1)
                    nc.vector.tensor_scalar(valid_row[:, :], mask_i[:, :], 0.0, None, ALU.not_equal)\
                        .then_inc(masks_made, 1)
                    wait(dve, probs_made, b * KT - KT)
                    nc.vector.tensor_scalar(neg_col[:, u, :], mask_n[u][:, :], 0.0, MASKED, ALU.is_equal, ALU.mult)\
                        .then_inc(masks_made, 1)
                    dve.wait_ge(masks_made, b * 3 + 3)
                for k in range(NKC):
                    cols = slice(k * KC, (k + 1) * KC)
                    dve.wait_ge(products, b * (NKC + NV) + k + 1)
                    wait(dve, k_lo_made, b * NKC)
                    if masked:
                        nc.vector.scalar_tensor_tensor(k_full[:, cols], s.ps[:, 4 + k % 2, 0:KC], bias[:, 1:2],
                                                       valid_row[:, cols], ALU.add, ALU.mult).then_inc(scratch_dve, 1)
                    else:
                        nc.vector.tensor_scalar(k_full[:, cols], s.ps[:, 4 + k % 2, 0:KC], bias[:, 1:2], None, ALU.add)\
                            .then_inc(scratch_dve, 1)
                if before is not None:
                    norm(before)
                for n in range(ROWS):
                    t, k = n // NKC, n % NKC
                    dve.wait_ge(k_rows, b * ROWS + n + 1)
                    if masked:
                        nc.vector.memset(carrier[:, n:n + 1], 0.0)
                        nc.vector.tensor_tensor_reduce(s.ps[:, 4 + n % 2, 0:KC], s.ps[:, 4 + n % 2, 0:KC], neg_row[:, k * KC:(k + 1) * KC],
                                                       1.0, -3e38, ALU.add, ALU.max, chunk_max[:, u, t, k:k + 1])\
                            .then_inc(scratch_dve, 1)
                    else:
                        nc.vector.tensor_reduce(chunk_max[:, u, t, k:k + 1], s.ps[:, 4 + n % 2, 0:KC], AX.X, ALU.max)\
                            .then_inc(scratch_dve, 1)
                dve.wait_ge(scratch_dve, b * ND + ND)
                wait(dve, max_turned, b - 1)
                nc.vector.tensor_reduce(max_col[:, u, :], chunk_max[:, u, :, :], AX.X, ALU.max, negate=True)\
                    .then_inc(max_made, 1)

            def split(b, u):
                dve.wait_ge(max_turned, b + 1)
                wait(dve, row_moved, b * 32 - 32)
                nc.vector.tensor_copy(max_hi[:, u, :], s.ps[0:RT, 7, 0:D]).then_inc(max_split, 1)
                dve.wait_ge(max_split, b * 2 + 1)
                nc.vector.tensor_tensor(max_lo[:, u, :], s.ps[0:RT, 7, 0:D], max_hi[:, u, :].bitcast(F32), ALU.subtract)\
                    .then_inc(max_split, 1)

            def norm(b):
                dve.wait_ge(sums_made, b + 1)
                nc.vector.reciprocal(inv[:, :], s.ps[:, 7, 256:256 + 4 * SQ]).then_inc(inverted, 1)
                dve.wait_ge(inverted, b + 1)
                nc.vector.tensor_tensor(heads_out[:, :, batch_of(b)], acc[:, :].rearrange("p (c q) -> p c q", c=4),
                                        inv[:, :].rearrange("p (c q) -> p c q", c=4), ALU.mult).then_inc(normed, 1)

            def first(b, u, i):
                prepare(b, u, i)
                split(b, u)

            def step(b, u, i):
                prepare(b + 1, *following(u, i), before=None if isinstance(b, int) and b == 0 else b - 1)
                split(b + 1, 1 - u)

            def end(b, u, i):
                norm(b - 1)
                norm(b)
            one_ahead(dve, first, step, end)

        batches.close()
        output_projection(nc, s, layer, heads_out, wo_quad, bv_quad, bias[:, 2:3])

def output_projection(nc, s, name, heads_out, wo_quad, bv_quad, bias):
    with ExitStack() as ctx:
        biased, product_made, added = (ctx.enter_context(nc.semaphore(f"{name}_{n}"))
                                       for n in ("biased", "product_made", "added"))
        block = ctx.enter_context(nc.Block())

        @block.tensor
        def _(pe):
            for c in range(NCH):
                pe.wait_ge(biased, c + 1)
                for g in range(4):
                    mm = nc.tensor.matmul(s.ps[:, c, 0:CH], wo_quad[:, g, :], heads_out[:, g, c * CH:(c + 1) * CH],
                                          start=(g == 0), stop=(g == 3))
                mm.then_inc(product_made, 1)

        @block.gpsimd
        def _(pool):
            for c in range(NCH):
                cols = heads_out[:, :, c * CH:(c + 1) * CH]
                nc.gpsimd.tensor_tensor(cols, cols, bcast(bv_quad[:, :], CH, 2), ALU.add).then_inc(biased, 1)

        @block.vector
        def _(dve):
            for c in range(NCH):
                dve.wait_ge(product_made, c + 1)
                nc.vector.scalar_tensor_tensor(s.x_T[:, c * CH:(c + 1) * CH], s.ps[:, c, 0:CH], bias,
                                               s.x_T[:, c * CH:(c + 1) * CH], ALU.add, ALU.add).then_inc(added, 1)


def quantized(nc, s, a):
    with ExitStack() as ctx:
        def sb(name, shape, dt=F32):
            return ctx.enter_context(nc.sbuf_tensor(f"q2_{name}", shape, dt))

        def sem(name):
            return ctx.enter_context(nc.semaphore(f"q2_{name}"))

        w1, w2, b1, b2 = sb("w1", [D, HID]), sb("w2", [D, HT, D]), sb("b1", [D, HT]), sb("b2", [D, 1])
        quarter = sb("quarter", [D, 1])
        h, clamped, cell, y0, y1, hq = (sb(n, [D, HT, CH]) for n in ("h", "clamped", "cell", "y0", "y1", "hq"))
        out = sb("out", [D, CH])
        load(nc, s, [(w1[:, :], a["L2_w1"]), (w2[:, :, :].rearrange("p j o -> p (j o)"), a["L2_w2"]),
                           (b1[:, :], a["L2_b1"]), (b2[:, :], a["L2_b2"])])
        ready, hidden_made, scaled, step, cells, ends, sloped, out_made = (
            sem(n) for n in ("ready", "hidden_made", "scaled", "step", "cells", "ends", "sloped", "out_made"))
        start_at_one(nc, [scaled, step, out_made])
        STEPS = 12
        block = ctx.enter_context(nc.Block())

        @block.tensor
        def _(pe):
            with pe.Fori(0, NCH) as c:
                pe.wait_ge(scaled, 1 + c * HT)
                for j in range(HT):
                    nc.tensor.matmul(s.ps[:, j, 0:CH], w1[:, j * D:(j + 1) * D], s.xn[:, bass.ds(c * CH, CH)],
                                     start=True, stop=True).then_inc(hidden_made, 1)
                pe.wait_ge(step, 1 + c * STEPS + 9)
                for j in range(HT):
                    mm = nc.tensor.matmul(s.ps[:, 4, 0:CH], w2[:, j, :], hq[:, j, :], start=(j == 0), stop=(j == HT - 1))
                mm.then_inc(out_made, 1)

        @block.scalar
        def _(act):
            act.wait_ge(ready, 3)
            with act.Fori(0, NCH) as c:
                act.wait_ge(step, 1 + c * STEPS)
                for j in range(HT):
                    act.wait_ge(hidden_made, c * HT + j + 1)
                    nc.scalar.activation(h[:, j, :], s.ps[:, j, 0:CH], ACT.Identity, bias=b1[:, j:j + 1], scale=256.0)\
                        .then_inc(scaled, 1)
                act.wait_ge(step, 1 + c * STEPS + 4)
                nc.scalar.activation(y0[:, :, :], cell[:, :, :], ACT.Gelu, scale=0.25).then_inc(ends, 1)
                nc.scalar.activation(y1[:, :, :], cell[:, :, :], ACT.Gelu, bias=quarter[:, 0:1], scale=0.25)\
                    .then_inc(ends, 1)

        @block.gpsimd
        def _(pool):
            with pool.Fori(0, NCH) as c:
                pool.wait_ge(ends, c * 2 + 2)
                nc.gpsimd.tensor_tensor(y1[:, :, :], y1[:, :, :], y0[:, :, :], ALU.subtract).then_inc(sloped, 1)
                pool.wait_ge(sloped, c * 2 + 1)
                pool.wait_ge(step, 1 + c * STEPS + 5)
                nc.gpsimd.tensor_tensor(y1[:, :, :], y1[:, :, :], clamped[:, :, :], ALU.mult).then_inc(sloped, 1)

        @block.vector
        def _(dve):
            nc.vector.memset(quarter[:, :], 0.25).then_inc(ready, 1)
            nc.vector.tensor_scalar(b1[:, :], b1[:, :], 256.0, None, ALU.mult).then_inc(ready, 1)
            nc.vector.tensor_scalar(b2[:, :], b2[:, :], 256.0, None, ALU.mult).then_inc(ready, 1)
            with dve.Fori(0, NCH) as c:
                count = [0]

                def chain(ins):
                    count[0] += 1
                    ins.then_inc(step, 1)
                    dve.wait_ge(step, 1 + c * STEPS + count[0])

                dve.wait_ge(scaled, 1 + c * HT + HT)
                chain(nc.vector.tensor_scalar(h[:, :, :], h[:, :, :], MAGIC, MAGIC, ALU.add, ALU.subtract))
                chain(nc.vector.tensor_scalar(clamped[:, :, :], h[:, :, :], -1024.0, 1024.0, ALU.max, ALU.min))
                chain(nc.vector.tensor_scalar(cell[:, :, :], clamped[:, :, :], 1.0 / 64, -0.5 + 1.0 / 128,
                                              ALU.mult, ALU.add))
                chain(nc.vector.tensor_scalar(cell[:, :, :], cell[:, :, :], MAGIC, MAGIC, ALU.add, ALU.subtract))
                chain(nc.vector.scalar_tensor_tensor(clamped[:, :, :], cell[:, :, :], -64.0, clamped[:, :, :],
                                                     ALU.mult, ALU.add))
                chain(nc.vector.tensor_scalar(h[:, :, :], h[:, :, :], -1024.0, 0.0, ALU.add, ALU.max))
                dve.wait_ge(sloped, c * 2 + 2)
                chain(nc.vector.scalar_tensor_tensor(y0[:, :, :], y1[:, :, :], 1.0 / 64, y0[:, :, :], ALU.mult, ALU.add))
                chain(nc.vector.scalar_tensor_tensor(h[:, :, :], y0[:, :, :], 256.0, h[:, :, :], ALU.mult, ALU.add))
                dve.wait_ge(out_made, 1 + c)
                chain(nc.vector.tensor_scalar(hq[:, :, :], h[:, :, :], MAGIC, MAGIC, ALU.add, ALU.subtract))
                dve.wait_ge(out_made, 1 + c + 1)
                chain(nc.vector.tensor_scalar(out[:, :], s.ps[:, 4, 0:CH], b2[:, 0:1], None, ALU.add))
                chain(nc.vector.tensor_scalar(out[:, :], out[:, :], MAGIC, MAGIC, ALU.add, ALU.subtract))
                chain(nc.vector.scalar_tensor_tensor(s.x_T[:, bass.ds(c * CH, CH)], out[:, :], 1.0 / 256,
                                                     s.x_T[:, bass.ds(c * CH, CH)], ALU.mult, ALU.add))


def routed(nc, s, a):
    NE = 3
    with ExitStack() as ctx:
        def sb(name, shape, dt=F32):
            return ctx.enter_context(nc.sbuf_tensor(f"r3_{name}", shape, dt))

        def sem(name):
            return ctx.enter_context(nc.semaphore(f"r3_{name}"))

        w1, w2, b1, b2 = sb("w1", [D, NE, HID]), sb("w2", [D, NE * HT, D]), sb("b1", [D, NE * HT]), sb("b2", [D, NE])
        gate, gates = sb("gate", [D, 2]), sb("gates", [D, 2, D])
        bias = sb("bias", [D, 1])
        second = sb("second", [D, CH])
        routed_x = sb("routed_x", [D, 2, CH])
        hidden = sb("hidden", [D, 4, CH])
        load(nc, s, [(w1[:, 0:2, :], a["L3_w1"]), (w1[:, 2, :], a["L3_sw1"]),
                           (w2[:, 0:2 * HT, :], a["L3_w2"]), (w2[:, 2 * HT:, :], a["L3_sw2"]),
                           (b1[:, 0:2 * HT], a["L3_b1"]), (b1[:, 2 * HT:], a["L3_sb1"]),
                           (b2[:, 0:2], a["L3_b2"]), (b2[:, 2:3], a["L3_sb2"]), (gate[:, :], a["L3_gate_w"])])
        ready, gates_made, second_taken, route, hidden_made, hidden_taken, out_made, out_taken = (
            sem(n) for n in ("ready", "gates_made", "second_taken", "route", "hidden_made", "hidden_taken",
                             "out_made", "out_taken"))
        start_at_one(nc, [route, second_taken, out_taken, hidden_taken, out_made, hidden_made])
        NT = NE * HT
        block = ctx.enter_context(nc.Block())

        @block.tensor
        def _(pe):
            pe.wait_ge(ready, 2)
            with pe.Fori(0, NCH) as c:
                chunk = s.xn[:, bass.ds(c * CH, CH)]
                pe.wait_ge(route, 1 + c * 3)
                pe.wait_ge(second_taken, 1 + c)
                for g in range(2):
                    nc.tensor.matmul(s.ps[:, 5 + g, 0:CH], gates[:, g, :], chunk, start=True, stop=True)\
                        .then_inc(gates_made, 1)
                pe.wait_ge(out_taken, 1 + c)
                order = [2, 0, 1]
                for n in range(NT + 2):
                    if n < NT:
                        e, j = order[n // HT], n % HT
                        if n >= 4:
                            pe.wait_ge(hidden_taken, 1 + c * NT + n - 3)
                        else:
                            pe.wait_ge(hidden_taken, 1 + c * NT)
                        if e < 2 and j == 0:
                            pe.wait_ge(route, 1 + c * 3 + 2 + e)
                        nc.tensor.matmul(s.ps[:, n % 4, 0:CH], w1[:, e, j * D:(j + 1) * D],
                                         chunk if e == 2 else routed_x[:, e, :], start=True, stop=True)\
                            .then_inc(hidden_made, 1)
                    if n >= 2:
                        m = n - 2
                        pe.wait_ge(hidden_taken, 1 + c * NT + m + 1)
                        nc.tensor.matmul(s.ps[:, 4, 0:CH], w2[:, order[m // HT] * HT + m % HT, :], hidden[:, m % 4, :],
                                         start=(m == 0), stop=(m == NT - 1)).then_inc(out_made, 1)

        @block.scalar
        def _(act):
            with act.Fori(0, NCH) as c:
                act.wait_ge(gates_made, c * 2 + 2)
                act.wait_ge(route, 1 + c * 3)
                nc.scalar.activation(second[:, :], s.ps[:, 6, 0:CH], ACT.Copy).then_inc(second_taken, 1)
                for n in range(NT):
                    e, j = [2, 0, 1][n // HT], n % HT
                    act.wait_ge(hidden_made, 1 + c * NT + n + 1)
                    if n >= 4:
                        act.wait_ge(out_made, 1 + c * NT + n - 3)
                    else:
                        act.wait_ge(out_made, 1 + c * NT)
                    nc.scalar.activation(hidden[:, n % 4, :], s.ps[:, n % 4, 0:CH], ACT.Relu,
                                         bias=b1[:, e * HT + j:e * HT + j + 1]).then_inc(hidden_taken, 1)

        @block.vector
        def _(dve):
            nc.vector.tensor_copy(gates[:, :, :], bcast(gate[:, :], D, 2)).then_inc(ready, 1)
            nc.vector.tensor_reduce(bias[:, :], b2[:, :], AX.X, ALU.add).then_inc(ready, 1)
            dve.wait_ge(ready, 2)
            with dve.Fori(0, NCH) as c:
                chunk = s.xn[:, bass.ds(c * CH, CH)]
                dve.wait_ge(second_taken, 1 + c + 1)
                dve.wait_ge(hidden_made, 1 + c * NT)
                nc.vector.tensor_tensor(routed_x[:, 1, :], s.ps[:, 5, 0:CH], second[:, :], ALU.is_ge).then_inc(route, 1)
                dve.wait_ge(route, 1 + c * 3 + 1)
                nc.vector.tensor_tensor(routed_x[:, 0, :], routed_x[:, 1, :], chunk, ALU.mult).then_inc(route, 1)
                dve.wait_ge(route, 1 + c * 3 + 2)
                nc.vector.tensor_tensor(routed_x[:, 1, :], chunk, routed_x[:, 0, :], ALU.subtract).then_inc(route, 1)
                dve.wait_ge(out_made, 1 + c * NT + NT)
                nc.vector.scalar_tensor_tensor(s.x_T[:, bass.ds(c * CH, CH)], s.ps[:, 4, 0:CH], bias[:, 0:1],
                                               s.x_T[:, bass.ds(c * CH, CH)], ALU.add, ALU.add).then_inc(out_taken, 1)


def attention_latents(nc, s, a):
    with ExitStack() as ctx:
        def sb(name, shape, dt=F32):
            return ctx.enter_context(nc.sbuf_tensor(f"l3_{name}", shape, dt))

        def sem(name):
            return ctx.enter_context(nc.semaphore(f"l3_{name}"))

        NP = 4
        affine = sb("affine", [D, 6])
        latents = sb("latents", [D, TOK])
        q = sb("q", [D, NP, TOK])
        wq, wk, wkT, wv = sb("wq", [D, HID]), sb("wk", [D, HID]), sb("wkT", [D, NP, D]), sb("wv", [D, HID])
        wo = sb("wo", [D, NP, D])
        bx_rows = sb("bx_rows", [SQ, D])
        values_bias, out_bias = sb("values_bias", [D, NP]), sb("out_bias", [D, 1])
        neg_cols = sb("neg_cols", [KP, B, KT])
        load(nc, s, [(affine[:, k:k + 1], a[f"L3_{n}"]) for k, n in
                           enumerate(("ln_x_w", "ln_x_b", "ln_l_w", "ln_l_b", "ln_o_w", "ln_o_b"))] +
             [(wq[:, :], a["L3_Wq"]), (wk[:, :], a["L3_Wk"]), (wkT[:, :, :], a["L3_WkT"]), (wv[:, :], a["L3_Wv"]),
              (wo[:, :, :], a["L3_Wo"]), (bx_rows[:, :], a["L3_bx_row"].broadcast_to([SQ, D]))])
        layer_norm(nc, s, "l3l", s.xn, latents, affine[:, 2:3], affine[:, 3:4])

        with ExitStack() as sub:
            def tmp(name, shape, dt=F32):
                return sub.enter_context(nc.sbuf_tensor(f"l3_{name}", shape, dt))

            masks = tmp("masks", [KP, B, KT], mybir.dt.uint8)
            scales = tmp("scales", [D, 2])
            head_sel, head_selT = tmp("head_sel", [D, NP, H8]), tmp("head_selT", [H8, NP, D])
            squares = tmp("squares", [D, NP, CH])
            inv = tmp("q_inv", [H8, CH])
            load(nc, s, [(masks[:, :, :], a["mask_B"].rearrange("b (p t) -> p b t", t=KT)), (scales[0:DH, 0:1], a["L3_q_scale"]),
                                (scales[DH:D, 0:1], a["L3_q_scale"]), (scales[0:DH, 1:2], a["L3_k_scale"]),
                                (scales[DH:D, 1:2], a["L3_k_scale"])])
            made, step, q_made, squared, norms_made, std, spread_made = (
                sub.enter_context(nc.semaphore(f"l3q_{n}")) for n in
                ("made", "step", "q_made", "squared", "norms_made", "std", "spread_made"))
            with nc.Block() as block:
                @block.gpsimd
                def _(pool):
                    nc.gpsimd.memset(head_sel[:, :, :], 1.0).then_inc(made, 1)
                    nc.gpsimd.memset(head_selT[:, :, :], 1.0).then_inc(made, 1)
                    pool.wait_ge(made, 2)
                    nc.gpsimd.affine_select(out=head_sel[:, :, :], in_=head_sel[:, :, :], compare_op=ALU.is_ge, fill=0.0,
                                            base=0, pattern=[[D, NP], [-DH, H8]], channel_multiplier=1).then_inc(made, 1)
                    nc.gpsimd.affine_select(out=head_selT[:, :, :], in_=head_selT[:, :, :], compare_op=ALU.is_ge,
                                            fill=0.0, base=0, pattern=[[D, NP], [1, D]], channel_multiplier=-DH)\
                        .then_inc(made, 1)
                    pool.wait_ge(made, 4)
                    nc.gpsimd.affine_select(out=head_sel[:, :, :], in_=head_sel[:, :, :], compare_op=ALU.is_ge, fill=0.0,
                                            base=DH - 1, pattern=[[-D, NP], [DH, H8]], channel_multiplier=-1)\
                        .then_inc(made, 1)
                    nc.gpsimd.affine_select(out=head_selT[:, :, :], in_=head_selT[:, :, :], compare_op=ALU.is_ge,
                                            fill=0.0, base=DH - 1, pattern=[[-D, NP], [-1, D]],
                                            channel_multiplier=DH).then_inc(made, 1)

                @block.tensor
                def _(pe):
                    pe.wait_ge(made, 6)
                    for c in range(NCH):
                        if c:
                            pe.wait_ge(q_made, 4 * c)
                        for j in range(NP):
                            mm = nc.tensor.matmul(s.ps[:, j, 0:CH], wq[:, j * D:(j + 1) * D],
                                                  latents[:, c * CH:(c + 1) * CH], start=True, stop=True)
                        mm.then_inc(norms_made, 1)
                        pe.wait_ge(squared, c + 1)
                        for j in range(NP):
                            mm = nc.tensor.matmul(s.ps[0:H8, 4, 0:CH], head_sel[:, j, :], squares[:, j, :],
                                                  start=(j == 0), stop=(j == NP - 1))
                        mm.then_inc(norms_made, 1)
                        pe.wait_ge(step, 2 + 3 * c + 2)
                        for j in range(NP):
                            if j:
                                pe.wait_ge(q_made, 4 * c + j)
                            nc.tensor.matmul(s.ps[:, 5, 0:CH], head_selT[:, j, :], inv[:, :], start=True, stop=True)\
                                .then_inc(spread_made, 1)

                @block.scalar
                def _(act):
                    for c in range(NCH):
                        act.wait_ge(norms_made, 2 * c + 1)
                        nc.scalar.activation(squares[:, :, :], s.ps[:, 0:NP, 0:CH], ACT.Square).then_inc(squared, 1)
                        act.wait_ge(norms_made, 2 * c + 2)
                        if c:
                            act.wait_ge(spread_made, 4 * c)
                        nc.scalar.activation(inv[:, :], s.ps[0:H8, 4, 0:CH], ACT.Sqrt).then_inc(std, 1)

                @block.vector
                def _(dve):
                    nc.vector.tensor_scalar(neg_cols[:, :, :], masks[:, :, :], 0.0, NEVER, ALU.is_equal, ALU.mult)\
                        .then_inc(step, 1)
                    nc.vector.scalar_tensor_tensor(scales[:, 0:1], scales[:, 0:1], 8.0, scales[:, 1:2], ALU.mult,
                                                   ALU.mult).then_inc(step, 1)
                    for c in range(NCH):
                        dve.wait_ge(squared, c + 1)
                        dve.wait_ge(std, c + 1)
                        nc.vector.tensor_scalar(inv[:, :], inv[:, :], L2_EPS, None, ALU.max).then_inc(step, 1)
                        dve.wait_ge(step, 2 + 3 * c + 1)
                        nc.vector.reciprocal(inv[:, :], inv[:, :]).then_inc(step, 1)
                        nc.vector.tensor_scalar(q[:, :, c * CH:(c + 1) * CH], s.ps[:, 0:NP, 0:CH], scales[:, 0:1],
                                                None, ALU.mult).then_inc(step, 1)
                        dve.wait_ge(step, 2 + 3 * c + 3)
                        for j in range(NP):
                            dve.wait_ge(spread_made, 4 * c + j + 1)
                            cols = q[:, j, c * CH:(c + 1) * CH]
                            nc.vector.tensor_tensor(cols, cols, s.ps[:, 5, 0:CH], ALU.mult).then_inc(q_made, 1)

        bias_made, bias_taken = sem("bias_made"), sem("bias_taken")
        with nc.Block() as block:
            @block.tensor
            def _(pe):
                for j in range(NP):
                    mm = nc.tensor.matmul(s.ps[:, 0, j:j + 1], wv[:, j * D:(j + 1) * D], affine[:, 1:2], start=True,
                                          stop=True, skip_group_check=True)
                mm.then_inc(bias_made, 1)
                pe.wait_ge(bias_taken, 1)
                for j in range(NP):
                    mm = nc.tensor.matmul(s.ps[:, 1, 0:1], wo[:, j, :], values_bias[:, j:j + 1], start=(j == 0),
                                          stop=(j == NP - 1))
                mm.then_inc(bias_made, 1)

            @block.vector
            def _(dve):
                dve.wait_ge(bias_made, 1)
                nc.vector.tensor_copy(values_bias[:, :], s.ps[:, 0, 0:NP]).then_inc(bias_taken, 1)
                dve.wait_ge(bias_made, 2)
                nc.vector.tensor_copy(out_bias[:, :], s.ps[:, 1, 0:1]).then_inc(bias_taken, 1)

        T = KT + 1
        NG = KT // 4
        raw = [sb(f"ctx_N{u}", [KP, KT, D]) for u in range(2)]
        z = [sb(f"z{u}", [KP, KT, D]) for u in range(2)]
        stats, moments, rstd = sb("stats", [KP, KT, 6]), sb("moments", [KP, 4, KT]), sb("rstd", [KP, KT])
        mean_rstd = sb("mean_rstd", [KP, KT])
        xnT = [sb(f"xnT{u}", [D, SK + SQ]) for u in range(2)]
        lat_N = [sb(f"lat_N{u}", [SQ, D]) for u in range(2)]
        squares = sb("k_squares", [KP, 2, HID])
        norms = sb("norms", [KP, KT + 1, H8])
        inv_norms = sb("inv_norms", [KP, KT + 1, H8])
        q_blocks = sb("q_blocks", [D, NP, 2, SQ])
        G = sb("G", [D, HQ3])
        neg = [sb(f"neg{u}", [KP, KT]) for u in range(2)]
        S = sb("S", [KP, KT + 1, HQ3])
        top = sb("top", [KP, HQ3])
        neg_max = sb("neg_max", [2 * SQ, NP])
        diag = sb("diag", [2 * SQ, NP, 2 * SQ])
        shift = sb("shift", [KP, HQ3])
        prob_sum = sb("prob_sum", [KP, NG, HQ3])
        inv, mixed, mixed_lat = sb("inv", [D, NP * SQ]), sb("mixed", [D, HQ3]), sb("mixed_lat", [D, HQ3])
        heads = sb("heads", [D, NP, SQ])
        loaded = [sem("even_loaded"), sem("odd_loaded")]
        (init, blocks_zeroed, lat_copied, qb_made, stats_made, mean_made, std_made, rstd_made, z_made, turned,
         xnT_made, lat_turned, lat_made, k_made, squared, reduced, root_made, inv_made, G_made, G_taken, negs_made,
         raw_made, S_made, topped, top_turned, maxed, diag_made, spread_made, shift_made, shifted, exps_made,
         summed, sums_made, lat_mixed, mixed_made, inv_sums, heads_made, heads_taken, y_made, y_taken) = (
            sem(n) for n in (
                "init", "blocks_zeroed", "lat_copied", "qb_made", "stats_made", "mean_made", "std_made", "rstd_made",
                "z_made", "turned", "xnT_made", "lat_turned", "lat_made", "k_made", "squared", "reduced", "root_made",
                "inv_made", "G_made", "G_taken", "negs_made", "raw_made", "S_made", "topped", "top_turned", "maxed",
                "diag_made", "spread_made", "shift_made", "shifted", "exps_made", "summed", "sums_made", "lat_mixed", "mixed_made",
                "inv_sums", "heads_made", "heads_taken", "y_made", "y_taken"))
        NM = 4

        AHEAD = 5

        def rows(t):
            return KP if t < KT else SQ

        batches = ExitStack()
        block = batches.enter_context(nc.Block())

        def staged(eng, first, step, last):
            first()
            step(0, 0, 0, True)
            with eng.Fori(0, B // 2 - 2) as j:
                step(j * 2 + 1, 1, j, True)
                step(j * 2 + 2, 0, j + 1, True)
            step(B - 3, 1, B // 2 - 2, True)
            step(B - 2, 0, B // 2 - 1, False)
            last(B - 1, 1, B // 2 - 1)

        @block.sync
        def _(sp):
            def fetch(b, u):
                wait(sp, z_made, b - 1)
                sp.dma_start(raw[u][:, :, :], a["ctx_N"][bass.ds(b, 1)].rearrange("a (p t) d -> (a p) t d", t=KT))\
                    .then_inc(loaded[u], 16)
            fetch(0, 0)
            fetch(1, 1)
            with sp.Fori(1, B // 2) as j:
                fetch(j * 2, 0)
                fetch(j * 2 + 1, 1)

        @block.gpsimd
        def _(pool):
            def queries(b):
                wait(pool, G_made, b)
                for half in range(2):
                    r = slice(half * DH, (half + 1) * DH)
                    nc.gpsimd.tensor_copy(q_blocks[r, :, half, :], q[r, :, batch_of(b)]).then_inc(qb_made, 1)
                    pool.wait_ge(qb_made, b * 2 + half + 1)

            def take_latents(b, u):
                wait(pool, raw_made, b * T - T)
                nc.gpsimd.tensor_copy(xnT[u][:, SK:], latents[:, batch_of(b)]).then_inc(lat_copied, 1)
                pool.wait_ge(lat_copied, b + 1)

            def subtract_maxima(b):
                pool.wait_ge(shift_made, b + 1)
                for t in range(T):
                    r = rows(t)
                    nc.gpsimd.tensor_tensor(S[0:r, t, :], S[0:r, t, :], shift[0:r, :], ALU.add).then_inc(shifted, 1)

            def first():
                nc.gpsimd.memset(q_blocks[:, :, :, :], 0.0).then_inc(blocks_zeroed, 1)
                pool.wait_ge(blocks_zeroed, 1)
                take_latents(0, 0)
                queries(0)
                take_latents(1, 1)
                queries(1)

            def step(b, u, i, more):
                subtract_maxima(b)
                if more:
                    take_latents(b + 2, u)
                    queries(b + 2)

            def last(b, u, i):
                subtract_maxima(b)
            staged(pool, first, step, last)

        @block.tensor
        def _(pe):
            def turn_context(b, u, g):
                if g == 0:
                    pe.wait_ge(z_made, b + 1)
                if g < 2:
                    wait(pe, squared, b * T)
                elif g < NG:
                    pe.wait_ge(xnT_made, b * NG + g - 1)
                if g < NG:
                    for t in range(4):
                        mm = nc.tensor.transpose(s.ps[:, g % 2, t * KP:(t + 1) * KP], z[u][:, 4 * g + t, :],
                                                 s.ident[0:KP, 0:KP])
                    mm.then_inc(turned, 1)
                else:
                    nc.tensor.transpose(s.ps[0:SQ, NG % 2, 0:D], xnT[u][:, SK:], s.ident[:, :]).then_inc(lat_turned, 1)

            def latents_may_turn(b):
                pe.wait_ge(lat_copied, b + 1)
                pe.wait_ge(xnT_made, b * NG + 2)

            def key_product(b, u, t):
                if t == 0:
                    pe.wait_ge(xnT_made, b * NG + NG)
                elif t == 1:
                    pe.wait_ge(lat_made, b + 1)
                else:
                    pe.wait_ge(squared, b * T + t - 1)
                nc.tensor.matmul(s.ps[0:rows(t), t % 2, 0:HID], xnT[u][:, t * KP:t * KP + rows(t)], wk[:, :],
                                 start=True, stop=True).then_inc(k_made, 1)

            def queries_through_keys(b):
                pe.wait_ge(qb_made, b * 2 + 2)
                wait(pe, maxed, b)
                for j in range(NP):
                    mm = nc.tensor.matmul(s.ps[:, 4, j * 2 * SQ:(j + 1) * 2 * SQ], wkT[:, j, :],
                                          q_blocks[:, j, :, :].rearrange("p h q -> p (h q)"), start=True, stop=True,
                                          skip_group_check=True)
                mm.then_inc(G_made, 1)

            def score_product(b, u, t):
                if t == 0:
                    pe.wait_ge(G_taken, b + 1)
                wait(pe, S_made, b * T + max(t - 1, 0))
                nc.tensor.matmul(s.ps[0:rows(t), 2 + t % 2, 0:HQ3], xnT[u][:, t * KP:t * KP + rows(t)], G[:, :],
                                 start=True, stop=True).then_inc(raw_made, 1)

            def turn_maxima(b):
                pe.wait_ge(topped, b * KT + KT)
                wait(pe, y_taken, b)
                for j in range(NP):
                    mm = nc.tensor.transpose(s.ps[0:2 * SQ, 4, j * KP:(j + 1) * KP], top[:, j * 2 * SQ:(j + 1) * 2 * SQ],
                                             s.ident[0:KP, 0:KP])
                mm.then_inc(top_turned, 1)

            def spread_maxima(b):
                pe.wait_ge(diag_made, b + 1)
                wait(pe, heads_taken, b)
                nc.tensor.matmul(s.ps[0:KP, 5, 0:HQ3], s.ones[0:2 * SQ, 0:KP], diag[:, :, :].rearrange("p j q -> p (j q)"),
                                 start=True, stop=True).then_inc(spread_made, 1)

            def half_sums(keys, probs, start, stop):
                for half in range(2):
                    mm = nc.tensor.matmul(s.ps[half * DH:(half + 1) * DH, 5, 0:NP * SQ].rearrange("p (j q) -> p j q", j=NP),
                                          s.ones[0:keys, 0:DH],
                                          probs.rearrange("p (j h q) -> p h j q", j=NP, h=2)[:, half],
                                          start=start, stop=stop, skip_group_check=True)
                return mm

            def weigh(b, u, t):
                pe.wait_ge(exps_made, b * T + t + 1)
                nc.tensor.matmul(s.ps[:, 6, 0:HQ3], z[u][:, t, :], S[:, t, :], start=(t == 0), stop=(t == KT - 1))

            def weigh_latents(b, u):
                pe.wait_ge(exps_made, b * T + T)
                nc.tensor.matmul(s.ps[:, 7, 0:HQ3], lat_N[u][:, :], S[0:SQ, KT, :], start=True, stop=True)
                half_sums(SQ, S[0:SQ, KT, :], True, False)
                for g in range(NG):
                    pe.wait_ge(summed, b * NG + g + 1)
                    mm = half_sums(KP, prob_sum[:, g, :], False, g == NG - 1)
                mm.then_inc(sums_made, 1)

            def value_product(b):
                pe.wait_ge(mixed_made, b + 1)
                for h in range(H8):
                    r = slice((h % 2) * DH, (h % 2 + 1) * DH)
                    cols = slice(256 + (h // 2) * SQ, 256 + (h // 2 + 1) * SQ)
                    mm = nc.tensor.matmul(s.ps[r, 5, cols], wv[:, h * DH:(h + 1) * DH], mixed[:, h * SQ:(h + 1) * SQ],
                                          start=True, stop=True, skip_group_check=True)
                mm.then_inc(heads_made, 1)

            def project_out(b):
                pe.wait_ge(heads_taken, b + 1)
                for j in range(NP):
                    mm = nc.tensor.matmul(s.ps[:, 4, 0:SQ], wo[:, j, :], heads[:, j, :], start=(j == 0), stop=(j == NP - 1))
                mm.then_inc(y_made, 1)

            def scores(b, u, more, between):
                for t in range(T):
                    if more and t == T - 1:
                        latents_may_turn(b + 1)
                    score_product(b, u, t)
                    if t in between:
                        between[t]()
                    if more and t >= T - 1 - NG:
                        turn_context(b + 1, 1 - u, t - (T - 1 - NG))

            def first():
                pe.wait_ge(init, 1)
                for g in range(NG + 1):
                    if g == NG:
                        latents_may_turn(0)
                    turn_context(0, 0, g)
                for t in range(T):
                    key_product(0, 0, t)
                queries_through_keys(0)
                scores(0, 0, True, {})

            def step(b, u, i, more):
                turn_maxima(b)
                for t in range(T):
                    key_product(b + 1, 1 - u, t)
                    if t == 1:
                        spread_maxima(b)
                    if t == 4:
                        queries_through_keys(b + 1)
                    if t >= AHEAD:
                        weigh(b, u, t - AHEAD)
                for t in range(T - AHEAD, KT):
                    weigh(b, u, t)
                weigh_latents(b, u)
                scores(b + 1, 1 - u, more, {2: lambda: value_product(b), 7: lambda: project_out(b)})

            def last(b, u, i):
                turn_maxima(b)
                spread_maxima(b)
                for t in range(KT):
                    weigh(b, u, t)
                weigh_latents(b, u)
                value_product(b)
                project_out(b)
            staged(pe, first, step, last)

        @block.scalar
        def _(act):
            def std(b):
                act.wait_ge(stats_made, b * (KT + NM) + KT + NM)
                wait(act, z_made, b)
                nc.scalar.activation(rstd[:, :], moments[:, 3, :], ACT.Sqrt, bias=s.eps[0:KP, 0:1], scale=1.0 / D)\
                    .then_inc(std_made, 1)

            def normalize(b, u):
                act.wait_ge(rstd_made, b * 2 + 2)
                wait(act, sums_made, b - 1)
                for t in range(KT):
                    ins = nc.scalar.activation(z[u][:, t, :], raw[u][:, t, :], ACT.Identity, bias=mean_rstd[:, t:t + 1],
                                               scale=rstd[:, t:t + 1])
                ins.then_inc(z_made, 1)

            def take_context(b, u):
                wait(act, raw_made, b * T - T)
                for g in range(NG):
                    act.wait_ge(turned, b * NG + g + 1)
                    nc.scalar.activation(xnT[u][:, g * 4 * KP:(g + 1) * 4 * KP], s.ps[:, g % 2, 0:4 * KP], ACT.Identity,
                                         bias=affine[:, 1:2], scale=affine[:, 0:1]).then_inc(xnT_made, 1)

            def square(b, t):
                act.wait_ge(k_made, b * T + t + 1)
                wait(act, reduced, b * T + t - 1)
                nc.scalar.activation(squares[0:rows(t), t % 2, :], s.ps[0:rows(t), t % 2, 0:HID], ACT.Square)\
                    .then_inc(squared, 1)

            def take_queries(b):
                act.wait_ge(G_made, b + 1)
                wait(act, raw_made, b * T)
                nc.scalar.activation(G[:, :], s.ps[:, 4, 0:HQ3], ACT.Copy).then_inc(G_taken, 1)

            def root(b):
                act.wait_ge(reduced, b * T + T)
                nc.scalar.activation(inv_norms[:, :, :], norms[:, :, :], ACT.Sqrt).then_inc(root_made, 1)

            def take_shift(b):
                act.wait_ge(spread_made, b + 1)
                nc.scalar.activation(shift[:, :], s.ps[0:KP, 5, 0:HQ3], ACT.Copy).then_inc(shift_made, 1)

            def exp(b, t):
                act.wait_ge(shifted, b * T + t + 1)
                nc.scalar.activation(S[0:rows(t), t, :], S[0:rows(t), t, :], ACT.Exp).then_inc(exps_made, 1)

            def take_latents_sum(b):
                act.wait_ge(sums_made, b + 1)
                wait(act, mixed_made, b)
                nc.scalar.activation(mixed_lat[:, :], s.ps[:, 7, 0:HQ3], ACT.Copy).then_inc(lat_mixed, 1)

            def first():
                std(0)
                normalize(0, 0)
                std(1)
                normalize(1, 1)
                take_context(0, 0)
                for t in range(T):
                    square(0, t)
                take_queries(0)
                root(0)
                take_context(1, 1)

            def step(b, u, i, more):
                take_shift(b)
                for t in range(T):
                    square(b + 1, t)
                    exp(b, t)
                take_queries(b + 1)
                if more:
                    std(b + 2)
                root(b + 1)
                take_latents_sum(b)
                if more:
                    normalize(b + 2, u)
                    take_context(b + 2, u)

            def last(b, u, i):
                take_shift(b)
                for t in range(T):
                    exp(b, t)
                take_latents_sum(b)
            staged(act, first, step, last)

        @block.vector
        def _(dve):
            def take_stats(b, u, t, count):
                if t == 0:
                    dve.wait_ge(loaded[u], count)
                nc.vector.bn_stats(stats[:, t, :], raw[u][:, t, :]).then_inc(stats_made, 1)

            def moments_of(b):
                dve.wait_ge(stats_made, b * (KT + NM) + KT)
                wait(dve, z_made, b)
                nc.vector.tensor_tensor(moments[:, 0, :], stats[:, :, 1], stats[:, :, 4], ALU.add).then_inc(stats_made, 1)
                nc.vector.tensor_tensor(moments[:, 1, :], stats[:, :, 1], stats[:, :, 4], ALU.subtract).then_inc(stats_made, 1)
                nc.vector.tensor_tensor(moments[:, 2, :], stats[:, :, 2], stats[:, :, 5], ALU.add).then_inc(stats_made, 1)
                dve.wait_ge(stats_made, b * (KT + NM) + KT + 3)
                nc.vector.tensor_scalar(moments[:, 0, :], moments[:, 0, :], 0.5, None, ALU.mult).then_inc(mean_made, 1)
                nc.vector.tensor_tensor(moments[:, 1, :], moments[:, 1, :], moments[:, 1, :], ALU.mult).then_inc(mean_made, 1)
                dve.wait_ge(mean_made, b * 2 + 2)
                nc.vector.scalar_tensor_tensor(moments[:, 3, :], moments[:, 1, :], D / 4.0, moments[:, 2, :], ALU.mult,
                                               ALU.add).then_inc(stats_made, 1)

            def invert_std(b):
                dve.wait_ge(std_made, b + 1)
                nc.vector.reciprocal(rstd[:, :], rstd[:, :]).then_inc(rstd_made, 1)
                dve.wait_ge(rstd_made, b * 2 + 1)
                nc.vector.scalar_tensor_tensor(mean_rstd[:, :], moments[:, 0, :], -1.0, rstd[:, :], ALU.mult, ALU.mult)\
                    .then_inc(rstd_made, 1)

            def take_negs(b, u):
                wait(dve, S_made, b * T - T)
                nc.vector.tensor_copy(neg[u][:, :], neg_cols[:, bass.ds(b, 1), :].rearrange("p a t -> p (a t)"))\
                    .then_inc(negs_made, 1)

            def reduce_squares(b, t):
                if t == 0:
                    wait(dve, root_made, b)
                r = rows(t)
                dve.wait_ge(squared, b * T + t + 1)
                nc.vector.tensor_reduce(norms[0:r, t, :], squares[0:r, t % 2, :].rearrange("p (h d) -> p h d", h=H8),
                                        AX.X, ALU.add).then_inc(reduced, 1)

            def invert_norms(b):
                dve.wait_ge(root_made, b + 1)
                nc.vector.tensor_scalar(inv_norms[:, :, :], inv_norms[:, :, :], L2_EPS, None, ALU.max).then_inc(inv_made, 1)
                dve.wait_ge(inv_made, b * 2 + 1)
                nc.vector.reciprocal(inv_norms[:, :, :], inv_norms[:, :, :]).then_inc(inv_made, 1)
                dve.wait_ge(inv_made, b * 2 + 2)

            def scale_scores(b, u, t):
                r = rows(t)
                dve.wait_ge(raw_made, b * T + t + 1)
                if t == 0:
                    dve.wait_ge(negs_made, b + 1)
                heads_of = (S[0:r, t, :].rearrange("p (h q) -> p h q", h=H8),
                            s.ps[0:r, 2 + t % 2, 0:HQ3].rearrange("p (h q) -> p h q", h=H8))
                factors = bcast(inv_norms[0:r, t, :], SQ, 2)
                if t < KT:
                    ins = nc.vector.scalar_tensor_tensor(*heads_of, neg[u][:, t:t + 1], factors, ALU.add, ALU.mult)
                else:
                    ins = nc.vector.tensor_tensor(*heads_of, factors, ALU.mult)
                ins.then_inc(S_made, 1)

            def raise_top(b, t):
                r = rows(t)
                dve.wait_ge(S_made, b * T + t + 1)
                wait(dve, topped, b * KT + t - 1)
                nc.vector.tensor_tensor(top[0:r, :], S[0:r, 0, :] if t == 1 else top[0:r, :], S[0:r, t, :], ALU.max)\
                    .then_inc(topped, 1)

            def scores(b, u, between):
                for t in range(T):
                    scale_scores(b, u, t)
                    if t >= 2:
                        raise_top(b, t - 1)
                    if t in between:
                        between[t]()
                raise_top(b, KT)

            def maxima(b):
                dve.wait_ge(top_turned, b + 1)
                nc.vector.tensor_reduce(neg_max[:, :], s.ps[0:2 * SQ, 4, 0:NP * KP].rearrange("p (j k) -> p j k", j=NP),
                                        AX.X, ALU.max, negate=True).then_inc(maxed, 1)
                dve.wait_ge(maxed, b + 1)
                nc.vector.tensor_tensor(diag[:, :, :], bcast(s.ident[0:2 * SQ, 0:2 * SQ], NP, 1),
                                        bcast(neg_max[:, :], 2 * SQ, 2), ALU.mult).then_inc(diag_made, 1)

            def sum_probs(b, g):
                dve.wait_ge(exps_made, b * T + 4 * g + 4)
                nc.vector.tensor_reduce(prob_sum[:, g, :], S[:, 4 * g:4 * g + 4, :].rearrange("p t c -> p c t"), AX.X,
                                        ALU.add).then_inc(summed, 1)

            def center_latents(b, u):
                dve.wait_ge(lat_turned, b + 1)
                wait(dve, sums_made, b - 1)
                nc.vector.tensor_tensor(lat_N[u][:, :], s.ps[0:SQ, NG % 2, 0:D], bx_rows[:, :], ALU.subtract)\
                    .then_inc(lat_made, 1)

            def mix(b):
                dve.wait_ge(sums_made, b + 1)
                nc.vector.reciprocal(inv[:, :], s.ps[:, 5, 0:NP * SQ]).then_inc(inv_sums, 1)
                dve.wait_ge(lat_mixed, b + 1)
                nc.vector.scalar_tensor_tensor(mixed[:, :], s.ps[:, 6, 0:HQ3], affine[:, 0:1], mixed_lat[:, :],
                                               ALU.mult, ALU.add).then_inc(mixed_made, 1)

            def take_heads(b):
                dve.wait_ge(inv_sums, b + 1)
                dve.wait_ge(heads_made, b + 1)
                nc.vector.tensor_tensor(heads[:, :, :].rearrange("p j q -> p (j q)"), s.ps[:, 5, 256:256 + NP * SQ],
                                        inv[:, :], ALU.mult).then_inc(heads_taken, 1)

            def take_output(b):
                dve.wait_ge(y_made, b + 1)
                nc.vector.tensor_scalar(latents[:, batch_of(b)], s.ps[:, 4, 0:SQ], out_bias[:, 0:1], None, ALU.add)\
                    .then_inc(y_taken, 1)

            def first():
                nc.vector.memset(norms[:, :, :], 1.0).then_inc(init, 1)
                dve.wait_ge(init, 1)
                for t in range(KT):
                    take_stats(0, 0, t, 16)
                moments_of(0)
                invert_std(0)
                take_negs(0, 0)
                take_negs(1, 1)
                for t in range(KT):
                    take_stats(1, 1, t, 16)
                moments_of(1)
                invert_std(1)
                center_latents(0, 0)
                for t in range(T):
                    reduce_squares(0, t)
                invert_norms(0)
                scores(0, 0, {})
                center_latents(1, 1)

            def step(b, u, i, more):
                maxima(b)
                for t in range(T):
                    reduce_squares(b + 1, t)
                    if more and t < KT:
                        take_stats(b + 2, u, t, i * 16 + 32)
                    if t % 4 == 2 and t > 4:
                        sum_probs(b, t // 4 - 1)
                if more:
                    moments_of(b + 2)
                sum_probs(b, NG - 1)
                invert_norms(b + 1)
                if more:
                    take_negs(b + 2, u)
                    invert_std(b + 2)
                mix(b)
                scores(b + 1, 1 - u, {3: lambda: take_heads(b), 9: lambda: take_output(b)})
                if more:
                    center_latents(b + 2, u)

            def last(b, u, i):
                maxima(b)
                for g in range(NG):
                    sum_probs(b, g)
                mix(b)
                take_heads(b)
                take_output(b)
            staged(dve, first, step, last)

        batches.close()
        layer_norm(nc, s, "l3o", latents, s.xn, affine[:, 4:5], affine[:, 5:6], add_to=s.x_T)


def build(nc, a, out_T):
    with ExitStack() as ctx:
        def sb(name, shape, dt=F32):
            return ctx.enter_context(nc.sbuf_tensor(name, shape, dt))

        def sem(name):
            return ctx.enter_context(nc.semaphore(name))

        s = Shared()
        s.ps = ctx.enter_context(nc.psum_tensor("ps", [D, 8, 512], F32))
        s.x_T, s.xn, s.ident, s.ones = sb("x_T", [D, TOK]), sb("xn", [D, TOK]), sb("ident", [D, D]), sb("ones", [D, D])
        s.average, s.eps = sb("average", [D, D]), sb("eps", [D, 1])
        s.w1, s.w2 = sb("moe_w1", [D, E * HID]), sb("moe_w2", [D, E * HT * D])
        s.means_made, s.centred, s.squared, s.vars_made, s.std_made, s.inverted, s.scaled = (
            sem(n) for n in ("means_made", "centred", "squared", "vars_made", "std_made", "inverted", "scaled"))
        s.product_made, s.product_taken, s.loaded, s.x_loaded, s.zeroed, s.consts_made = (
            sem(n) for n in ("product_made", "product_taken", "loaded", "x_loaded", "zeroed", "consts_made"))
        moe_loaded = {"L0": sem("L0_moe_loaded"), "L1": sem("L1_moe_loaded")}
        stored = sem("stored")

        def norm(name):
            layer_norm(nc, s, name, s.x_T, s.xn)

        setup(nc, s, a)
        start_moe_loads(nc, s, a, "L0", moe_loaded["L0"])
        stages = [
            lambda: attention_one_head(nc, s, a),
            lambda: mixture(nc, s, a, "L0", moe_loaded["L0"], top2=False),
            lambda: (start_moe_loads(nc, s, a, "L1", moe_loaded["L1"]),
                     attention_16_heads(nc, s, a, "L1", masked=True, biased=True)),
            lambda: mixture(nc, s, a, "L1", moe_loaded["L1"], top2=True),
            lambda: attention_16_heads(nc, s, a, "L2", masked=False, biased=False),
            lambda: quantized(nc, s, a),
            lambda: attention_latents(nc, s, a),
            lambda: routed(nc, s, a),
        ]
        for n, stage in enumerate(stages):
            norm(f"norm{n}")
            stage()

        with nc.Block() as block:
            @block.sync
            def _(sp):
                sp.dma_start(out_T, s.x_T[:, :]).then_inc(stored, 16)
                sp.wait_ge(stored, 16)


def _layouts(i, np):
    def by_tile(m):
        m = m.reshape((B, KP, KT) + m.shape[2:])
        return np.ascontiguousarray(np.moveaxis(m, (2, 1), (-2, -1))).reshape((B,) + m.shape[3:] + (SK,))

    a = {"x_T": i["x"].reshape(TOK, D).T, "ctx_N": i["ctx_1024"], "ctx_T": by_tile(i["ctx_1024"]),
         "mask_T": by_tile(i["mask_BxS2_ik0"]), "mask_N": i["mask_BxS2_ik0"],
         "mask_B": i["mask_BxS2_bk0"],
         "L0_WqT": i["L0_xattn_Wq"].T, "L0_Wk": i["L0_xattn_Wk"], "L0_bq": i["L0_xattn_bq"][:, None],
         "L0_bk": i["L0_xattn_bk"][:, None]}
    for n in ("Wq", "Wk", "Wv", "Wo"):
        a[f"L1_{n}T"] = i[f"L1_xattn_{n}"].T
        a[f"L2_{n}T"] = i[f"L2_xattn_w_{n[1]}"].T
        a[f"L1_b{n[1]}"] = i[f"L1_xattn_b{n[1]}"][:, None]
    for n in ("L1_WoT", "L2_WoT", "L1_bv"):
        a[n] = a[n].reshape(4, 4, DK, -1).transpose(1, 2, 0, 3)
    a["L1_bv"] = a["L1_bv"].reshape(4, DK, 4)
    a["L0_gate_w"] = i["L0_ffn_gate_w"].T
    a["L1_gate_w"] = i["L1_ffn_gate_w"]
    a["L0_w1"] = i["L0_ffn_w1"].transpose(2, 0, 1).reshape(D, E * HID)
    a["L0_w2"] = i["L0_ffn_w2"].reshape(E, D, HT, D).transpose(3, 0, 2, 1).reshape(D, E * HT * D)
    a["L1_w1"] = i["L1_ffn_w1"].transpose(1, 0, 2).reshape(D, E * HID)
    a["L1_w2"] = i["L1_ffn_w2"].reshape(E, HT, D, D).transpose(2, 0, 1, 3).reshape(D, E * HT * D)
    for n in ("L0", "L1"):
        a[f"{n}_gate_b"] = i[f"{n}_ffn_gate_b"][None, :]
        a[f"{n}_b1"] = i[f"{n}_ffn_b1"].reshape(E * HT, D).T
        a[f"{n}_b2"] = i[f"{n}_ffn_b2"]
    a["L2_w1"] = i["L2_ffn_w1"]
    a["L2_w2"] = i["L2_ffn_w2"].reshape(HT, D, D).transpose(1, 0, 2).reshape(D, HT * D)
    a["L2_b1"] = i["L2_ffn_b1"].reshape(HT, D).T
    a["L2_b2"] = i["L2_ffn_b2"][:, None]
    for n in ("ln_x_w", "ln_x_b", "ln_l_w", "ln_l_b", "ln_o_w", "ln_o_b", "q_scale", "k_scale"):
        a[f"L3_{n}"] = i[f"L3_xattn_{n}"][:, None]
    a["L3_bx_row"] = i["L3_xattn_ln_x_b"][None, :]
    a["L3_Wq"] = i["L3_xattn_Wq"]
    a["L3_Wk"] = i["L3_xattn_Wkv"][:, :HID]
    a["L3_Wv"] = i["L3_xattn_Wkv"][:, HID:]
    a["L3_WkT"] = i["L3_xattn_Wkv"][:, :HID].T.reshape(HT, D, D).transpose(1, 0, 2)
    a["L3_Wo"] = i["L3_xattn_Wo"].reshape(HT, D, D).transpose(1, 0, 2)
    a["L3_gate_w"] = i["L3_ffn_gate_w"].T
    a["L3_w1"] = i["L3_ffn_w1"].transpose(1, 0, 2)
    a["L3_sw1"] = i["L3_ffn_sw1"]
    a["L3_w2"] = i["L3_ffn_w2"].reshape(2 * HT, D, D).transpose(1, 0, 2)
    a["L3_sw2"] = i["L3_ffn_sw2"].reshape(HT, D, D).transpose(1, 0, 2)
    a["L3_b1"] = i["L3_ffn_b1"].reshape(2 * HT, D).T
    a["L3_sb1"] = i["L3_ffn_sb1"].reshape(HT, D).T
    a["L3_b2"] = i["L3_ffn_b2"].T
    a["L3_sb2"] = i["L3_ffn_sb2"][:, None]
    return {k: np.ascontiguousarray(v) for k, v in a.items()}


def kernel(**inputs):
    import numpy as np
    import concourse.bacc as bacc
    from concourse.bass_utils import run_bass_kernel_spmd

    arrays = _layouts({k: np.asarray(v) for k, v in inputs.items()}, np)
    nc = bacc.Bacc("TRN2", target_bir_lowering=False, num_devices=1)
    a = {k: nc.dram_tensor(f"in_{k}", v.shape, mybir.dt.from_np(v.dtype), kind="ExternalInput").ap()
         for k, v in arrays.items()}
    out_T = nc.dram_tensor("out_T", [D, TOK], F32, kind="ExternalOutput").ap()
    build(nc, a, out_T)
    r = run_bass_kernel_spmd(nc, [{f"in_{k}": v for k, v in arrays.items()}], core_ids=[0])
    return np.ascontiguousarray(r.results[0]["out_T"].T).reshape(B, SQ, D)
```

```python
from contextlib import ExitStack

import concourse.bass as bass
from concourse import mybir

F32 = mybir.dt.float32
F32R = mybir.dt.float32r
I32 = mybir.dt.int32
ALU = mybir.AluOpType
ACT = mybir.ActivationFunctionType
AX = mybir.AxisListType

B, SQ, D = 32, 56, 128
SK = 1500
KT = 12
KP = SK // KT
TOK = B * SQ
NCH = 4
CH = TOK // NCH
NKC = 3
KC = SK // NKC
E, HID = 8, 512
HT = HID // D
TT = TOK // D
H16, DK = 16, 8
NG, HG = 2, 8
GF = HG * DK
GC = HG * SQ
HQ = H16 * SQ
RW = 2 * SQ
RT = HQ // RW
H8, DH = 8, 64
HQ3 = H8 * SQ
LN_EPS, L2_EPS = 1e-5, 1e-12
MAGIC = 12582912.0
MASKED = -1e9
NEVER = -1e30


class Shared:
    norms = scaled_steps = products = loads = 0


def bcast(ap, n, at):
    shape = list(ap.shape)
    return ap.unsqueeze(at).broadcast_to(shape[:at] + [n] + shape[at:])


def one_ahead(eng, first, step, last):
    first(0, 0, 0)
    step(0, 0, 0)
    step(1, 1, 0)
    with eng.Fori(1, B // 2 - 1) as j:
        step(j * 2, 0, j)
        step(j * 2 + 1, 1, j)
    step(B - 2, 0, B // 2 - 1)
    last(B - 1, 1, B // 2 - 1)


def following(u, i):
    return (1 - u, i) if u == 0 else (0, i + 1)


def nothing(b, u, i):
    pass


def wait(eng, sem, value):
    if not isinstance(value, int) or value > 0:
        eng.wait_ge(sem, value)


def plain(eng, s):
    eng.wait_ge(s.x_loaded, 16)


def start_at_one(nc, sems):
    with nc.Block() as block:
        @block.sync
        def _(sp):
            for sem in sems:
                sp.sem_inc(sem, 1)


def clear(nc, sems):
    with nc.Block() as block:
        @block.gpsimd
        def _(pool):
            for sem in sems:
                pool.sem_clear(sem)


def batch_of(b):
    return bass.ds(b * SQ, SQ)


def setup(nc, s, a):
    zeroed, consts_made = s.zeroed, s.consts_made
    with nc.Block() as block:
        @block.sync
        def _(sp):
            sp.dma_start(s.x_T[:, :], a["x_T"]).then_inc(s.x_loaded, 16)
            sp.wait_ge(s.x_loaded, 16)

        @block.gpsimd
        def _(pool):
            nc.gpsimd.memset(s.ident[:, :], 0.0).then_inc(zeroed, 1)
            pool.wait_ge(zeroed, 1)
            nc.gpsimd.affine_select(out=s.ident[:, :], in_=s.ident[:, :], compare_op=ALU.not_equal, fill=1.0,
                                    base=0, pattern=[[-1, D]], channel_multiplier=1).then_inc(consts_made, 1)

        @block.vector
        def _(dve):
            nc.vector.memset(s.ones[:, :], 1.0).then_inc(consts_made, 1)
            nc.vector.memset(s.average[:, :], 1.0 / D).then_inc(consts_made, 1)
            nc.vector.memset(s.eps[:, :], LN_EPS).then_inc(consts_made, 1)


def layer_norm(nc, s, name, src, dst, weight=None, bias=None, add_to=None):
    calls, n0, scaled0 = s.norms, s.norms * NCH, s.scaled_steps
    steps = 1 + (weight is not None) + (add_to is not None)
    s.norms += 1
    s.scaled_steps += steps * NCH
    tiles = [list(range(4 * c, min(4 * c + 4, TT))) for c in range(NCH)]

    def cols(t, c):
        return t[:, tiles[c][0] * D:(tiles[c][-1] + 1) * D]

    with ExitStack() as ctx:
        squares = ctx.enter_context(nc.sbuf_tensor(f"{name}_squares", [D, TOK], F32))
        rstd = ctx.enter_context(nc.sbuf_tensor(f"{name}_rstd", [D, TT], F32))
        block = ctx.enter_context(nc.Block())

        def bank(c):
            return s.ps[:, c, 0:len(tiles[c]) * D]

        @block.tensor
        def _(pe):
            for c in range(NCH):
                nc.tensor.matmul(bank(c), s.average[:, :], cols(src, c), start=True, stop=True)\
                    .then_inc(s.means_made, 1)
            for c in range(NCH):
                pe.wait_ge(s.squared, n0 + c + 1)
                for t in tiles[c]:
                    mm = nc.tensor.matmul(s.ps[:, NCH, t:t + 1], squares[:, t * D:(t + 1) * D], s.average[:, 0:1],
                                          start=True, stop=True, skip_group_check=True)
            mm.then_inc(s.vars_made, 1)
            pe.wait_ge(s.inverted, calls + 1)
            for c in range(NCH):
                for k, t in enumerate(tiles[c]):
                    mm = nc.tensor.matmul(s.ps[:, c, k * D:(k + 1) * D], rstd[:, t:t + 1].broadcast_to([D, D]),
                                          s.ident[:, :], start=True, stop=True, skip_group_check=True)
                mm.then_inc(s.spread_made, 1)

        @block.scalar
        def _(act):
            for c in range(NCH):
                act.wait_ge(s.centred, n0 + c + 1)
                nc.scalar.activation(cols(squares, c), cols(dst, c), ACT.Square).then_inc(s.squared, 1)
            act.wait_ge(s.vars_made, calls + 1)
            nc.scalar.activation(rstd[:, :], s.ps[:, NCH, 0:TT], ACT.Sqrt, bias=s.eps[:, 0:1]).then_inc(s.std_made, 1)

        @block.vector
        def _(dve):
            for c in range(NCH):
                dve.wait_ge(s.means_made, n0 + c + 1)
                nc.vector.tensor_tensor(cols(dst, c), cols(src, c), bank(c), ALU.subtract).then_inc(s.centred, 1)
            dve.wait_ge(s.std_made, calls + 1)
            nc.vector.reciprocal(rstd[:, :], rstd[:, :]).then_inc(s.inverted, 1)
            for c in range(NCH):
                dve.wait_ge(s.spread_made, n0 + c + 1)
                nc.vector.tensor_tensor(cols(dst, c), cols(dst, c), bank(c), ALU.mult).then_inc(s.scaled, 1)
                if weight is not None:
                    dve.wait_ge(s.scaled, scaled0 + c * steps + 1)
                    nc.vector.tensor_scalar(cols(dst, c), cols(dst, c), weight, bias, ALU.mult, ALU.add)\
                        .then_inc(s.scaled, 1)
                if add_to is not None:
                    dve.wait_ge(s.scaled, scaled0 + c * steps + 2)
                    nc.vector.tensor_tensor(cols(add_to, c), cols(add_to, c), cols(dst, c), ALU.add)\
                        .then_inc(s.scaled, 1)


def project(nc, s, pairs):
    n0 = s.products
    s.products += len(pairs) * NCH
    with nc.Block() as block:
        @block.tensor
        def _(pe):
            n = 0
            for i, (dst, w, src, bias, scale) in enumerate(pairs):
                if i:
                    pe.wait_ge(s.product_taken, n0 + n)
                for c in range(NCH):
                    nc.tensor.matmul(s.ps[0:w.shape[1], n % 8, 0:CH], w, src[:, c * CH:(c + 1) * CH],
                                     start=True, stop=True).then_inc(s.product_made, 1)
                    n += 1

        @block.vector
        def _(dve):
            n = 0
            for dst, w, src, bias, scale in pairs:
                for c in range(NCH):
                    dve.wait_ge(s.product_made, n0 + n + 1)
                    nc.vector.tensor_scalar(dst[:, c * CH:(c + 1) * CH], s.ps[0:w.shape[1], n % 8, 0:CH],
                                            0.0 if bias is None else bias, scale, ALU.add, ALU.mult)\
                        .then_inc(s.product_taken, 1)
                    n += 1


def load(nc, s, pairs):
    s.loads += len(pairs)
    with nc.Block() as block:
        @block.sync
        def _(sp):
            for dst, src in pairs:
                sp.dma_start(dst, src).then_inc(s.loaded, 16)
            sp.wait_ge(s.loaded, 16 * s.loads)


def attention_one_head(nc, s, a):
    with ExitStack() as ctx:
        def sb(name, shape, dt=F32):
            return ctx.enter_context(nc.sbuf_tensor(f"a0_{name}", shape, dt))

        sems = []

        def sem(name):
            sems.append(ctx.enter_context(nc.semaphore(f"a0_{name}")))
            return sems[-1]

        wq, wk, bias = sb("wq", [D, D]), sb("wk", [D, D]), sb("bias", [D, 2])
        q, qk, qbk = sb("q", [D, TOK]), sb("qk", [D, TOK]), sb("qbk", [1, TOK])
        q_b = [sb(f"q_b{u}", [D, SQ]) for u in range(2)]
        q_r = [sb(f"q_r{u}", [D, SQ], F32R) for u in range(2)]
        ctx_N = [sb(f"ctx_N{u}", [KP, KT, D]) for u in range(2)]
        ctx_T = [sb(f"ctx_T{u}", [D, KT, KP]) for u in range(2)]
        ctx_R = [sb(f"ctx_R{u}", [D, SK], F32R) for u in range(2)]
        max_col = sb("max_col", [SQ, 2])
        shift = sb("shift", [1, 2, SQ])
        probs = [sb(f"probs{u}", [KP, KT, SQ]) for u in range(2)]
        prob_sum = sb("prob_sum", [KP, 2, SQ])
        raised = sb("raised", [1, SQ])
        inv, delta = sb("inv", [D, SQ]), sb("delta", [D, SQ])

        load(nc, s, [(wq[:, :], a["L0_WqT"]), (wk[:, :], a["L0_Wk"]), (bias[:, 0:1], a["L0_bq"]),
                           (bias[:, 1:2], a["L0_bk"])])
        project(nc, s, [(q, wq[:, :], s.xn, bias[:, 0:1], 1.0 / 32), (qk, wk[:, :], q, None, 1.0),
                               (qbk, bias[:, 1:2], q, None, 1.0)])

        T_loaded = [sem("even_T_loaded"), sem("odd_T_loaded")]
        N_loaded = [sem("even_N_loaded"), sem("odd_N_loaded")]
        q_taken, rounded, rows_made, max_made, max_turned, shift_made = (
            sem(n) for n in ("q_taken", "rounded", "rows_made", "max_made", "max_turned", "shift_made"))
        scores_made, probs_made, summed, out_made, max_raised, inverted, scaled, added = (
            sem(n) for n in ("scores_made", "probs_made", "summed", "out_made", "max_raised", "inverted", "scaled", "added"))
        HALF = KT // 2
        batches = ExitStack()
        block = batches.enter_context(nc.Block())

        @block.sync
        def _(sp):
            def fetch(b, u):
                wait(sp, scores_made, b - 1)
                sp.dma_start(ctx_T[u][:, :, :], a["ctx_T"][bass.ds(b, 1)].rearrange("a d (t p) -> (a d) t p", t=KT))\
                    .then_inc(T_loaded[u], 16)
                wait(sp, out_made, b - 1)
                sp.dma_start(ctx_N[u][:, :, :], a["ctx_N"][bass.ds(b, 1)].rearrange("a (p t) d -> (a p) t d", t=KT))\
                    .then_inc(N_loaded[u], 16)
            fetch(0, 0)
            fetch(1, 1)
            with sp.Fori(1, B // 2) as j:
                fetch(j * 2, 0)
                fetch(j * 2 + 1, 1)

        @block.gpsimd
        def _(pool):
            def take_queries(b, u, i):
                wait(pool, scores_made, b - 1)
                nc.gpsimd.tensor_copy(q_b[u][:, :], qk[:, batch_of(b)]).then_inc(q_taken, 1)
                nc.gpsimd.tensor_copy(q_r[u][:, :], qk[:, batch_of(b)]).then_inc(q_taken, 1)

            def step(b, u, i):
                take_queries(b + 1, *following(u, i))
            one_ahead(pool, take_queries, step, nothing)

        @block.tensor
        def _(pe):
            def score_rows(b, u):
                pe.wait_ge(rounded, b + 1)
                pe.wait_ge(q_taken, b * 2 + 2)
                wait(pe, shift_made, b)
                for k in range(NKC):
                    mm = nc.tensor.matmul(s.ps[0:SQ, k, 0:KC], q_r[u][:, :], ctx_R[u][:, k * KC:(k + 1) * KC],
                                          start=True, stop=True)
                mm.then_inc(rows_made, 1)

            def turn_maxima(b, u):
                plain(pe, s)
                pe.wait_ge(max_made, b + 1)
                pe.wait_ge(rows_made, b + 1)
                nc.tensor.transpose(s.ps[0:1, 0, 0:SQ], max_col[:, u:u + 1], s.ident[0:SQ, 0:SQ])\
                    .then_inc(max_turned, 1)

            def scores(b, u):
                wait(pe, probs_made, b - 1)
                for h in range(2):
                    for t in range(HALF):
                        nc.tensor.matmul(s.ps[0:KP, 3 + 2 * u + h, t * SQ:(t + 1) * SQ], ctx_T[u][:, h * HALF + t, :],
                                         q_b[u][:, :], start=(t == 0), stop=False, skip_group_check=True)
                pe.wait_ge(shift_made, b + 1)
                for h in range(2):
                    mm = nc.tensor.matmul(s.ps[0:KP, 3 + 2 * u + h, 0:HALF * SQ], s.ones[0:1, 0:KP],
                                          bcast(shift[:, u, :], HALF, 1), start=False, stop=True,
                                          skip_group_check=True)
                mm.then_inc(scores_made, 1)

            def outputs(b, u, i):
                pe.wait_ge(N_loaded[u], i * 16 + 16)
                pe.wait_ge(probs_made, b + 1)
                wait(pe, scaled, b)
                for t in range(KT):
                    nc.tensor.matmul(s.ps[:, 7, 64:64 + SQ], ctx_N[u][:, t, :], probs[u][:, t, :],
                                     start=(t == 0), stop=False, skip_group_check=True)
                pe.wait_ge(summed, b + 1)
                nc.tensor.matmul(s.ps[:, 7, 128:128 + SQ], s.ones[0:KP, :], prob_sum[:, u, :],
                                 start=False, stop=True, skip_group_check=True).then_inc(out_made, 1)

            def first(b, u, i):
                score_rows(b, u)
                turn_maxima(b, u)

            def step(b, u, i):
                scores(b, u)
                score_rows(b + 1, 1 - u)
                if not (isinstance(b, int) and b == 0):
                    outputs(b - 1, 1 - u, i - 1 if u == 0 else i)
                turn_maxima(b + 1, 1 - u)

            def last(b, u, i):
                scores(b, u)
                outputs(b - 1, 1 - u, i)
                outputs(b, u, i)
            one_ahead(pe, first, step, last)

        @block.scalar
        def _(act):
            def exps(b, u, i):
                act.wait_ge(scores_made, b + 1)
                wait(act, out_made, b - 1)
                wait(act, summed, b - 1)
                nc.scalar.activation(probs[u][:, :, :].rearrange("p (h t) q -> p h (t q)", h=2),
                                     s.ps[0:KP, 3 + 2 * u:5 + 2 * u, 0:HALF * SQ], ACT.Exp).then_inc(probs_made, 1)
            one_ahead(act, nothing, exps, exps)

        @block.vector
        def _(dve):
            def round_keys(b, u, i):
                dve.wait_ge(T_loaded[u], i * 16 + 16)
                wait(dve, rows_made, b - 1)
                nc.vector.tensor_copy(ctx_R[u][:, :].rearrange("d (t p) -> d t p", t=KT), ctx_T[u][:, :, :])\
                    .then_inc(rounded, 1)

            def maxima(b, u):
                dve.wait_ge(rows_made, b + 1)
                wait(dve, max_turned, b - 1)
                nc.vector.tensor_reduce(max_col[:, u:u + 1], s.ps[0:SQ, 0:NKC, 0:KC], AX.XY, ALU.max)\
                    .then_inc(max_made, 1)

            def shifts(b, u):
                dve.wait_ge(max_turned, b + 1)
                wait(dve, scores_made, b - 1)
                nc.vector.tensor_tensor(raised[:, :], s.ps[0:1, 0, 0:SQ], qbk[0:1, batch_of(b)], ALU.add)\
                    .then_inc(max_raised, 1)
                dve.wait_ge(max_raised, b + 1)
                nc.vector.tensor_tensor(shift[:, u, :], qbk[0:1, batch_of(b)], raised[:, :], ALU.subtract)\
                    .then_inc(shift_made, 1)

            def sums(b, u):
                dve.wait_ge(probs_made, b + 1)
                wait(dve, out_made, b - 1)
                nc.vector.tensor_reduce(prob_sum[:, u, :], probs[u][:, :, :].rearrange("p t q -> p q t"), AX.X,
                                        ALU.add).then_inc(summed, 1)

            def outputs(b):
                dve.wait_ge(out_made, b + 1)
                nc.vector.reciprocal(inv[:, :], s.ps[:, 7, 128:128 + SQ]).then_inc(inverted, 1)
                dve.wait_ge(inverted, b + 1)
                wait(dve, added, b)
                nc.vector.tensor_tensor(delta[:, :], s.ps[:, 7, 64:64 + SQ], inv[:, :], ALU.mult).then_inc(scaled, 1)
                dve.wait_ge(scaled, b + 1)
                nc.vector.tensor_tensor(s.x_T[:, batch_of(b)], s.x_T[:, batch_of(b)], delta[:, :], ALU.add)\
                    .then_inc(added, 1)

            def first(b, u, i):
                round_keys(b, u, i)
                maxima(b, u)
                shifts(b, u)

            def step(b, u, i):
                later = not (isinstance(b, int) and b == 0)
                round_keys(b + 1, *following(u, i))
                if later:
                    sums(b - 1, 1 - u)
                maxima(b + 1, 1 - u)
                if later:
                    outputs(b - 1)
                shifts(b + 1, 1 - u)

            def last(b, u, i):
                sums(b - 1, 1 - u)
                outputs(b - 1)
                sums(b, u)
                outputs(b)
            one_ahead(dve, first, step, last)

        batches.close()
        clear(nc, sems)


def mixture(nc, s, a, layer, norm, top2):
    with ExitStack() as ctx:
        def sb(name, shape, dt=F32):
            return ctx.enter_context(nc.sbuf_tensor(f"{layer}f_{name}", shape, dt))

        sems = []

        def sem(name):
            sems.append(ctx.enter_context(nc.semaphore(f"{layer}f_{name}")))
            return sems[-1]

        w1, w2 = sb("w1", [D, E * HID]), sb("w2", [D, E * HT * D])
        moe_loaded = sem("moe_loaded")
        with nc.Block() as block:
            @block.sync
            def _(sp):
                sp.dma_start(w1[:, :], a[f"{layer}_w1"]).then_inc(moe_loaded, 16)
                sp.dma_start(w2[:, :], a[f"{layer}_w2"]).then_inc(moe_loaded, 16)
        norm()

        gate_w, gate_b = sb("gate_w", [D, E]), sb("gate_b", [1, E])
        b1, neg_b1, b2 = sb("b1", [D, E, HT]), sb("neg_b1", [D, E, HT]), sb("b2", [E, D])
        b1_blocks = sb("b1_blocks", [D, E, HT, E])
        rank = sb("rank", [D, E])
        logits, best, eq, won, second, gates = (sb(n, [D, TT, E]) for n in
                                                ("logits", "best", "eq", "won", "second", "gates"))
        row_max, row_rank = sb("row_max", [D, TT]), sb("row_rank", [D, TT])
        weight_hi, weight_lo = sb("weight_hi", [E, TOK], F32R), sb("weight_lo", [E, TOK], F32R)
        weight_T = sb("weight_T", [E, TOK])
        pick = sb("pick", [E, E, D], F32R)
        expert_bias = sb("expert_bias", [E, D])
        spread = sb("spread", [D, 2, CH])
        hidden = sb("hidden", [D, 4, CH])

        load(nc, s, [(gate_w[:, :], a[f"{layer}_gate_w"]), (gate_b[:, :], a[f"{layer}_gate_b"]),
                                  (b1[:, :, :].rearrange("p e j -> p (e j)"), a[f"{layer}_b1"]),
                                  (b2[:, :], a[f"{layer}_b2"])])

        logits_made, gates_ready, step, exps_made, bias_made, rank_made = (
            sem(n) for n in ("logits_made", "gates_ready", "step", "exps_made", "bias_made", "rank_made"))
        with nc.Block() as block:
            @block.tensor
            def _(pe):
                for t in range(TT):
                    nc.tensor.matmul(s.ps[:, 7, t * E:(t + 1) * E], s.xn[:, t * D:(t + 1) * D], gate_w[:, :],
                                     start=(t == 0), stop=False, skip_group_check=True)
                    mm = nc.tensor.matmul(s.ps[:, 7, t * E:(t + 1) * E], s.ones[0:1, :], gate_b[:, :],
                                          start=False, stop=True, skip_group_check=True)
                mm.then_inc(logits_made, 1)
                pe.wait_ge(moe_loaded, 32)
                pe.wait_ge(bias_made, 2)
                for n in range(E * HT):
                    mm = nc.tensor.matmul(s.ps[0:E, 6, 0:D], b1_blocks[:, n // HT, n % HT, :],
                                          w2[:, n * D:(n + 1) * D], start=(n == 0), stop=(n == E * HT - 1))
                mm.then_inc(logits_made, 1)
                pe.wait_ge(gates_ready, 1)
                for t in range(TT):
                    mm = nc.tensor.transpose(s.ps[0:E, t // 4, (t % 4) * D:(t % 4 + 1) * D], gates[:, t, :], s.ident[:, :])
                mm.then_inc(logits_made, 1)

            @block.scalar
            def _(act):
                if top2:
                    act.wait_ge(exps_made, 1)
                    nc.scalar.activation(best[:, :, :], best[:, :, :], ACT.Exp).then_inc(exps_made, 1)

            @block.gpsimd
            def _(pool):
                nc.gpsimd.memset(b1_blocks[:, :, :, :], 0.0).then_inc(bias_made, 1)
                for e in range(E):
                    nc.gpsimd.memset(rank[:, e:e + 1], float(E - e)).then_inc(rank_made, 1)

            @block.vector
            def _(dve):
                count = [0]

                def chain(ins):
                    count[0] += 1
                    ins.then_inc(step, 1)
                    dve.wait_ge(step, count[0])

                dve.wait_ge(bias_made, 1)
                for e in range(E):
                    ins = nc.vector.tensor_copy(b1_blocks[:, e, :, e], b1[:, e, :])
                ins.then_inc(bias_made, 1)
                chain(nc.vector.tensor_scalar(neg_b1[:, :, :], b1[:, :, :], -1.0, None, ALU.mult))
                chain(nc.vector.tensor_copy(pick[:, :, :], bcast(s.ident[0:E, 0:E], D, 2)))
                dve.wait_ge(rank_made, E)
                dve.wait_ge(logits_made, 1)
                chain(nc.vector.tensor_copy(logits[:, :, :].rearrange("p t e -> p (t e)"), s.ps[:, 7, 0:TT * E]))

                def choose(values, chosen):
                    chain(nc.vector.tensor_reduce(row_max[:, :], values[:, :, :], AX.X, ALU.max))
                    chain(nc.vector.tensor_tensor(eq[:, :, :], values[:, :, :], bcast(row_max[:, :], E, 2), ALU.is_equal))
                    chain(nc.vector.tensor_tensor(eq[:, :, :], eq[:, :, :], bcast(rank[:, :], TT, 1), ALU.mult))
                    chain(nc.vector.tensor_reduce(row_rank[:, :], eq[:, :, :], AX.X, ALU.max))
                    chain(nc.vector.tensor_tensor(chosen[:, :, :], eq[:, :, :], bcast(row_rank[:, :], E, 2), ALU.is_equal))

                choose(logits, won)
                if top2:
                    nc.vector.tensor_tensor(best[:, :, :], logits[:, :, :], bcast(row_max[:, :], E, 2), ALU.subtract)\
                        .then_inc(exps_made, 1)
                    chain(nc.vector.scalar_tensor_tensor(logits[:, :, :], won[:, :, :], -1e38, logits[:, :, :],
                                                         ALU.mult, ALU.add))
                    dve.wait_ge(exps_made, 2)
                    choose(logits, second)
                    chain(nc.vector.tensor_tensor(won[:, :, :], won[:, :, :], second[:, :, :], ALU.add))
                    chain(nc.vector.tensor_tensor(won[:, :, :], won[:, :, :], best[:, :, :], ALU.mult))
                    chain(nc.vector.tensor_reduce(row_max[:, :], won[:, :, :], AX.X, ALU.add))
                    chain(nc.vector.reciprocal(row_max[:, :], row_max[:, :]))
                    chain(nc.vector.tensor_tensor(won[:, :, :], won[:, :, :], bcast(row_max[:, :], E, 2), ALU.mult))
                nc.vector.tensor_copy(gates[:, :, :], won[:, :, :]).then_inc(gates_ready, 1)
                dve.wait_ge(logits_made, 2)
                chain(nc.vector.tensor_tensor(expert_bias[:, :], s.ps[0:E, 6, 0:D], b2[:, :], ALU.add))
                dve.wait_ge(logits_made, 3)
                for k in range(4):
                    n = min(4, TT - 4 * k) * D
                    chain(nc.vector.tensor_copy(weight_T[:, 4 * k * D:4 * k * D + n], s.ps[0:E, k, 0:n]))
                chain(nc.vector.tensor_copy(weight_hi[:, :], weight_T[:, :]))
                chain(nc.vector.tensor_tensor(weight_lo[:, :], weight_T[:, :], weight_hi[:, :].bitcast(F32), ALU.subtract))

        hidden_made, hidden_taken, out_made, out_taken, spread_made, spread_taken = (
            sem(n) for n in ("hidden_made", "hidden_taken", "out_made", "out_taken", "spread_made", "spread_taken"))
        start_at_one(nc, [spread_taken, hidden_taken, out_taken, out_made])
        NT = E * HT
        with nc.Block() as block:
            @block.tensor
            def _(pe):
                with pe.Fori(0, NCH) as c:
                    def spread_weights(e):
                        mm = nc.tensor.matmul(s.ps[:, 5 + e % 2, 0:CH], pick[:, e, :], weight_hi[:, bass.ds(c * CH, CH)],
                                              start=True, stop=not top2)
                        if top2:
                            mm = nc.tensor.matmul(s.ps[:, 5 + e % 2, 0:CH], pick[:, e, :],
                                                  weight_lo[:, bass.ds(c * CH, CH)], start=False, stop=True)
                        mm.then_inc(spread_made, 1)

                    def first_product(n):
                        if n % HT == 0:
                            pe.wait_ge(spread_taken, 1 + c * E + max(n // HT - 1, 0))
                        if n >= 4:
                            pe.wait_ge(hidden_taken, 1 + c * NT + n - 3)
                        else:
                            pe.wait_ge(hidden_taken, 1 + c * NT)
                        nc.tensor.matmul(s.ps[:, n % 4, 0:CH], w1[:, n * D:(n + 1) * D],
                                         s.xn[:, bass.ds(c * CH, CH)], start=True, stop=True).then_inc(hidden_made, 1)

                    def second_product(n):
                        pe.wait_ge(hidden_taken, 1 + c * NT + n + 1)
                        mm = nc.tensor.matmul(s.ps[:, 4, 0:CH], w2[:, n * D:(n + 1) * D], hidden[:, n % 4, :],
                                              start=False, stop=(n == NT - 1))
                        mm.then_inc(out_made, 1)

                    pe.wait_ge(out_taken, 1 + c)
                    nc.tensor.matmul(s.ps[:, 4, 0:CH], expert_bias[:, :], weight_T[:, bass.ds(c * CH, CH)],
                                     start=True, stop=False)
                    for n in range(NT + 2):
                        if n < NT:
                            first_product(n)
                            if n % HT == 0:
                                spread_weights(n // HT)
                        if n >= 2:
                            second_product(n - 2)

            @block.scalar
            def _(act):
                with act.Fori(0, NCH) as c:
                    for e in range(E):
                        act.wait_ge(spread_made, c * E + e + 1)
                        if e >= 2:
                            act.wait_ge(hidden_taken, 1 + c * NT + (e - 1) * HT)
                        else:
                            act.wait_ge(hidden_taken, 1 + c * NT)
                        nc.scalar.activation(spread[:, e % 2, :], s.ps[:, 5 + e % 2, 0:CH], ACT.Copy)\
                            .then_inc(spread_taken, 1)

            @block.vector
            def _(dve):
                with dve.Fori(0, NCH) as c:
                    for n in range(NT):
                        e = n // HT
                        dve.wait_ge(hidden_made, c * NT + n + 1)
                        dve.wait_ge(spread_taken, 1 + c * E + e + 1)
                        if n >= 4:
                            dve.wait_ge(out_made, 1 + c * NT + n - 3)
                        else:
                            dve.wait_ge(out_made, 1 + c * NT)
                        nc.vector.scalar_tensor_tensor(hidden[:, n % 4, :], s.ps[:, n % 4, 0:CH],
                                                       neg_b1[:, e, n % HT:n % HT + 1], spread[:, e % 2, :],
                                                       ALU.max, ALU.mult).then_inc(hidden_taken, 1)
                    dve.wait_ge(out_made, 1 + c * NT + NT)
                    nc.vector.tensor_tensor(s.x_T[:, bass.ds(c * CH, CH)], s.x_T[:, bass.ds(c * CH, CH)],
                                            s.ps[:, 4, 0:CH], ALU.add).then_inc(out_taken, 1)

        clear(nc, sems)


def attention_16_heads(nc, s, a, layer, masked, biased):
    with ExitStack() as ctx:
        def sb(name, shape, dt=F32):
            return ctx.enter_context(nc.sbuf_tensor(f"{layer}a_{name}", shape, dt))

        def sem(name):
            return ctx.enter_context(nc.semaphore(f"{layer}a_{name}"))

        wq, wk = sb("wq", [D, NG, 2, GF]), sb("wk", [D, NG, 2, GF])
        wv = sb("wv", [D, D])
        wo_quad = sb("wo_quad", [D, 4, D])
        bias, bias_q, bias_k = sb("bias", [D, 1]), sb("bias_q", [D, NG]), sb("bias_k", [D, NG])
        bv_quad = sb("bv_quad", [D, 4])
        head_mask, group_mask = sb("head_mask", [D, H16]), sb("group_mask", [D, HG])
        sum_rows = sb("sum_rows", [D, 4, 32])
        q = [sb(f"q{g}", [D, TOK]) for g in range(NG)]
        q_lo = [sb(f"q_lo{g}", [GF, TOK]) for g in range(NG)]
        heads_out = sb("heads_out", [D, 4, TOK])
        ctx_T = [sb(f"ctx_T{u}", [D, KT, KP]) for u in range(2)]
        k_full = [sb(f"k_full{n}", [D, KC]) for n in range(2)]
        k_both = [[sb(f"k_both{g}{u}", [D, SK], F32R) for u in range(2)] for g in range(NG)]
        k_hi = [[sb(f"k_hi{g}{u}", [GF + 2, SK], F32R) for u in range(2)] for g in range(NG)]
        v = [sb(f"v{u}", [KP, KT, H16, DK + 1]) for u in range(2)]
        q_both = [[sb(f"q_both{g}{u}", [D, GC], F32R) for u in range(2)] for g in range(NG)]
        q_shift = [[sb(f"q_shift{g}{u}", [GF + 2, GC], F32R) for u in range(2)] for g in range(NG)]
        chunk_max = sb("chunk_max", [RW, 2, RT, NKC])
        max_col = sb("max_col", [RW, 2, RT])
        max_hi, max_lo = sb("max_hi", [RT, 2, RW], F32R), sb("max_lo", [RT, 2, RW], F32R)
        probs = [sb(f"probs{u}", [KP, HQ]) for u in range(2)]
        acc = sb("acc", [D, 4 * SQ])
        inv = sb("inv", [D, 4 * SQ])
        if masked:
            mask_i = sb("mask_i", [D, SK], I32)
            mask_n = [sb(f"mask_n{u}", [KP, KT], I32) for u in range(2)]
            neg_row, valid_row = sb("neg_row", [D, SK]), sb("valid_row", [D, SK])
            neg_col = sb("neg_col", [KP, 2, KT])
            carrier = sb("carrier", [1, RT * NKC])

        prep_loaded, zeroed, cut, prep = sem("prep_loaded"), sem("zeroed"), sem("cut"), sem("prep")
        with nc.Block() as block:
            @block.gpsimd
            def _(pool):
                nc.gpsimd.memset(wo_quad[:, :, :], 0.0).then_inc(zeroed, 1)
                nc.gpsimd.memset(bv_quad[:, :], 0.0).then_inc(zeroed, 1)
                nc.gpsimd.memset(bias[:, :], 0.0).then_inc(zeroed, 1)
                nc.gpsimd.memset(bias_q[:, :], 0.0).then_inc(zeroed, 1)
                nc.gpsimd.memset(bias_k[:, :], 0.0).then_inc(zeroed, 1)
                nc.gpsimd.memset(acc[:, :], 0.0).then_inc(zeroed, 1)
                for u in range(2):
                    nc.gpsimd.memset(v[u][:, :, :, DK:DK + 1], 1.0).then_inc(zeroed, 1)
                nc.gpsimd.memset(head_mask[:, :], 1.0).then_inc(zeroed, 1)
                pool.wait_ge(zeroed, 9)
                nc.gpsimd.affine_select(out=head_mask[:, :], in_=head_mask[:, :], compare_op=ALU.is_ge, fill=0.0,
                                        base=0, pattern=[[-DK, H16]], channel_multiplier=1).then_inc(cut, 1)
                pool.wait_ge(cut, 1)
                nc.gpsimd.affine_select(out=head_mask[:, :], in_=head_mask[:, :], compare_op=ALU.is_ge, fill=0.0,
                                        base=DK - 1, pattern=[[DK, H16]], channel_multiplier=-1).then_inc(cut, 1)

            @block.vector
            def _(dve):
                for g in range(NG):
                    for u in range(2):
                        nc.vector.tensor_copy(k_hi[g][u][GF:, :], s.ones[GF:GF + 2, 0:1].broadcast_to([2, SK]))\
                            .then_inc(prep, 1)
                dve.wait_ge(cut, 2)
                nc.vector.tensor_tensor(group_mask[:, :], head_mask[:, 0:HG], head_mask[:, HG:], ALU.add).then_inc(prep, 1)
                nc.vector.tensor_copy(sum_rows[:, :, :], bcast(s.ident[:, DK:D:32], 32, 2)).then_inc(prep, 1)

            @block.sync
            def _(sp):
                for twice in range(2):
                    for w, name in ((wq, "WqT"), (wk, "WkT")):
                        sp.dma_start(w[:, :, twice, :], a[f"{layer}_{name}"].rearrange("i (g f) -> i g f", g=NG))\
                            .then_inc(prep_loaded, 16)
                sp.dma_start(wv[:, :], a[f"{layer}_WvT"]).then_inc(prep_loaded, 16)
                sp.wait_ge(zeroed, 9)
                n = 5
                for j in range(4):
                    sp.dma_start(wo_quad[32 * j:32 * j + DK, :, :],
                                 a[f"{layer}_WoT"][j])\
                        .then_inc(prep_loaded, 16)
                    n += 1
                    if biased:
                        sp.dma_start(bv_quad[32 * j:32 * j + DK, :],
                                     a[f"{layer}_bv"][j])\
                            .then_inc(prep_loaded, 16)
                        n += 1
                if biased:
                    sp.dma_start(bias[:, :], a[f"{layer}_bo"]).then_inc(prep_loaded, 16)
                    n += 1
                    for column, name in ((bias_q, "bq"), (bias_k, "bk")):
                        for g in range(NG):
                            for twice in range(2):
                                sp.dma_start(column[twice * GF:(twice + 1) * GF, g:g + 1],
                                             a[f"{layer}_{name}"][g * GF:(g + 1) * GF]).then_inc(prep_loaded, 16)
                                n += 1
                sp.wait_ge(prep_loaded, 16 * n)

        project(nc, s, [(q[g], wq[:, g].rearrange("i r f -> i (r f)"), s.xn, bias_q[:, g:g + 1], float(DK) ** -0.5)
                        for g in range(NG)])

        loaded = [sem("even_loaded"), sem("odd_loaded")]
        (q_split, qd_made, masks_made, k_both_made, k_hi_made, k_lo_made, scratch_dve, scratch_act, k_rows,
         max_made, max_turned, max_split, row_moved, scores_made, probs_made, probs_used, acc_taken, sums_made,
         inverted, normed, products) = (
            sem(n) for n in ("q_split", "qd_made", "masks_made", "k_both_made", "k_hi_made", "k_lo_made", "scratch_dve", "scratch_act", "k_rows", "max_made", "max_turned", "max_split",
                             "row_moved", "scores_made", "probs_made", "probs_used", "acc_taken", "sums_made",
                             "inverted", "normed", "products"))
        NV = 3
        NK = NG * NKC
        ROWS = RT * NKC
        ND = NK + ROWS
        NL = 3 if masked else 1
        JT = RT // NG

        slots = [[] for t in range(KT)]
        for n in range(NK):
            slots[n].append(("keys", n))
        for n in range(ROWS):
            slots[2 + n // 3].append(("rows", n))
        for g in range(NV):
            slots[KT - 3 + (g + 1) // 2].append(("values", g))
        order = [item for slot in slots for item in slot]

        def bank(item):
            return 4 + order.index(item) % 2

        def emptied_by_dve(item):
            return len([kind for kind, n in order[:order.index(item) + 1] if kind != "values"])

        def wait_for_bank(pe, b, item):
            k = order.index(item)
            if k < 2:
                b, before = b - 1, [other for other in order if bank(other) == bank(item)][-1]
            else:
                before = order[k - 2]
            if before[0] == "values":
                wait(pe, scratch_act, b * NV + before[1] + 1)
            else:
                wait(pe, scratch_dve, b * ND + emptied_by_dve(before))

        def rows_of(n):
            m, j = n // JT, n % JT
            return (m % NG) * JT + j, m // NG, m % NG
        batches = ExitStack()
        block = batches.enter_context(nc.Block())

        @block.sync
        def _(sp):
            def fetch(b, u):
                wait(sp, products, b * (NK + NV) - (NK + NV))
                sp.dma_start(ctx_T[u][:, :, :], a["ctx_T"][bass.ds(b, 1)].rearrange("a d (t p) -> (a d) t p", t=KT))\
                    .then_inc(loaded[u], 16)
                if masked:
                    wait(sp, masks_made, b * 3)
                    sp.dma_start(mask_i[:, :], a["mask_T"][bass.ds(b, 1)].broadcast_to([D, SK]))\
                        .then_inc(loaded[u], 16)
                    sp.dma_start(mask_n[u][:, :], a["mask_N"][bass.ds(b, 1)].rearrange("a (p t) -> (a p) t", t=KT))\
                        .then_inc(loaded[u], 16)

            def move_rows(b, u):
                sp.wait_ge(max_split, b * 2 + 2)
                wait(sp, scores_made, b * KT - KT)
                for k, part in enumerate((max_hi, max_lo)):
                    for g in range(NG):
                        sp.dma_start(q_shift[g][u][GF + k:GF + k + 1, :].bitcast(F32),
                                     part[g * (RT // 2):(g + 1) * (RT // 2), u, :].bitcast(F32)).then_inc(row_moved, 16)

            fetch(0, 0)
            fetch(1, 1)
            move_rows(0, 0)
            fetch(2, 0)
            move_rows(1, 1)
            fetch(3, 1)
            move_rows(2, 0)
            with sp.Fori(1, B // 2 - 1) as j:
                fetch(j * 2 + 2, 0)
                move_rows(j * 2 + 1, 1)
                fetch(j * 2 + 3, 1)
                move_rows(j * 2 + 2, 0)
            move_rows(B - 1, 1)

        @block.gpsimd
        def _(pool):
            def take_queries(b, u, g):
                for n, (part, dst) in enumerate(((q[g], q_both[g][u][:, :]), (q_lo[g], q_shift[g][u][0:GF, :]))):
                    rows = dst.shape[0]
                    nc.gpsimd.tensor_tensor(dst.rearrange("p (h q) -> p h q", h=HG),
                                            bcast(part[:, batch_of(b)], HG, 1), bcast(group_mask[0:rows, :], SQ, 2),
                                            ALU.mult).then_inc(qd_made, 1)
                    pool.wait_ge(qd_made, b * 4 + 2 * g + n + 1)

            def take_keys_lo(b, u, n):
                pool.wait_ge(k_both_made, b * NK + n + 1)
                lo = k_both[n % 2][u][GF:, n // 2 * KC:(n // 2 + 1) * KC]
                nc.gpsimd.tensor_tensor(lo, k_full[n % 2][GF:, :], lo.bitcast(F32), ALU.subtract).then_inc(k_lo_made, 1)
                pool.wait_ge(k_lo_made, b * NK + n + 1)

            def prepare(b, u, i):
                pool.wait_ge(q_split, 4 * NCH)
                wait(pool, scores_made, b * KT - KT)
                for n in range(NK):
                    take_keys_lo(b, u, n)
                    if n < NG:
                        take_queries(b, u, n)

            def step(b, u, i):
                prepare(b + 1, *following(u, i))
            one_ahead(pool, prepare, step, nothing)

        @block.tensor
        def _(pe):
            def keys_product(b, u, i, n):
                if n == 0:
                    pe.wait_ge(loaded[u], i * (16 * NL) + 16 * NL)
                wait_for_bank(pe, b, ("keys", n))
                k = n // 2
                nc.tensor.matmul(s.ps[:, bank(("keys", n)), 0:KC], wk[:, n % 2].rearrange("i r f -> i (r f)"),
                                 ctx_T[u][:, :, :].rearrange("d t p -> d (t p)")[:, k * KC:(k + 1) * KC],
                                 start=True, stop=True).then_inc(products, 1)

            def values_product(b, u, i, g):
                wait_for_bank(pe, b, ("values", g))
                for t in range(4):
                    mm = nc.tensor.matmul(s.ps[0:KP, bank(("values", g)), t * D:(t + 1) * D], ctx_T[u][:, 4 * g + t, :],
                                          wv[:, :], start=True, stop=True, skip_group_check=True)
                mm.then_inc(products, 1)

            def score_rows(b, u, i, n):
                t, k, g = rows_of(n)
                j = t % JT
                if j == 0:
                    pe.wait_ge(k_hi_made, b * NK + n // JT + 1)
                    pe.wait_ge(qd_made, b * 4 + 2 * g + 1)
                wait_for_bank(pe, b, ("rows", n))
                nc.tensor.matmul(s.ps[0:RW, bank(("rows", n)), 0:KC], q_both[g][u][0:GF, j * RW:(j + 1) * RW],
                                 k_hi[g][u][0:GF, k * KC:(k + 1) * KC], start=True, stop=True).then_inc(k_rows, 1)

            make = {"keys": keys_product, "values": values_product, "rows": score_rows}

            def turn(b, u):
                pe.wait_ge(max_made, b + 1)
                wait(pe, normed, b - 2)
                nc.tensor.transpose(s.ps[0:RT, 7, 0:RW], max_col[:, u, :], s.ident[0:RW, 0:RW]).then_inc(max_turned, 1)

            def values(b, u, t):
                pe.wait_ge(probs_made, b * KT + t + 1)
                if t == 0:
                    wait(pe, acc_taken, b * 4)
                for h in range(H16):
                    j, c = h % 4, h // 4
                    mm = nc.tensor.matmul(s.ps[32 * j:32 * j + DK + 1, 6, c * SQ:(c + 1) * SQ], v[u][:, t, h, :],
                                          probs[t % 2][:, h * SQ:(h + 1) * SQ], start=(t == 0 and c == 0),
                                          stop=(t == KT - 1), skip_group_check=True)
                mm.then_inc(probs_used, 1)

            def spread_sums(b, split):
                pe.wait_ge(acc_taken, b * 4 + 4)
                pe.wait_ge(max_split, split)
                nc.tensor.matmul(s.ps[:, 7, 256:256 + 4 * SQ], sum_rows[:, :, :].rearrange("p j i -> p (j i)"),
                                 acc[:, :], start=True, stop=True).then_inc(sums_made, 1)

            def step(b, u, i, last=False):
                later = not (isinstance(b, int) and b == 0)
                pe.wait_ge(k_lo_made, b * NK + NK)
                pe.wait_ge(qd_made, b * 4 + 4)
                for t in range(KT):
                    ahead = [] if last else slots[t]
                    wait(pe, probs_made, b * KT + t - 1)
                    tile = slice(t * KP, (t + 1) * KP)
                    for g in range(NG):
                        nc.tensor.matmul(s.ps[0:KP, 2 * (t % 2) + g, 0:GC], k_both[g][u][:, tile], q_both[g][u][:, :],
                                         start=True, stop=False)
                    if t == 0 and later:
                        values(b - 1, 1 - u, KT - 1)
                    for kind, n in ahead[:1]:
                        make[kind](b + 1, *following(u, i), n)
                    if t == 0:
                        pe.wait_ge(row_moved, b * 64 + 64)
                    for g in range(NG):
                        mm = nc.tensor.matmul(s.ps[0:KP, 2 * (t % 2) + g, 0:GC], k_hi[g][u][:, tile], q_shift[g][u][:, :],
                                              start=False, stop=True)
                    mm.then_inc(scores_made, 1)
                    for kind, n in ahead[1:2]:
                        make[kind](b + 1, *following(u, i), n)
                    if t == KT - 1 and later:
                        spread_sums(b - 1, b * 2 + (2 if last else 4))
                    if t:
                        values(b, u, t - 1)
                    for kind, n in ahead[2:]:
                        make[kind](b + 1, *following(u, i), n)
                    if t == KT - 2 and not last:
                        turn(b + 1, 1 - u)

            def first(b, u, i):
                for kind, n in order:
                    make[kind](b, u, i, n)
                turn(b, u)

            def end(b, u, i):
                step(b, u, i, last=True)
                values(b, u, KT - 1)
                spread_sums(b, b * 2 + 2)
            one_ahead(pe, first, step, end)

        @block.scalar
        def _(act):
            def take_keys(b, u, n):
                act.wait_ge(scratch_dve, b * ND + emptied_by_dve(("keys", n)))
                wait(act, scores_made, b * KT - KT)
                cols = slice(n // 2 * KC, (n // 2 + 1) * KC)
                nc.scalar.activation(k_both[n % 2][u][:, cols], k_full[n % 2][:, :], ACT.Copy).then_inc(k_both_made, 1)
                nc.scalar.activation(k_hi[n % 2][u][0:GF, cols], k_full[n % 2][0:GF, :], ACT.Copy).then_inc(k_hi_made, 1)

            def take_values(b, u, g):
                if g == 0:
                    wait(act, probs_used, b * KT - KT)
                act.wait_ge(products, b * (NK + NV) + NK + g + 1)
                nc.scalar.activation(v[u][:, 4 * g:4 * g + 4, :, 0:DK],
                                     s.ps[0:KP, bank(("values", g)), :].rearrange("p (t h d) -> p t h d", t=4, h=H16),
                                     ACT.Copy).then_inc(scratch_act, 1)

            take = {"keys": take_keys, "values": take_values}

            def first(b, u, i):
                for kind, n in order:
                    if kind in take:
                        take[kind](b, u, n)

            def step(b, u, i, last=False):
                for t in range(KT):
                    act.wait_ge(scores_made, b * KT + t + 1)
                    wait(act, probs_used, b * KT + t - 1)
                    if masked and t == 0:
                        act.wait_ge(masks_made, b * 3 + 3)
                    nc.scalar.activation(probs[t % 2][:, :].rearrange("p (h c) -> p h c", h=2),
                                         s.ps[0:KP, 2 * (t % 2):2 * (t % 2) + 2, 0:HQ // 2], ACT.Exp,
                                         bias=neg_col[:, u, t:t + 1] if masked else 0.0).then_inc(probs_made, 1)
                    for kind, n in [] if last else slots[t]:
                        if kind in take:
                            take[kind](b + 1, 1 - u, n)
                act.wait_ge(probs_used, b * KT + KT)
                wait(act, normed, b)
                for j in range(4):
                    rows = slice(32 * j, 32 * j + DK + 1)
                    nc.scalar.activation(acc[rows, :], s.ps[rows, 6, 0:4 * SQ], ACT.Copy).then_inc(acc_taken, 1)

            def end(b, u, i):
                step(b, u, i, last=True)
            one_ahead(act, first, step, end)

        @block.vector
        def _(dve):
            for n in range(NG * NCH):
                g, c = n // NCH, n % NCH
                cols, rounded = slice(c * CH, (c + 1) * CH), q_both[c // 2][c % 2]
                if g:
                    dve.wait_ge(q_split, 2 * (n - NCH) + 2)
                nc.vector.tensor_copy(rounded[0:GF, :], q[g][0:GF, cols]).then_inc(q_split, 1)
                dve.wait_ge(q_split, 2 * n + 1)
                nc.vector.tensor_tensor(q_lo[g][:, cols], q[g][0:GF, cols], rounded[0:GF, :].bitcast(F32), ALU.subtract)\
                    .then_inc(q_split, 1)

            def empty_keys(b, n):
                g, cols = n % 2, slice(n // 2 * KC, (n // 2 + 1) * KC)
                product = s.ps[:, bank(("keys", n)), 0:KC]
                dve.wait_ge(products, b * (NK + NV) + n + 1)
                wait(dve, k_lo_made, b * NK + n - 1)
                wait(dve, k_hi_made, b * NK + n - 1)
                if masked:
                    nc.vector.scalar_tensor_tensor(k_full[n % 2][:, :], product, bias_k[:, g:g + 1], valid_row[:, cols],
                                                   ALU.add, ALU.mult).then_inc(scratch_dve, 1)
                else:
                    nc.vector.tensor_scalar(k_full[n % 2][:, :], product, bias_k[:, g:g + 1], None, ALU.add)\
                        .then_inc(scratch_dve, 1)

            def empty_rows(b, u, n):
                t, k, g = rows_of(n)
                scores, best = s.ps[0:RW, bank(("rows", n)), 0:KC], chunk_max[:, u, t, k:k + 1]
                dve.wait_ge(k_rows, b * ROWS + n + 1)
                if masked:
                    nc.vector.memset(carrier[:, n:n + 1], 0.0)
                    nc.vector.tensor_tensor_reduce(scores, scores, neg_row[0:RW, k * KC:(k + 1) * KC], 1.0, -3e38,
                                                   ALU.add, ALU.max, best).then_inc(scratch_dve, 1)
                else:
                    nc.vector.tensor_reduce(best, scores, AX.X, ALU.max).then_inc(scratch_dve, 1)

            def prepare(b, u, i):
                if masked:
                    dve.wait_ge(loaded[u], i * (16 * NL) + 16 * NL)
                    nc.vector.tensor_scalar(neg_row[:, :], mask_i[:, :], 0.0, MASKED, ALU.is_equal, ALU.mult)\
                        .then_inc(masks_made, 1)
                    nc.vector.tensor_scalar(valid_row[:, :], mask_i[:, :], 0.0, None, ALU.not_equal)\
                        .then_inc(masks_made, 1)
                    wait(dve, probs_made, b * KT - KT)
                    nc.vector.tensor_scalar(neg_col[:, u, :], mask_n[u][:, :], 0.0, MASKED, ALU.is_equal, ALU.mult)\
                        .then_inc(masks_made, 1)
                    dve.wait_ge(masks_made, b * 3 + 3)
                for kind, n in order:
                    if kind == "keys":
                        empty_keys(b, n)
                    elif kind == "rows":
                        empty_rows(b, u, n)
                dve.wait_ge(scratch_dve, b * ND + ND)
                wait(dve, max_turned, b - 1)
                nc.vector.tensor_reduce(max_col[:, u, :], chunk_max[:, u, :, :], AX.X, ALU.max, negate=True)\
                    .then_inc(max_made, 1)

            def split(b, u):
                dve.wait_ge(max_turned, b + 1)
                wait(dve, row_moved, b * 64 - 64)
                nc.vector.tensor_copy(max_hi[:, u, :], s.ps[0:RT, 7, 0:RW]).then_inc(max_split, 1)
                dve.wait_ge(max_split, b * 2 + 1)
                nc.vector.tensor_tensor(max_lo[:, u, :], s.ps[0:RT, 7, 0:RW], max_hi[:, u, :].bitcast(F32), ALU.subtract)\
                    .then_inc(max_split, 1)

            def norm(b):
                dve.wait_ge(sums_made, b + 1)
                nc.vector.reciprocal(inv[:, :], s.ps[:, 7, 256:256 + 4 * SQ]).then_inc(inverted, 1)
                dve.wait_ge(inverted, b + 1)
                nc.vector.tensor_tensor(heads_out[:, :, batch_of(b)], acc[:, :].rearrange("p (c q) -> p c q", c=4),
                                        inv[:, :].rearrange("p (c q) -> p c q", c=4), ALU.mult).then_inc(normed, 1)

            def first(b, u, i):
                prepare(b, u, i)
                split(b, u)

            def step(b, u, i):
                prepare(b + 1, *following(u, i))
                split(b + 1, 1 - u)
                if not (isinstance(b, int) and b == 0):
                    norm(b - 1)

            def end(b, u, i):
                norm(b - 1)
                norm(b)
            one_ahead(dve, first, step, end)

        batches.close()
        output_projection(nc, s, layer, heads_out, wo_quad, bv_quad, bias[:, 0:1])

def output_projection(nc, s, name, heads_out, wo_quad, bv_quad, bias):
    with ExitStack() as ctx:
        biased, product_made, added = (ctx.enter_context(nc.semaphore(f"{name}_{n}"))
                                       for n in ("biased", "product_made", "added"))
        block = ctx.enter_context(nc.Block())

        @block.tensor
        def _(pe):
            for c in range(NCH):
                pe.wait_ge(biased, c + 1)
                for g in range(4):
                    mm = nc.tensor.matmul(s.ps[:, c, 0:CH], wo_quad[:, g, :], heads_out[:, g, c * CH:(c + 1) * CH],
                                          start=(g == 0), stop=(g == 3))
                mm.then_inc(product_made, 1)

        @block.gpsimd
        def _(pool):
            for c in range(NCH):
                cols = heads_out[:, :, c * CH:(c + 1) * CH]
                nc.gpsimd.tensor_tensor(cols, cols, bcast(bv_quad[:, :], CH, 2), ALU.add).then_inc(biased, 1)

        @block.vector
        def _(dve):
            for c in range(NCH):
                dve.wait_ge(product_made, c + 1)
                nc.vector.scalar_tensor_tensor(s.x_T[:, c * CH:(c + 1) * CH], s.ps[:, c, 0:CH], bias,
                                               s.x_T[:, c * CH:(c + 1) * CH], ALU.add, ALU.add).then_inc(added, 1)


def quantized(nc, s, a):
    with ExitStack() as ctx:
        def sb(name, shape, dt=F32):
            return ctx.enter_context(nc.sbuf_tensor(f"q2_{name}", shape, dt))

        def sem(name):
            return ctx.enter_context(nc.semaphore(f"q2_{name}"))

        w1, w2, b1, b2 = sb("w1", [D, HID]), sb("w2", [D, HT, D]), sb("b1", [D, HT]), sb("b2", [D, 1])
        quarter = sb("quarter", [D, 1])
        h, clamped, cell, y0, y1, hq = (sb(n, [D, HT, CH]) for n in ("h", "clamped", "cell", "y0", "y1", "hq"))
        out = sb("out", [D, CH])
        load(nc, s, [(w1[:, :], a["L2_w1"]), (w2[:, :, :].rearrange("p j o -> p (j o)"), a["L2_w2"]),
                           (b1[:, :], a["L2_b1"]), (b2[:, :], a["L2_b2"])])
        ready, hidden_made, scaled, step, cells, ends, sloped, out_made = (
            sem(n) for n in ("ready", "hidden_made", "scaled", "step", "cells", "ends", "sloped", "out_made"))
        start_at_one(nc, [scaled, step, out_made])
        STEPS = 12
        block = ctx.enter_context(nc.Block())

        @block.tensor
        def _(pe):
            with pe.Fori(0, NCH) as c:
                pe.wait_ge(scaled, 1 + c * HT)
                for j in range(HT):
                    nc.tensor.matmul(s.ps[:, j, 0:CH], w1[:, j * D:(j + 1) * D], s.xn[:, bass.ds(c * CH, CH)],
                                     start=True, stop=True).then_inc(hidden_made, 1)
                pe.wait_ge(step, 1 + c * STEPS + 9)
                for j in range(HT):
                    mm = nc.tensor.matmul(s.ps[:, 4, 0:CH], w2[:, j, :], hq[:, j, :], start=(j == 0), stop=(j == HT - 1))
                mm.then_inc(out_made, 1)

        @block.scalar
        def _(act):
            act.wait_ge(ready, 3)
            with act.Fori(0, NCH) as c:
                act.wait_ge(step, 1 + c * STEPS)
                for j in range(HT):
                    act.wait_ge(hidden_made, c * HT + j + 1)
                    nc.scalar.activation(h[:, j, :], s.ps[:, j, 0:CH], ACT.Identity, bias=b1[:, j:j + 1], scale=256.0)\
                        .then_inc(scaled, 1)
                act.wait_ge(step, 1 + c * STEPS + 4)
                nc.scalar.activation(y0[:, :, :], cell[:, :, :], ACT.Gelu, scale=0.25).then_inc(ends, 1)
                nc.scalar.activation(y1[:, :, :], cell[:, :, :], ACT.Gelu, bias=quarter[:, 0:1], scale=0.25)\
                    .then_inc(ends, 1)

        @block.gpsimd
        def _(pool):
            with pool.Fori(0, NCH) as c:
                pool.wait_ge(ends, c * 2 + 2)
                nc.gpsimd.tensor_tensor(y1[:, :, :], y1[:, :, :], y0[:, :, :], ALU.subtract).then_inc(sloped, 1)
                pool.wait_ge(sloped, c * 2 + 1)
                pool.wait_ge(step, 1 + c * STEPS + 5)
                nc.gpsimd.tensor_tensor(y1[:, :, :], y1[:, :, :], clamped[:, :, :], ALU.mult).then_inc(sloped, 1)

        @block.vector
        def _(dve):
            nc.vector.memset(quarter[:, :], 0.25).then_inc(ready, 1)
            nc.vector.tensor_scalar(b1[:, :], b1[:, :], 256.0, None, ALU.mult).then_inc(ready, 1)
            nc.vector.tensor_scalar(b2[:, :], b2[:, :], 256.0, None, ALU.mult).then_inc(ready, 1)
            with dve.Fori(0, NCH) as c:
                count = [0]

                def chain(ins):
                    count[0] += 1
                    ins.then_inc(step, 1)
                    dve.wait_ge(step, 1 + c * STEPS + count[0])

                dve.wait_ge(scaled, 1 + c * HT + HT)
                chain(nc.vector.tensor_scalar(h[:, :, :], h[:, :, :], MAGIC, MAGIC, ALU.add, ALU.subtract))
                chain(nc.vector.tensor_scalar(clamped[:, :, :], h[:, :, :], -1024.0, 1024.0, ALU.max, ALU.min))
                chain(nc.vector.tensor_scalar(cell[:, :, :], clamped[:, :, :], 1.0 / 64, -0.5 + 1.0 / 128,
                                              ALU.mult, ALU.add))
                chain(nc.vector.tensor_scalar(cell[:, :, :], cell[:, :, :], MAGIC, MAGIC, ALU.add, ALU.subtract))
                chain(nc.vector.scalar_tensor_tensor(clamped[:, :, :], cell[:, :, :], -64.0, clamped[:, :, :],
                                                     ALU.mult, ALU.add))
                chain(nc.vector.tensor_scalar(h[:, :, :], h[:, :, :], -1024.0, 0.0, ALU.add, ALU.max))
                dve.wait_ge(sloped, c * 2 + 2)
                chain(nc.vector.scalar_tensor_tensor(y0[:, :, :], y1[:, :, :], 1.0 / 64, y0[:, :, :], ALU.mult, ALU.add))
                chain(nc.vector.scalar_tensor_tensor(h[:, :, :], y0[:, :, :], 256.0, h[:, :, :], ALU.mult, ALU.add))
                dve.wait_ge(out_made, 1 + c)
                chain(nc.vector.tensor_scalar(hq[:, :, :], h[:, :, :], MAGIC, MAGIC, ALU.add, ALU.subtract))
                dve.wait_ge(out_made, 1 + c + 1)
                chain(nc.vector.tensor_scalar(out[:, :], s.ps[:, 4, 0:CH], b2[:, 0:1], None, ALU.add))
                chain(nc.vector.tensor_scalar(out[:, :], out[:, :], MAGIC, MAGIC, ALU.add, ALU.subtract))
                chain(nc.vector.scalar_tensor_tensor(s.x_T[:, bass.ds(c * CH, CH)], out[:, :], 1.0 / 256,
                                                     s.x_T[:, bass.ds(c * CH, CH)], ALU.mult, ALU.add))


def routed(nc, s, a):
    NE = 3
    with ExitStack() as ctx:
        def sb(name, shape, dt=F32):
            return ctx.enter_context(nc.sbuf_tensor(f"r3_{name}", shape, dt))

        def sem(name):
            return ctx.enter_context(nc.semaphore(f"r3_{name}"))

        w1, w2, b1, b2 = sb("w1", [D, NE, HID]), sb("w2", [D, NE * HT, D]), sb("b1", [D, NE * HT]), sb("b2", [D, NE])
        gate, gates = sb("gate", [D, 2]), sb("gates", [D, 2, D])
        bias = sb("bias", [D, 1])
        second = sb("second", [D, CH])
        routed_x = sb("routed_x", [D, 2, CH])
        hidden = sb("hidden", [D, 4, CH])
        load(nc, s, [(w1[:, 0:2, :], a["L3_w1"]), (w1[:, 2, :], a["L3_sw1"]),
                           (w2[:, 0:2 * HT, :], a["L3_w2"]), (w2[:, 2 * HT:, :], a["L3_sw2"]),
                           (b1[:, 0:2 * HT], a["L3_b1"]), (b1[:, 2 * HT:], a["L3_sb1"]),
                           (b2[:, 0:2], a["L3_b2"]), (b2[:, 2:3], a["L3_sb2"]), (gate[:, :], a["L3_gate_w"])])
        ready, gates_made, second_taken, route, hidden_made, hidden_taken, out_made, out_taken = (
            sem(n) for n in ("ready", "gates_made", "second_taken", "route", "hidden_made", "hidden_taken",
                             "out_made", "out_taken"))
        start_at_one(nc, [route, second_taken, out_taken, hidden_taken, out_made, hidden_made])
        NT = NE * HT
        block = ctx.enter_context(nc.Block())

        @block.tensor
        def _(pe):
            pe.wait_ge(ready, 2)
            with pe.Fori(0, NCH) as c:
                chunk = s.xn[:, bass.ds(c * CH, CH)]
                pe.wait_ge(route, 1 + c * 3)
                pe.wait_ge(second_taken, 1 + c)
                for g in range(2):
                    nc.tensor.matmul(s.ps[:, 5 + g, 0:CH], gates[:, g, :], chunk, start=True, stop=True)\
                        .then_inc(gates_made, 1)
                pe.wait_ge(out_taken, 1 + c)
                order = [2, 0, 1]
                for n in range(NT + 2):
                    if n < NT:
                        e, j = order[n // HT], n % HT
                        if n >= 4:
                            pe.wait_ge(hidden_taken, 1 + c * NT + n - 3)
                        else:
                            pe.wait_ge(hidden_taken, 1 + c * NT)
                        if e < 2 and j == 0:
                            pe.wait_ge(route, 1 + c * 3 + 2 + e)
                        nc.tensor.matmul(s.ps[:, n % 4, 0:CH], w1[:, e, j * D:(j + 1) * D],
                                         chunk if e == 2 else routed_x[:, e, :], start=True, stop=True)\
                            .then_inc(hidden_made, 1)
                    if n >= 2:
                        m = n - 2
                        pe.wait_ge(hidden_taken, 1 + c * NT + m + 1)
                        nc.tensor.matmul(s.ps[:, 4, 0:CH], w2[:, order[m // HT] * HT + m % HT, :], hidden[:, m % 4, :],
                                         start=(m == 0), stop=(m == NT - 1)).then_inc(out_made, 1)

        @block.scalar
        def _(act):
            with act.Fori(0, NCH) as c:
                act.wait_ge(gates_made, c * 2 + 2)
                act.wait_ge(route, 1 + c * 3)
                nc.scalar.activation(second[:, :], s.ps[:, 6, 0:CH], ACT.Copy).then_inc(second_taken, 1)
                for n in range(NT):
                    e, j = [2, 0, 1][n // HT], n % HT
                    act.wait_ge(hidden_made, 1 + c * NT + n + 1)
                    if n >= 4:
                        act.wait_ge(out_made, 1 + c * NT + n - 3)
                    else:
                        act.wait_ge(out_made, 1 + c * NT)
                    nc.scalar.activation(hidden[:, n % 4, :], s.ps[:, n % 4, 0:CH], ACT.Relu,
                                         bias=b1[:, e * HT + j:e * HT + j + 1]).then_inc(hidden_taken, 1)

        @block.vector
        def _(dve):
            nc.vector.tensor_copy(gates[:, :, :], bcast(gate[:, :], D, 2)).then_inc(ready, 1)
            nc.vector.tensor_reduce(bias[:, :], b2[:, :], AX.X, ALU.add).then_inc(ready, 1)
            dve.wait_ge(ready, 2)
            with dve.Fori(0, NCH) as c:
                chunk = s.xn[:, bass.ds(c * CH, CH)]
                dve.wait_ge(second_taken, 1 + c + 1)
                dve.wait_ge(hidden_made, 1 + c * NT)
                nc.vector.tensor_tensor(routed_x[:, 1, :], s.ps[:, 5, 0:CH], second[:, :], ALU.is_ge).then_inc(route, 1)
                dve.wait_ge(route, 1 + c * 3 + 1)
                nc.vector.tensor_tensor(routed_x[:, 0, :], routed_x[:, 1, :], chunk, ALU.mult).then_inc(route, 1)
                dve.wait_ge(route, 1 + c * 3 + 2)
                nc.vector.tensor_tensor(routed_x[:, 1, :], chunk, routed_x[:, 0, :], ALU.subtract).then_inc(route, 1)
                dve.wait_ge(out_made, 1 + c * NT + NT)
                nc.vector.scalar_tensor_tensor(s.x_T[:, bass.ds(c * CH, CH)], s.ps[:, 4, 0:CH], bias[:, 0:1],
                                               s.x_T[:, bass.ds(c * CH, CH)], ALU.add, ALU.add).then_inc(out_taken, 1)


def attention_latents(nc, s, a):
    with ExitStack() as ctx:
        def sb(name, shape, dt=F32):
            return ctx.enter_context(nc.sbuf_tensor(f"l3_{name}", shape, dt))

        def sem(name):
            return ctx.enter_context(nc.semaphore(f"l3_{name}"))

        NP = 4
        affine = sb("affine", [D, 6])
        latents = sb("latents", [D, TOK])
        q = sb("q", [D, NP, TOK])
        wq, wk, wkT, wv = sb("wq", [D, HID]), sb("wk", [D, HID]), sb("wkT", [D, NP, D]), sb("wv", [D, HID])
        wo = sb("wo", [D, NP, D])
        bx_rows = sb("bx_rows", [SQ, D])
        values_bias, out_bias = sb("values_bias", [D, NP]), sb("out_bias", [D, 1])
        neg_cols = sb("neg_cols", [KP, B, KT])
        load(nc, s, [(affine[:, k:k + 1], a[f"L3_{n}"]) for k, n in
                           enumerate(("ln_x_w", "ln_x_b", "ln_l_w", "ln_l_b", "ln_o_w", "ln_o_b"))] +
             [(wq[:, :], a["L3_Wq"]), (wk[:, :], a["L3_Wk"]), (wkT[:, :, :], a["L3_WkT"]), (wv[:, :], a["L3_Wv"]),
              (wo[:, :, :], a["L3_Wo"]), (bx_rows[:, :], a["L3_bx_row"].broadcast_to([SQ, D]))])
        layer_norm(nc, s, "l3l", s.xn, latents, affine[:, 2:3], affine[:, 3:4])

        with ExitStack() as sub:
            def tmp(name, shape, dt=F32):
                return sub.enter_context(nc.sbuf_tensor(f"l3_{name}", shape, dt))

            masks = tmp("masks", [KP, B, KT], mybir.dt.uint8)
            scales = tmp("scales", [D, 2])
            head_sel, head_selT = tmp("head_sel", [D, NP, H8]), tmp("head_selT", [H8, NP, D])
            squares = tmp("squares", [D, NP, CH])
            inv = tmp("q_inv", [H8, CH])
            load(nc, s, [(masks[:, :, :], a["mask_B"].rearrange("b (p t) -> p b t", t=KT)), (scales[0:DH, 0:1], a["L3_q_scale"]),
                                (scales[DH:D, 0:1], a["L3_q_scale"]), (scales[0:DH, 1:2], a["L3_k_scale"]),
                                (scales[DH:D, 1:2], a["L3_k_scale"])])
            made, step, q_made, squared, norms_made, std, spread_made = (
                sub.enter_context(nc.semaphore(f"l3q_{n}")) for n in
                ("made", "step", "q_made", "squared", "norms_made", "std", "spread_made"))
            with nc.Block() as block:
                @block.gpsimd
                def _(pool):
                    nc.gpsimd.memset(head_sel[:, :, :], 1.0).then_inc(made, 1)
                    nc.gpsimd.memset(head_selT[:, :, :], 1.0).then_inc(made, 1)
                    pool.wait_ge(made, 2)
                    nc.gpsimd.affine_select(out=head_sel[:, :, :], in_=head_sel[:, :, :], compare_op=ALU.is_ge, fill=0.0,
                                            base=0, pattern=[[D, NP], [-DH, H8]], channel_multiplier=1).then_inc(made, 1)
                    nc.gpsimd.affine_select(out=head_selT[:, :, :], in_=head_selT[:, :, :], compare_op=ALU.is_ge,
                                            fill=0.0, base=0, pattern=[[D, NP], [1, D]], channel_multiplier=-DH)\
                        .then_inc(made, 1)
                    pool.wait_ge(made, 4)
                    nc.gpsimd.affine_select(out=head_sel[:, :, :], in_=head_sel[:, :, :], compare_op=ALU.is_ge, fill=0.0,
                                            base=DH - 1, pattern=[[-D, NP], [DH, H8]], channel_multiplier=-1)\
                        .then_inc(made, 1)
                    nc.gpsimd.affine_select(out=head_selT[:, :, :], in_=head_selT[:, :, :], compare_op=ALU.is_ge,
                                            fill=0.0, base=DH - 1, pattern=[[-D, NP], [-1, D]],
                                            channel_multiplier=DH).then_inc(made, 1)

                @block.tensor
                def _(pe):
                    pe.wait_ge(made, 6)
                    for c in range(NCH):
                        if c:
                            pe.wait_ge(q_made, 4 * c)
                        for j in range(NP):
                            mm = nc.tensor.matmul(s.ps[:, j, 0:CH], wq[:, j * D:(j + 1) * D],
                                                  latents[:, c * CH:(c + 1) * CH], start=True, stop=True)
                        mm.then_inc(norms_made, 1)
                        pe.wait_ge(squared, c + 1)
                        for j in range(NP):
                            mm = nc.tensor.matmul(s.ps[0:H8, 4, 0:CH], head_sel[:, j, :], squares[:, j, :],
                                                  start=(j == 0), stop=(j == NP - 1))
                        mm.then_inc(norms_made, 1)
                        pe.wait_ge(step, 2 + 3 * c + 2)
                        for j in range(NP):
                            if j:
                                pe.wait_ge(q_made, 4 * c + j)
                            nc.tensor.matmul(s.ps[:, 5, 0:CH], head_selT[:, j, :], inv[:, :], start=True, stop=True)\
                                .then_inc(spread_made, 1)

                @block.scalar
                def _(act):
                    for c in range(NCH):
                        act.wait_ge(norms_made, 2 * c + 1)
                        nc.scalar.activation(squares[:, :, :], s.ps[:, 0:NP, 0:CH], ACT.Square).then_inc(squared, 1)
                        act.wait_ge(norms_made, 2 * c + 2)
                        if c:
                            act.wait_ge(spread_made, 4 * c)
                        nc.scalar.activation(inv[:, :], s.ps[0:H8, 4, 0:CH], ACT.Sqrt).then_inc(std, 1)

                @block.vector
                def _(dve):
                    nc.vector.tensor_scalar(neg_cols[:, :, :], masks[:, :, :], 0.0, NEVER, ALU.is_equal, ALU.mult)\
                        .then_inc(step, 1)
                    nc.vector.scalar_tensor_tensor(scales[:, 0:1], scales[:, 0:1], 8.0, scales[:, 1:2], ALU.mult,
                                                   ALU.mult).then_inc(step, 1)
                    for c in range(NCH):
                        dve.wait_ge(squared, c + 1)
                        dve.wait_ge(std, c + 1)
                        nc.vector.tensor_scalar(inv[:, :], inv[:, :], L2_EPS, None, ALU.max).then_inc(step, 1)
                        dve.wait_ge(step, 2 + 3 * c + 1)
                        nc.vector.reciprocal(inv[:, :], inv[:, :]).then_inc(step, 1)
                        nc.vector.tensor_scalar(q[:, :, c * CH:(c + 1) * CH], s.ps[:, 0:NP, 0:CH], scales[:, 0:1],
                                                None, ALU.mult).then_inc(step, 1)
                        dve.wait_ge(step, 2 + 3 * c + 3)
                        for j in range(NP):
                            dve.wait_ge(spread_made, 4 * c + j + 1)
                            cols = q[:, j, c * CH:(c + 1) * CH]
                            nc.vector.tensor_tensor(cols, cols, s.ps[:, 5, 0:CH], ALU.mult).then_inc(q_made, 1)

        bias_made, bias_taken = sem("bias_made"), sem("bias_taken")
        with nc.Block() as block:
            @block.tensor
            def _(pe):
                for j in range(NP):
                    mm = nc.tensor.matmul(s.ps[:, 0, j:j + 1], wv[:, j * D:(j + 1) * D], affine[:, 1:2], start=True,
                                          stop=True, skip_group_check=True)
                mm.then_inc(bias_made, 1)
                pe.wait_ge(bias_taken, 1)
                for j in range(NP):
                    mm = nc.tensor.matmul(s.ps[:, 1, 0:1], wo[:, j, :], values_bias[:, j:j + 1], start=(j == 0),
                                          stop=(j == NP - 1))
                mm.then_inc(bias_made, 1)

            @block.vector
            def _(dve):
                dve.wait_ge(bias_made, 1)
                nc.vector.tensor_copy(values_bias[:, :], s.ps[:, 0, 0:NP]).then_inc(bias_taken, 1)
                dve.wait_ge(bias_made, 2)
                nc.vector.tensor_copy(out_bias[:, :], s.ps[:, 1, 0:1]).then_inc(bias_taken, 1)

        T = KT + 1
        NG = KT // 4
        raw = [sb(f"ctx_N{u}", [KP, KT, D]) for u in range(2)]
        z = [sb(f"z{u}", [KP, KT, D]) for u in range(2)]
        stats, moments, rstd = sb("stats", [KP, KT, 6]), sb("moments", [KP, 4, KT]), sb("rstd", [KP, KT])
        mean_rstd = sb("mean_rstd", [KP, KT])
        xnT = [sb(f"xnT{u}", [D, SK + SQ]) for u in range(2)]
        lat_N = [sb(f"lat_N{u}", [SQ, D]) for u in range(2)]
        squares = sb("k_squares", [KP, 2, HID])
        norms = sb("norms", [KP, KT + 1, H8])
        inv_norms = sb("inv_norms", [KP, KT + 1, H8])
        q_blocks = sb("q_blocks", [D, NP, 2, SQ])
        G = sb("G", [D, HQ3])
        neg = [sb(f"neg{u}", [KP, KT]) for u in range(2)]
        S = sb("S", [KP, KT + 1, HQ3])
        top = sb("top", [KP, HQ3])
        neg_max = sb("neg_max", [2 * SQ, NP])
        diag = sb("diag", [2 * SQ, NP, 2 * SQ])
        shift = sb("shift", [KP, HQ3])
        prob_sum = sb("prob_sum", [KP, NG, HQ3])
        inv, mixed, mixed_lat = sb("inv", [D, NP * SQ]), sb("mixed", [D, HQ3]), sb("mixed_lat", [D, HQ3])
        heads = sb("heads", [D, NP, SQ])
        loaded = [sem("even_loaded"), sem("odd_loaded")]
        (init, blocks_zeroed, lat_copied, qb_made, stats_made, mean_made, std_made, rstd_made, z_made, turned,
         xnT_made, lat_turned, lat_made, k_made, squared, reduced, root_made, inv_made, G_made, G_taken, negs_made,
         raw_made, S_made, topped, top_turned, maxed, diag_made, spread_made, shift_made, shifted, exps_made,
         summed, sums_made, lat_mixed, mixed_made, inv_sums, heads_made, heads_taken, y_made, y_taken) = (
            sem(n) for n in (
                "init", "blocks_zeroed", "lat_copied", "qb_made", "stats_made", "mean_made", "std_made", "rstd_made",
                "z_made", "turned", "xnT_made", "lat_turned", "lat_made", "k_made", "squared", "reduced", "root_made",
                "inv_made", "G_made", "G_taken", "negs_made", "raw_made", "S_made", "topped", "top_turned", "maxed",
                "diag_made", "spread_made", "shift_made", "shifted", "exps_made", "summed", "sums_made", "lat_mixed", "mixed_made",
                "inv_sums", "heads_made", "heads_taken", "y_made", "y_taken"))
        NM = 4

        AHEAD = 5

        def rows(t):
            return KP if t < KT else SQ

        batches = ExitStack()
        block = batches.enter_context(nc.Block())

        def staged(eng, first, step, last):
            first()
            step(0, 0, 0, True)
            with eng.Fori(0, B // 2 - 2) as j:
                step(j * 2 + 1, 1, j, True)
                step(j * 2 + 2, 0, j + 1, True)
            step(B - 3, 1, B // 2 - 2, True)
            step(B - 2, 0, B // 2 - 1, False)
            last(B - 1, 1, B // 2 - 1)

        @block.sync
        def _(sp):
            def fetch(b, u):
                wait(sp, z_made, b - 1)
                sp.dma_start(raw[u][:, :, :], a["ctx_N"][bass.ds(b, 1)].rearrange("a (p t) d -> (a p) t d", t=KT))\
                    .then_inc(loaded[u], 16)
            fetch(0, 0)
            fetch(1, 1)
            with sp.Fori(1, B // 2) as j:
                fetch(j * 2, 0)
                fetch(j * 2 + 1, 1)

        @block.gpsimd
        def _(pool):
            def queries(b):
                wait(pool, G_made, b)
                for half in range(2):
                    r = slice(half * DH, (half + 1) * DH)
                    nc.gpsimd.tensor_copy(q_blocks[r, :, half, :], q[r, :, batch_of(b)]).then_inc(qb_made, 1)
                    pool.wait_ge(qb_made, b * 2 + half + 1)

            def take_latents(b, u):
                wait(pool, raw_made, b * T - T)
                nc.gpsimd.tensor_copy(xnT[u][:, SK:], latents[:, batch_of(b)]).then_inc(lat_copied, 1)
                pool.wait_ge(lat_copied, b + 1)

            def subtract_maxima(b):
                pool.wait_ge(shift_made, b + 1)
                for t in range(T):
                    r = rows(t)
                    nc.gpsimd.tensor_tensor(S[0:r, t, :], S[0:r, t, :], shift[0:r, :], ALU.add).then_inc(shifted, 1)

            def first():
                nc.gpsimd.memset(q_blocks[:, :, :, :], 0.0).then_inc(blocks_zeroed, 1)
                pool.wait_ge(blocks_zeroed, 1)
                take_latents(0, 0)
                queries(0)
                take_latents(1, 1)
                queries(1)

            def step(b, u, i, more):
                subtract_maxima(b)
                if more:
                    take_latents(b + 2, u)
                    queries(b + 2)

            def last(b, u, i):
                subtract_maxima(b)
            staged(pool, first, step, last)

        @block.tensor
        def _(pe):
            def turn_context(b, u, g):
                if g == 0:
                    pe.wait_ge(z_made, b + 1)
                if g < 2:
                    wait(pe, squared, b * T)
                elif g < NG:
                    pe.wait_ge(xnT_made, b * NG + g - 1)
                if g < NG:
                    for t in range(4):
                        mm = nc.tensor.transpose(s.ps[:, g % 2, t * KP:(t + 1) * KP], z[u][:, 4 * g + t, :],
                                                 s.ident[0:KP, 0:KP])
                    mm.then_inc(turned, 1)
                else:
                    nc.tensor.transpose(s.ps[0:SQ, NG % 2, 0:D], xnT[u][:, SK:], s.ident[:, :]).then_inc(lat_turned, 1)

            def latents_may_turn(b):
                pe.wait_ge(lat_copied, b + 1)
                pe.wait_ge(xnT_made, b * NG + 2)

            def key_product(b, u, t):
                if t == 0:
                    pe.wait_ge(xnT_made, b * NG + NG)
                elif t == 1:
                    pe.wait_ge(lat_made, b + 1)
                else:
                    pe.wait_ge(squared, b * T + t - 1)
                nc.tensor.matmul(s.ps[0:rows(t), t % 2, 0:HID], xnT[u][:, t * KP:t * KP + rows(t)], wk[:, :],
                                 start=True, stop=True).then_inc(k_made, 1)

            def queries_through_keys(b):
                pe.wait_ge(qb_made, b * 2 + 2)
                wait(pe, maxed, b)
                for j in range(NP):
                    mm = nc.tensor.matmul(s.ps[:, 4, j * 2 * SQ:(j + 1) * 2 * SQ], wkT[:, j, :],
                                          q_blocks[:, j, :, :].rearrange("p h q -> p (h q)"), start=True, stop=True,
                                          skip_group_check=True)
                mm.then_inc(G_made, 1)

            def score_product(b, u, t):
                if t == 0:
                    pe.wait_ge(G_taken, b + 1)
                wait(pe, S_made, b * T + max(t - 1, 0))
                nc.tensor.matmul(s.ps[0:rows(t), 2 + t % 2, 0:HQ3], xnT[u][:, t * KP:t * KP + rows(t)], G[:, :],
                                 start=True, stop=True).then_inc(raw_made, 1)

            def turn_maxima(b):
                pe.wait_ge(topped, b * KT + KT)
                wait(pe, y_taken, b)
                for j in range(NP):
                    mm = nc.tensor.transpose(s.ps[0:2 * SQ, 4, j * KP:(j + 1) * KP], top[:, j * 2 * SQ:(j + 1) * 2 * SQ],
                                             s.ident[0:KP, 0:KP])
                mm.then_inc(top_turned, 1)

            def spread_maxima(b):
                pe.wait_ge(diag_made, b + 1)
                wait(pe, heads_taken, b)
                nc.tensor.matmul(s.ps[0:KP, 5, 0:HQ3], s.ones[0:2 * SQ, 0:KP], diag[:, :, :].rearrange("p j q -> p (j q)"),
                                 start=True, stop=True).then_inc(spread_made, 1)

            def half_sums(keys, probs, start, stop):
                for half in range(2):
                    mm = nc.tensor.matmul(s.ps[half * DH:(half + 1) * DH, 5, 0:NP * SQ].rearrange("p (j q) -> p j q", j=NP),
                                          s.ones[0:keys, 0:DH],
                                          probs.rearrange("p (j h q) -> p h j q", j=NP, h=2)[:, half],
                                          start=start, stop=stop, skip_group_check=True)
                return mm

            def weigh(b, u, t):
                pe.wait_ge(exps_made, b * T + t + 1)
                nc.tensor.matmul(s.ps[:, 6, 0:HQ3], z[u][:, t, :], S[:, t, :], start=(t == 0), stop=(t == KT - 1))

            def weigh_latents(b, u):
                pe.wait_ge(exps_made, b * T + T)
                nc.tensor.matmul(s.ps[:, 7, 0:HQ3], lat_N[u][:, :], S[0:SQ, KT, :], start=True, stop=True)
                half_sums(SQ, S[0:SQ, KT, :], True, False)
                for g in range(NG):
                    pe.wait_ge(summed, b * NG + g + 1)
                    mm = half_sums(KP, prob_sum[:, g, :], False, g == NG - 1)
                mm.then_inc(sums_made, 1)

            def value_product(b):
                pe.wait_ge(mixed_made, b + 1)
                for h in range(H8):
                    r = slice((h % 2) * DH, (h % 2 + 1) * DH)
                    cols = slice(256 + (h // 2) * SQ, 256 + (h // 2 + 1) * SQ)
                    mm = nc.tensor.matmul(s.ps[r, 5, cols], wv[:, h * DH:(h + 1) * DH], mixed[:, h * SQ:(h + 1) * SQ],
                                          start=True, stop=True, skip_group_check=True)
                mm.then_inc(heads_made, 1)

            def project_out(b):
                pe.wait_ge(heads_taken, b + 1)
                for j in range(NP):
                    mm = nc.tensor.matmul(s.ps[:, 4, 0:SQ], wo[:, j, :], heads[:, j, :], start=(j == 0), stop=(j == NP - 1))
                mm.then_inc(y_made, 1)

            def scores(b, u, more, between):
                for t in range(T):
                    if more and t == T - 1:
                        latents_may_turn(b + 1)
                    score_product(b, u, t)
                    if t in between:
                        between[t]()
                    if more and t >= T - 1 - NG:
                        turn_context(b + 1, 1 - u, t - (T - 1 - NG))

            def first():
                pe.wait_ge(init, 1)
                for g in range(NG + 1):
                    if g == NG:
                        latents_may_turn(0)
                    turn_context(0, 0, g)
                for t in range(T):
                    key_product(0, 0, t)
                queries_through_keys(0)
                scores(0, 0, True, {})

            def step(b, u, i, more):
                turn_maxima(b)
                for t in range(T):
                    key_product(b + 1, 1 - u, t)
                    if t == 1:
                        spread_maxima(b)
                    if t == 4:
                        queries_through_keys(b + 1)
                    if t >= AHEAD:
                        weigh(b, u, t - AHEAD)
                for t in range(T - AHEAD, KT):
                    weigh(b, u, t)
                weigh_latents(b, u)
                scores(b + 1, 1 - u, more, {2: lambda: value_product(b), 7: lambda: project_out(b)})

            def last(b, u, i):
                turn_maxima(b)
                spread_maxima(b)
                for t in range(KT):
                    weigh(b, u, t)
                weigh_latents(b, u)
                value_product(b)
                project_out(b)
            staged(pe, first, step, last)

        @block.scalar
        def _(act):
            def std(b):
                act.wait_ge(stats_made, b * (KT + NM) + KT + NM)
                wait(act, z_made, b)
                nc.scalar.activation(rstd[:, :], moments[:, 3, :], ACT.Sqrt, bias=s.eps[0:KP, 0:1], scale=1.0 / D)\
                    .then_inc(std_made, 1)

            def normalize(b, u):
                act.wait_ge(rstd_made, b * 2 + 2)
                wait(act, sums_made, b - 1)
                for t in range(KT):
                    ins = nc.scalar.activation(z[u][:, t, :], raw[u][:, t, :], ACT.Identity, bias=mean_rstd[:, t:t + 1],
                                               scale=rstd[:, t:t + 1])
                ins.then_inc(z_made, 1)

            def take_context(b, u):
                wait(act, raw_made, b * T - T)
                for g in range(NG):
                    act.wait_ge(turned, b * NG + g + 1)
                    nc.scalar.activation(xnT[u][:, g * 4 * KP:(g + 1) * 4 * KP], s.ps[:, g % 2, 0:4 * KP], ACT.Identity,
                                         bias=affine[:, 1:2], scale=affine[:, 0:1]).then_inc(xnT_made, 1)

            def square(b, t):
                act.wait_ge(k_made, b * T + t + 1)
                wait(act, reduced, b * T + t - 1)
                nc.scalar.activation(squares[0:rows(t), t % 2, :], s.ps[0:rows(t), t % 2, 0:HID], ACT.Square)\
                    .then_inc(squared, 1)

            def take_queries(b):
                act.wait_ge(G_made, b + 1)
                wait(act, raw_made, b * T)
                nc.scalar.activation(G[:, :], s.ps[:, 4, 0:HQ3], ACT.Copy).then_inc(G_taken, 1)

            def root(b):
                act.wait_ge(reduced, b * T + T)
                nc.scalar.activation(inv_norms[:, :, :], norms[:, :, :], ACT.Sqrt).then_inc(root_made, 1)

            def take_shift(b):
                act.wait_ge(spread_made, b + 1)
                nc.scalar.activation(shift[:, :], s.ps[0:KP, 5, 0:HQ3], ACT.Copy).then_inc(shift_made, 1)

            def exp(b, t):
                act.wait_ge(shifted, b * T + t + 1)
                nc.scalar.activation(S[0:rows(t), t, :], S[0:rows(t), t, :], ACT.Exp).then_inc(exps_made, 1)

            def take_latents_sum(b):
                act.wait_ge(sums_made, b + 1)
                wait(act, mixed_made, b)
                nc.scalar.activation(mixed_lat[:, :], s.ps[:, 7, 0:HQ3], ACT.Copy).then_inc(lat_mixed, 1)

            def first():
                std(0)
                normalize(0, 0)
                std(1)
                normalize(1, 1)
                take_context(0, 0)
                for t in range(T):
                    square(0, t)
                take_queries(0)
                root(0)
                take_context(1, 1)

            def step(b, u, i, more):
                take_shift(b)
                for t in range(T):
                    square(b + 1, t)
                    exp(b, t)
                take_queries(b + 1)
                if more:
                    std(b + 2)
                root(b + 1)
                take_latents_sum(b)
                if more:
                    normalize(b + 2, u)
                    take_context(b + 2, u)

            def last(b, u, i):
                take_shift(b)
                for t in range(T):
                    exp(b, t)
                take_latents_sum(b)
            staged(act, first, step, last)

        @block.vector
        def _(dve):
            def take_stats(b, u, t, count):
                if t == 0:
                    dve.wait_ge(loaded[u], count)
                nc.vector.bn_stats(stats[:, t, :], raw[u][:, t, :]).then_inc(stats_made, 1)

            def moments_of(b):
                dve.wait_ge(stats_made, b * (KT + NM) + KT)
                wait(dve, z_made, b)
                nc.vector.tensor_tensor(moments[:, 0, :], stats[:, :, 1], stats[:, :, 4], ALU.add).then_inc(stats_made, 1)
                nc.vector.tensor_tensor(moments[:, 1, :], stats[:, :, 1], stats[:, :, 4], ALU.subtract).then_inc(stats_made, 1)
                nc.vector.tensor_tensor(moments[:, 2, :], stats[:, :, 2], stats[:, :, 5], ALU.add).then_inc(stats_made, 1)
                dve.wait_ge(stats_made, b * (KT + NM) + KT + 3)
                nc.vector.tensor_scalar(moments[:, 0, :], moments[:, 0, :], 0.5, None, ALU.mult).then_inc(mean_made, 1)
                nc.vector.tensor_tensor(moments[:, 1, :], moments[:, 1, :], moments[:, 1, :], ALU.mult).then_inc(mean_made, 1)
                dve.wait_ge(mean_made, b * 2 + 2)
                nc.vector.scalar_tensor_tensor(moments[:, 3, :], moments[:, 1, :], D / 4.0, moments[:, 2, :], ALU.mult,
                                               ALU.add).then_inc(stats_made, 1)

            def invert_std(b):
                dve.wait_ge(std_made, b + 1)
                nc.vector.reciprocal(rstd[:, :], rstd[:, :]).then_inc(rstd_made, 1)
                dve.wait_ge(rstd_made, b * 2 + 1)
                nc.vector.scalar_tensor_tensor(mean_rstd[:, :], moments[:, 0, :], -1.0, rstd[:, :], ALU.mult, ALU.mult)\
                    .then_inc(rstd_made, 1)

            def take_negs(b, u):
                wait(dve, S_made, b * T - T)
                nc.vector.tensor_copy(neg[u][:, :], neg_cols[:, bass.ds(b, 1), :].rearrange("p a t -> p (a t)"))\
                    .then_inc(negs_made, 1)

            def reduce_squares(b, t):
                if t == 0:
                    wait(dve, root_made, b)
                r = rows(t)
                dve.wait_ge(squared, b * T + t + 1)
                nc.vector.tensor_reduce(norms[0:r, t, :], squares[0:r, t % 2, :].rearrange("p (h d) -> p h d", h=H8),
                                        AX.X, ALU.add).then_inc(reduced, 1)

            def invert_norms(b):
                dve.wait_ge(root_made, b + 1)
                nc.vector.tensor_scalar(inv_norms[:, :, :], inv_norms[:, :, :], L2_EPS, None, ALU.max).then_inc(inv_made, 1)
                dve.wait_ge(inv_made, b * 2 + 1)
                nc.vector.reciprocal(inv_norms[:, :, :], inv_norms[:, :, :]).then_inc(inv_made, 1)
                dve.wait_ge(inv_made, b * 2 + 2)

            def scale_scores(b, u, t):
                r = rows(t)
                dve.wait_ge(raw_made, b * T + t + 1)
                if t == 0:
                    dve.wait_ge(negs_made, b + 1)
                heads_of = (S[0:r, t, :].rearrange("p (h q) -> p h q", h=H8),
                            s.ps[0:r, 2 + t % 2, 0:HQ3].rearrange("p (h q) -> p h q", h=H8))
                factors = bcast(inv_norms[0:r, t, :], SQ, 2)
                if t < KT:
                    ins = nc.vector.scalar_tensor_tensor(*heads_of, neg[u][:, t:t + 1], factors, ALU.add, ALU.mult)
                else:
                    ins = nc.vector.tensor_tensor(*heads_of, factors, ALU.mult)
                ins.then_inc(S_made, 1)

            def raise_top(b, t):
                r = rows(t)
                dve.wait_ge(S_made, b * T + t + 1)
                wait(dve, topped, b * KT + t - 1)
                nc.vector.tensor_tensor(top[0:r, :], S[0:r, 0, :] if t == 1 else top[0:r, :], S[0:r, t, :], ALU.max)\
                    .then_inc(topped, 1)

            def scores(b, u, between):
                for t in range(T):
                    scale_scores(b, u, t)
                    if t >= 2:
                        raise_top(b, t - 1)
                    if t in between:
                        between[t]()
                raise_top(b, KT)

            def maxima(b):
                dve.wait_ge(top_turned, b + 1)
                nc.vector.tensor_reduce(neg_max[:, :], s.ps[0:2 * SQ, 4, 0:NP * KP].rearrange("p (j k) -> p j k", j=NP),
                                        AX.X, ALU.max, negate=True).then_inc(maxed, 1)
                dve.wait_ge(maxed, b + 1)
                nc.vector.tensor_tensor(diag[:, :, :], bcast(s.ident[0:2 * SQ, 0:2 * SQ], NP, 1),
                                        bcast(neg_max[:, :], 2 * SQ, 2), ALU.mult).then_inc(diag_made, 1)

            def sum_probs(b, g):
                dve.wait_ge(exps_made, b * T + 4 * g + 4)
                nc.vector.tensor_reduce(prob_sum[:, g, :], S[:, 4 * g:4 * g + 4, :].rearrange("p t c -> p c t"), AX.X,
                                        ALU.add).then_inc(summed, 1)

            def center_latents(b, u):
                dve.wait_ge(lat_turned, b + 1)
                wait(dve, sums_made, b - 1)
                nc.vector.tensor_tensor(lat_N[u][:, :], s.ps[0:SQ, NG % 2, 0:D], bx_rows[:, :], ALU.subtract)\
                    .then_inc(lat_made, 1)

            def mix(b):
                dve.wait_ge(sums_made, b + 1)
                nc.vector.reciprocal(inv[:, :], s.ps[:, 5, 0:NP * SQ]).then_inc(inv_sums, 1)
                dve.wait_ge(lat_mixed, b + 1)
                nc.vector.scalar_tensor_tensor(mixed[:, :], s.ps[:, 6, 0:HQ3], affine[:, 0:1], mixed_lat[:, :],
                                               ALU.mult, ALU.add).then_inc(mixed_made, 1)

            def take_heads(b):
                dve.wait_ge(inv_sums, b + 1)
                dve.wait_ge(heads_made, b + 1)
                nc.vector.tensor_tensor(heads[:, :, :].rearrange("p j q -> p (j q)"), s.ps[:, 5, 256:256 + NP * SQ],
                                        inv[:, :], ALU.mult).then_inc(heads_taken, 1)

            def take_output(b):
                dve.wait_ge(y_made, b + 1)
                nc.vector.tensor_scalar(latents[:, batch_of(b)], s.ps[:, 4, 0:SQ], out_bias[:, 0:1], None, ALU.add)\
                    .then_inc(y_taken, 1)

            def first():
                nc.vector.memset(norms[:, :, :], 1.0).then_inc(init, 1)
                dve.wait_ge(init, 1)
                for t in range(KT):
                    take_stats(0, 0, t, 16)
                moments_of(0)
                invert_std(0)
                take_negs(0, 0)
                take_negs(1, 1)
                for t in range(KT):
                    take_stats(1, 1, t, 16)
                moments_of(1)
                invert_std(1)
                center_latents(0, 0)
                for t in range(T):
                    reduce_squares(0, t)
                invert_norms(0)
                scores(0, 0, {})
                center_latents(1, 1)

            def step(b, u, i, more):
                maxima(b)
                for t in range(T):
                    reduce_squares(b + 1, t)
                    if more and t < KT:
                        take_stats(b + 2, u, t, i * 16 + 32)
                    if t % 4 == 2 and t > 4:
                        sum_probs(b, t // 4 - 1)
                if more:
                    moments_of(b + 2)
                sum_probs(b, NG - 1)
                invert_norms(b + 1)
                if more:
                    take_negs(b + 2, u)
                    invert_std(b + 2)
                mix(b)
                scores(b + 1, 1 - u, {3: lambda: take_heads(b), 9: lambda: take_output(b)})
                if more:
                    center_latents(b + 2, u)

            def last(b, u, i):
                maxima(b)
                for g in range(NG):
                    sum_probs(b, g)
                mix(b)
                take_heads(b)
                take_output(b)
            staged(dve, first, step, last)

        batches.close()
        layer_norm(nc, s, "l3o", latents, s.xn, affine[:, 4:5], affine[:, 5:6], add_to=s.x_T)


def build(nc, a, out_T):
    with ExitStack() as ctx:
        def sb(name, shape, dt=F32):
            return ctx.enter_context(nc.sbuf_tensor(name, shape, dt))

        def sem(name):
            return ctx.enter_context(nc.semaphore(name))

        s = Shared()
        s.ps = ctx.enter_context(nc.psum_tensor("ps", [D, 8, 512], F32))
        s.x_T, s.xn, s.ident, s.ones = sb("x_T", [D, TOK]), sb("xn", [D, TOK]), sb("ident", [D, D]), sb("ones", [D, D])
        s.average, s.eps = sb("average", [D, D]), sb("eps", [D, 1])
        s.means_made, s.centred, s.squared, s.vars_made, s.std_made, s.inverted, s.spread_made, s.scaled = (
            sem(n) for n in ("means_made", "centred", "squared", "vars_made", "std_made", "inverted", "spread_made",
                             "scaled"))
        s.product_made, s.product_taken, s.loaded, s.x_loaded, s.zeroed, s.consts_made = (
            sem(n) for n in ("product_made", "product_taken", "loaded", "x_loaded", "zeroed", "consts_made"))
        stored = sem("stored")

        def normalized(phase):
            layer_norm(nc, s, f"norm{phase}", s.x_T, s.xn)

        def run(phase, stage, *args):
            normalized(phase)
            stage(nc, s, a, *args)

        setup(nc, s, a)
        run(0, attention_one_head)
        mixture(nc, s, a, "L0", lambda: normalized(1), False)
        run(2, attention_16_heads, "L1", True, True)
        mixture(nc, s, a, "L1", lambda: normalized(3), True)
        run(4, attention_16_heads, "L2", False, False)
        run(5, quantized)
        run(6, attention_latents)
        run(7, routed)

        with nc.Block() as block:
            @block.sync
            def _(sp):
                sp.dma_start(out_T, s.x_T[:, :]).then_inc(stored, 16)
                sp.wait_ge(stored, 16)


def _layouts(i, np):
    def by_tile(m):
        m = m.reshape((B, KP, KT) + m.shape[2:])
        return np.ascontiguousarray(np.moveaxis(m, (2, 1), (-2, -1))).reshape((B,) + m.shape[3:] + (SK,))

    a = {"x_T": i["x"].reshape(TOK, D).T, "ctx_N": i["ctx_1024"], "ctx_T": by_tile(i["ctx_1024"]),
         "mask_T": by_tile(i["mask_BxS2_ik0"]), "mask_N": i["mask_BxS2_ik0"],
         "mask_B": i["mask_BxS2_bk0"],
         "L0_WqT": i["L0_xattn_Wq"].T, "L0_Wk": i["L0_xattn_Wk"], "L0_bq": i["L0_xattn_bq"][:, None],
         "L0_bk": i["L0_xattn_bk"][:, None]}
    for n in ("Wq", "Wk", "Wv", "Wo"):
        a[f"L1_{n}T"] = i[f"L1_xattn_{n}"].T
        a[f"L2_{n}T"] = i[f"L2_xattn_w_{n[1]}"].T
        a[f"L1_b{n[1]}"] = i[f"L1_xattn_b{n[1]}"][:, None]
    for n in ("L1_WoT", "L2_WoT", "L1_bv"):
        a[n] = a[n].reshape(4, 4, DK, -1).transpose(1, 2, 0, 3)
    a["L1_bv"] = a["L1_bv"].reshape(4, DK, 4)
    a["L0_gate_w"] = i["L0_ffn_gate_w"].T
    a["L1_gate_w"] = i["L1_ffn_gate_w"]
    a["L0_w1"] = i["L0_ffn_w1"].transpose(2, 0, 1).reshape(D, E * HID)
    a["L0_w2"] = i["L0_ffn_w2"].reshape(E, D, HT, D).transpose(3, 0, 2, 1).reshape(D, E * HT * D)
    a["L1_w1"] = i["L1_ffn_w1"].transpose(1, 0, 2).reshape(D, E * HID)
    a["L1_w2"] = i["L1_ffn_w2"].reshape(E, HT, D, D).transpose(2, 0, 1, 3).reshape(D, E * HT * D)
    for n in ("L0", "L1"):
        a[f"{n}_gate_b"] = i[f"{n}_ffn_gate_b"][None, :]
        a[f"{n}_b1"] = i[f"{n}_ffn_b1"].reshape(E * HT, D).T
        a[f"{n}_b2"] = i[f"{n}_ffn_b2"]
    a["L2_w1"] = i["L2_ffn_w1"]
    a["L2_w2"] = i["L2_ffn_w2"].reshape(HT, D, D).transpose(1, 0, 2).reshape(D, HT * D)
    a["L2_b1"] = i["L2_ffn_b1"].reshape(HT, D).T
    a["L2_b2"] = i["L2_ffn_b2"][:, None]
    for n in ("ln_x_w", "ln_x_b", "ln_l_w", "ln_l_b", "ln_o_w", "ln_o_b", "q_scale", "k_scale"):
        a[f"L3_{n}"] = i[f"L3_xattn_{n}"][:, None]
    a["L3_bx_row"] = i["L3_xattn_ln_x_b"][None, :]
    a["L3_Wq"] = i["L3_xattn_Wq"]
    a["L3_Wk"] = i["L3_xattn_Wkv"][:, :HID]
    a["L3_Wv"] = i["L3_xattn_Wkv"][:, HID:]
    a["L3_WkT"] = i["L3_xattn_Wkv"][:, :HID].T.reshape(HT, D, D).transpose(1, 0, 2)
    a["L3_Wo"] = i["L3_xattn_Wo"].reshape(HT, D, D).transpose(1, 0, 2)
    a["L3_gate_w"] = i["L3_ffn_gate_w"].T
    a["L3_w1"] = i["L3_ffn_w1"].transpose(1, 0, 2)
    a["L3_sw1"] = i["L3_ffn_sw1"]
    a["L3_w2"] = i["L3_ffn_w2"].reshape(2 * HT, D, D).transpose(1, 0, 2)
    a["L3_sw2"] = i["L3_ffn_sw2"].reshape(HT, D, D).transpose(1, 0, 2)
    a["L3_b1"] = i["L3_ffn_b1"].reshape(2 * HT, D).T
    a["L3_sb1"] = i["L3_ffn_sb1"].reshape(HT, D).T
    a["L3_b2"] = i["L3_ffn_b2"].T
    a["L3_sb2"] = i["L3_ffn_sb2"][:, None]
    return {k: np.ascontiguousarray(v) for k, v in a.items()}


def kernel(**inputs):
    import numpy as np
    import concourse.bacc as bacc
    from concourse.bass_utils import run_bass_kernel_spmd

    arrays = _layouts({k: np.asarray(v) for k, v in inputs.items()}, np)
    nc = bacc.Bacc("TRN2", target_bir_lowering=False, num_devices=1)
    a = {k: nc.dram_tensor(f"in_{k}", v.shape, mybir.dt.from_np(v.dtype), kind="ExternalInput").ap()
         for k, v in arrays.items()}
    out_T = nc.dram_tensor("out_T", [D, TOK], F32, kind="ExternalOutput").ap()
    build(nc, a, out_T)
    r = run_bass_kernel_spmd(nc, [{f"in_{k}": v for k, v in arrays.items()}], core_ids=[0])
    return np.ascontiguousarray(r.results[0]["out_T"].T).reshape(B, SQ, D)
```
